# Optimizing a Trainium2 kernel written in Bass

```python
import numpy as np
import jax
import jax.numpy as jnp

def _softmax(x, axis=-1):
    return jax.nn.softmax(x, axis=axis)

def _gelu(x):
    return jax.nn.gelu(x, approximate=True)

def _silu(x):
    return jax.nn.silu(x)

def _sigmoid(x):
    return jax.nn.sigmoid(x)

def _layernorm(x, axis=-1, eps=1e-05):
    m = jnp.mean(x, axis=axis, keepdims=True)
    v = jnp.var(x, axis=axis, keepdims=True)
    return (x - m) / jnp.sqrt(v + eps)

def _scatter_add(tgt, idx, src, axis=0):
    return tgt.at[idx].add(src)

def _segment_sum(src, seg, n):
    return jax.ops.segment_sum(src, seg, n)
kernel_name = 'mk_decoder_postln_d1_seqx_r8_95b9ea'

def setup_inputs(seed: int=0):
    np.random.seed(seed)
    _w = jnp.asarray

    def _rec_inputs():
        import jax
        import jax.numpy as jnp
        _rk = jax.random.key(seed)
        x = -0.0003929 + 0.9999 * jax.random.normal(jax.random.fold_in(_rk, 1), (16, 56, 256), jnp.float32)
        _lenS = 56 - jax.random.randint(jax.random.fold_in(_rk, 7), (16,), 0, max(1, 56 // 4) + 1, jnp.int32)
        _lenS2 = 1500 - jax.random.randint(jax.random.fold_in(_rk, 8), (16,), 0, max(1, 1500 // 4) + 1, jnp.int32)
        _ctx_2048P = jax.random.normal(jax.random.fold_in(_rk, 11), (16, 16, 256), jnp.float32)
        _ctx_2048c = jax.random.dirichlet(jax.random.fold_in(_rk, 511), 0.3 * jnp.ones((16,), jnp.float32), (16, 1500))
        _ctx_2048t = jnp.einsum('bsk,bkd->bsd', _ctx_2048c, _ctx_2048P)
        _ctx_2048t = _ctx_2048t * jax.lax.rsqrt(jnp.mean(jnp.square(_ctx_2048t)) + 1e-12) * 0.953939
        ctx_2048 = -0.000514642 + 1.00011 * (_ctx_2048t + 0.3 * jax.random.normal(jax.random.fold_in(_rk, 611), (16, 1500, 256), jnp.float32))
        _validS = jnp.arange(56)[None, :] < _lenS[:, None]
        _validS2 = jnp.arange(1500)[None, :] < _lenS2[:, None]
        _causal = jnp.tril(jnp.ones((56, 56), dtype=bool))
        mask_BxS2_ik0 = jnp.where(jnp.broadcast_to(_validS2[:, :], (16, 1500)), 0, 1).astype(jnp.int32)
        return (x, ctx_2048, mask_BxS2_ik0)
    x, ctx_2048, mask_BxS2_ik0 = _rec_inputs()

    def _L0_attn_setup():
        import jax, jax.numpy as jnp
        import numpy as np
        import math
        HIDDEN = 256
        NUM_HEADS = 16
        NUM_KV_HEADS = 8
        HEAD_DIM = HIDDEN // NUM_HEADS
        ROPE_THETA = 1000000.0
        SPARSITY_RATIO = 0.5
        VISION_SPARSITY_RATIO = 0.4
        BATCH = 2
        SEQ = 256

        def rotate_half(x):
            h = x.shape[-1] // 2
            return jnp.concatenate([-x[..., h:], x[..., :h]], axis=-1)
        key = jax.random.key(seed)
        ks = jax.random.split(key, 12)
        s = 1.0 / math.sqrt(HIDDEN)
        return {'hidden_states': jax.random.normal(ks[0], (BATCH, SEQ, HIDDEN), jnp.float32), 'Wq': jax.random.normal(ks[1], (HIDDEN, NUM_HEADS * HEAD_DIM), jnp.float32) * s, 'bq': jax.random.normal(ks[2], (NUM_HEADS * HEAD_DIM,), jnp.float32) * 0.01, 'Wk': jax.random.normal(ks[3], (HIDDEN, NUM_KV_HEADS * HEAD_DIM), jnp.float32) * s, 'bk': jax.random.normal(ks[4], (NUM_KV_HEADS * HEAD_DIM,), jnp.float32) * 0.01, 'Wv': jax.random.normal(ks[5], (HIDDEN, NUM_KV_HEADS * HEAD_DIM), jnp.float32) * s, 'bv': jax.random.normal(ks[6], (NUM_KV_HEADS * HEAD_DIM,), jnp.float32) * 0.01, 'Wo': jax.random.normal(ks[7], (NUM_HEADS * HEAD_DIM, HIDDEN), jnp.float32) * s, 'bo': jax.random.normal(ks[8], (HIDDEN,), jnp.float32) * 0.01, 'Wr': jax.random.normal(ks[9], (HIDDEN, NUM_HEADS), jnp.float32) * s, 'br': jax.random.normal(ks[10], (NUM_HEADS,), jnp.float32) * 0.01}
    _L0_attn_all = _L0_attn_setup()
    _L0_attn_in = {k: v for k, v in _L0_attn_all.items() if k in ('Wq', 'bq', 'Wk', 'bk', 'Wv', 'bv', 'Wo', 'bo', 'Wr', 'br')}
    del _L0_attn_all

    def _L0_xattn_setup():
        import jax, jax.numpy as jnp
        import numpy as np
        import math
        H = 256
        NH = 16
        HD = H // NH
        EPS_LN = 1e-05
        RES_SCALE_MAX = 0.3

        def _nan_clean(x, lim=10000.0):
            return jnp.nan_to_num(x, nan=0.0, posinf=lim, neginf=-lim)
        key = jax.random.key(seed)
        ks = jax.random.split(key, 12)
        B, S, T = (4, 256, 32)
        std = 1.0 / math.sqrt(H)
        return {'hidden_states': jax.random.normal(ks[0], (B, S, H), jnp.float32), 'audio_tokens': jax.random.normal(ks[1], (B, T, H), jnp.float32), 'attention_mask': jax.random.randint(ks[2], (B, T), 0, 2, jnp.int32), 'Wq': jax.random.normal(ks[3], (H, H), jnp.float32) * std, 'bq': jnp.zeros((H,), jnp.float32), 'Wk': jax.random.normal(ks[4], (H, H), jnp.float32) * std, 'bk': jnp.zeros((H,), jnp.float32), 'Wv': jax.random.normal(ks[5], (H, H), jnp.float32) * std, 'bv': jnp.zeros((H,), jnp.float32), 'Wo': jax.random.normal(ks[6], (H, H), jnp.float32) * std, 'bo': jnp.zeros((H,), jnp.float32), 'ln_gamma': jnp.ones((H,), jnp.float32), 'ln_beta': jnp.zeros((H,), jnp.float32), 'residual_scale': jnp.float32(0.05)}
    _L0_xattn_all = _L0_xattn_setup()
    _L0_xattn_in = {k: v for k, v in _L0_xattn_all.items() if k in ('Wq', 'bq', 'Wk', 'bk', 'Wv', 'bv', 'Wo', 'bo', 'ln_gamma', 'ln_beta', 'residual_scale')}
    del _L0_xattn_all

    def _L0_ffn_setup():
        import jax, jax.numpy as jnp
        import numpy as np
        EPS_NORM = 1e-06
        EPS_Q = 1e-08
        QB = 127.0

        def _ternary_quantize(w):
            scale = jnp.maximum(jnp.mean(jnp.abs(w)), EPS_Q)
            w_q = jnp.clip(jnp.round(w / scale), -1.0, 1.0)
            return (w_q, scale)

        def _activation_quant(x):
            gamma = jnp.maximum(jnp.max(jnp.abs(x), axis=-1, keepdims=True), EPS_Q)
            x_q = jnp.clip(jnp.round(x * QB / gamma), -QB, QB)
            return (x_q, gamma / QB)

        def _rmsnorm(x, weight):
            out = x * jax.lax.rsqrt(jnp.mean(x * x, axis=-1, keepdims=True) + EPS_NORM)
            return out * weight
        key = jax.random.key(seed)
        dim, expansion = (256, 4)
        hidden = dim * expansion
        B, S = (4, 512)
        k1, k2, k3 = jax.random.split(key, 3)
        x = jax.random.normal(k1, (B, S, dim), dtype=jnp.float32)
        weight_up = jax.random.normal(k2, (hidden, dim), dtype=jnp.float32) * 0.02
        weight_down = jax.random.normal(k3, (dim, hidden), dtype=jnp.float32) * 0.02
        norm_weight = jnp.ones((dim,), dtype=jnp.float32)
        gamma = jnp.full((dim,), 1e-05, dtype=jnp.float32)
        return {'x': x, 'weight_up': weight_up, 'weight_down': weight_down, 'norm_weight': norm_weight, 'gamma': gamma}
    _L0_ffn_all = _L0_ffn_setup()
    _L0_ffn_in = {k: v for k, v in _L0_ffn_all.items() if k in ('weight_up', 'weight_down', 'norm_weight', 'gamma')}
    del _L0_ffn_all
    return {'x': x, 'ctx_2048': ctx_2048, 'mask_BxS2_ik0': mask_BxS2_ik0, 'L0_attn_Wq': _L0_attn_in['Wq'], 'L0_attn_bq': _L0_attn_in['bq'], 'L0_attn_Wk': _L0_attn_in['Wk'], 'L0_attn_bk': _L0_attn_in['bk'], 'L0_attn_Wv': _L0_attn_in['Wv'], 'L0_attn_bv': _L0_attn_in['bv'], 'L0_attn_Wo': _L0_attn_in['Wo'], 'L0_attn_bo': _L0_attn_in['bo'], 'L0_attn_Wr': _L0_attn_in['Wr'], 'L0_attn_br': _L0_attn_in['br'], 'L0_xattn_Wq': _L0_xattn_in['Wq'], 'L0_xattn_bq': _L0_xattn_in['bq'], 'L0_xattn_Wk': _L0_xattn_in['Wk'], 'L0_xattn_bk': _L0_xattn_in['bk'], 'L0_xattn_Wv': _L0_xattn_in['Wv'], 'L0_xattn_bv': _L0_xattn_in['bv'], 'L0_xattn_Wo': _L0_xattn_in['Wo'], 'L0_xattn_bo': _L0_xattn_in['bo'], 'L0_xattn_ln_gamma': _L0_xattn_in['ln_gamma'], 'L0_xattn_ln_beta': _L0_xattn_in['ln_beta'], 'L0_xattn_residual_scale': _L0_xattn_in['residual_scale'], 'L0_ffn_weight_up': _L0_ffn_in['weight_up'], 'L0_ffn_weight_down': _L0_ffn_in['weight_down'], 'L0_ffn_norm_weight': _L0_ffn_in['norm_weight'], 'L0_ffn_gamma': _L0_ffn_in['gamma']}

def reference(x, ctx_2048, mask_BxS2_ik0, L0_attn_Wq, L0_attn_bq, L0_attn_Wk, L0_attn_bk, L0_attn_Wv, L0_attn_bv, L0_attn_Wo, L0_attn_bo, L0_attn_Wr, L0_attn_br, L0_xattn_Wq, L0_xattn_bq, L0_xattn_Wk, L0_xattn_bk, L0_xattn_Wv, L0_xattn_bv, L0_xattn_Wo, L0_xattn_bo, L0_xattn_ln_gamma, L0_xattn_ln_beta, L0_xattn_residual_scale, L0_ffn_weight_up, L0_ffn_weight_down, L0_ffn_norm_weight, L0_ffn_gamma):
    import jax
    import jax.numpy as jnp

    def _L0_attn_ref(hidden_states, Wq, bq, Wk, bk, Wv, bv, Wo, bo, Wr, br):
        import jax, jax.numpy as jnp
        import numpy as np
        import math
        HIDDEN = 256
        NUM_HEADS = 16
        NUM_KV_HEADS = 8
        HEAD_DIM = HIDDEN // NUM_HEADS
        ROPE_THETA = 1000000.0
        SPARSITY_RATIO = 0.5
        VISION_SPARSITY_RATIO = 0.4
        BATCH = 2
        SEQ = 256

        def rotate_half(x):
            h = x.shape[-1] // 2
            return jnp.concatenate([-x[..., h:], x[..., :h]], axis=-1)
        bsz, q_len, _ = hidden_states.shape
        q = (hidden_states @ Wq + bq).reshape(bsz, q_len, NUM_HEADS, HEAD_DIM).transpose(0, 2, 1, 3)
        k = (hidden_states @ Wk + bk).reshape(bsz, q_len, NUM_KV_HEADS, HEAD_DIM).transpose(0, 2, 1, 3)
        v = (hidden_states @ Wv + bv).reshape(bsz, q_len, NUM_KV_HEADS, HEAD_DIM).transpose(0, 2, 1, 3)
        pos = jnp.arange(q_len, dtype=jnp.float32)
        inv_freq = 1.0 / ROPE_THETA ** (jnp.arange(0, HEAD_DIM, 2, dtype=jnp.float32) / HEAD_DIM)
        freqs = pos[:, None] * inv_freq[None, :]
        emb = jnp.concatenate([freqs, freqs], axis=-1)
        cos = jnp.cos(emb)[None, None, :, :]
        sin = jnp.sin(emb)[None, None, :, :]
        q = q * cos + rotate_half(q) * sin
        k = k * cos + rotate_half(k) * sin
        n_rep = NUM_HEADS // NUM_KV_HEADS
        k = jnp.repeat(k, n_rep, axis=1)
        v = jnp.repeat(v, n_rep, axis=1)
        routing = jax.nn.sigmoid(hidden_states @ Wr + br).transpose(0, 2, 1)
        ratio = VISION_SPARSITY_RATIO if q_len > 64 else SPARSITY_RATIO
        topk = max(1, min(int(q_len * ratio), q_len))
        _, idx = jax.lax.top_k(routing, topk)
        mask = jax.vmap(jax.vmap(lambda i: jnp.zeros((q_len,), bool).at[i].set(True)))(idx)
        scores = jnp.einsum('bhqd,bhkd->bhqk', q, k) / math.sqrt(HEAD_DIM)
        sparse = jnp.where(mask[:, :, None, :], scores, -jnp.inf)
        probs = jax.nn.softmax(sparse.astype(jnp.float32), axis=-1).astype(q.dtype)
        out = jnp.einsum('bhqk,bhkd->bhqd', probs, v)
        out = out.transpose(0, 2, 1, 3).reshape(bsz, q_len, NUM_HEADS * HEAD_DIM)
        return out @ Wo + bo

    def _L0_xattn_ref(hidden_states, audio_tokens, attention_mask, Wq, bq, Wk, bk, Wv, bv, Wo, bo, ln_gamma, ln_beta, residual_scale):
        import jax, jax.numpy as jnp
        import numpy as np
        import math
        H = 256
        NH = 16
        HD = H // NH
        EPS_LN = 1e-05
        RES_SCALE_MAX = 0.3

        def _nan_clean(x, lim=10000.0):
            return jnp.nan_to_num(x, nan=0.0, posinf=lim, neginf=-lim)
        B, S, _ = hidden_states.shape
        T = audio_tokens.shape[1]
        hs = _nan_clean(hidden_states).astype(jnp.float32)
        at = _nan_clean(audio_tokens).astype(jnp.float32)

        def proj(x, W, b, L):
            y = x @ W.T + b
            return y.reshape(B, L, NH, HD).transpose(0, 2, 1, 3)
        q = _nan_clean(proj(hs, Wq, bq, S))
        k = _nan_clean(proj(at, Wk, bk, T))
        v = _nan_clean(proj(at, Wv, bv, T))
        scale = max(math.sqrt(HD), 1e-08)
        scores = jnp.einsum('bhsd,bhtd->bhst', q, k) / scale
        scores = jnp.clip(scores, -50.0, 50.0)
        scores = jnp.nan_to_num(scores, nan=0.0, posinf=50.0, neginf=-50.0)
        attend = (attention_mask.astype(jnp.float32) > 0.5)[:, None, None, :]
        scores = jnp.where(attend, scores, -10000.0)
        scores = jnp.clip(scores, -50.0, 50.0)
        probs = jax.nn.softmax(scores, axis=-1)
        probs = jnp.nan_to_num(probs, nan=0.0, posinf=1.0, neginf=0.0)
        probs = probs / (probs.sum(axis=-1, keepdims=True) + 1e-08)
        ctx = jnp.einsum('bhst,bhtd->bhsd', probs, v)
        ctx = ctx.transpose(0, 2, 1, 3).reshape(B, S, H)
        delta = _nan_clean(ctx @ Wo.T + bo)
        rs = jnp.clip(residual_scale, 0.0, RES_SCALE_MAX)
        delta = rs * delta
        mu = delta.mean(axis=-1, keepdims=True)
        var = jnp.mean((delta - mu) ** 2, axis=-1, keepdims=True)
        delta = (delta - mu) / jnp.sqrt(var + EPS_LN) * ln_gamma + ln_beta
        return delta

    def _L0_ffn_ref(x, weight_up, weight_down, norm_weight, gamma):
        import jax, jax.numpy as jnp
        import numpy as np
        EPS_NORM = 1e-06
        EPS_Q = 1e-08
        QB = 127.0

        def _ternary_quantize(w):
            scale = jnp.maximum(jnp.mean(jnp.abs(w)), EPS_Q)
            w_q = jnp.clip(jnp.round(w / scale), -1.0, 1.0)
            return (w_q, scale)

        def _activation_quant(x):
            gamma = jnp.maximum(jnp.max(jnp.abs(x), axis=-1, keepdims=True), EPS_Q)
            x_q = jnp.clip(jnp.round(x * QB / gamma), -QB, QB)
            return (x_q, gamma / QB)

        def _rmsnorm(x, weight):
            out = x * jax.lax.rsqrt(jnp.mean(x * x, axis=-1, keepdims=True) + EPS_NORM)
            return out * weight
        residual = x
        xn = _rmsnorm(x, norm_weight)
        w_up_q, s_up = _ternary_quantize(weight_up)
        w_down_q, s_down = _ternary_quantize(weight_down)
        x_q, s_x = _activation_quant(xn)
        h = jnp.einsum('bsd,hd->bsh', x_q * s_x, w_up_q * s_up)
        h = jax.nn.silu(h)
        out = jnp.einsum('bsh,dh->bsd', h, w_down_q * s_down)
        return residual + out * gamma
    x = _layernorm(x + _L0_attn_ref(x, L0_attn_Wq, L0_attn_bq, L0_attn_Wk, L0_attn_bk, L0_attn_Wv, L0_attn_bv, L0_attn_Wo, L0_attn_bo, L0_attn_Wr, L0_attn_br), axis=-1)
    x = _layernorm(x + _L0_xattn_ref(x, ctx_2048, mask_BxS2_ik0, L0_xattn_Wq, L0_xattn_bq, L0_xattn_Wk, L0_xattn_bk, L0_xattn_Wv, L0_xattn_bv, L0_xattn_Wo, L0_xattn_bo, L0_xattn_ln_gamma, L0_xattn_ln_beta, L0_xattn_residual_scale), axis=-1)
    x = _layernorm(x + _L0_ffn_ref(x, L0_ffn_weight_up, L0_ffn_weight_down, L0_ffn_norm_weight, L0_ffn_gamma), axis=-1)
    return x

_drawn_inputs = setup_inputs


def setup_inputs(seed=0):
    import zlib

    import numpy as np

    out = dict(_drawn_inputs(seed))
    spreads = {'L0_xattn_bq': (0.0, 0.268),
     'L0_xattn_bk': (0.0, 2.0),
     'L0_xattn_bv': (0.0, 0.1),
     'L0_xattn_bo': (0.0, 0.1),
     'L0_xattn_ln_gamma': (1.0, 0.2),
     'L0_xattn_ln_beta': (0.0, 0.1),
     'L0_ffn_norm_weight': (1.0, 0.6),
     'L0_ffn_gamma': (9.999999747378752e-06, 0.6)}
    factors = {'L0_attn_bq': 30.515,
     'L0_attn_bk': 63.346,
     'L0_attn_bv': 7.412,
     'L0_attn_bo': 8.0,
     'L0_ffn_weight_up': 200.0,
     'L0_ffn_weight_down': 200.0}
    for name, (base, spread) in spreads.items():
        noise = np.random.default_rng([zlib.crc32(name.encode()), seed]).standard_normal(out[name].shape)
        drawn = base * np.exp(spread * noise) if base else spread * noise
        out[name] = jnp.asarray(drawn.astype(out[name].dtype))
    for name, factor in factors.items():
        out[name] = (out[name] * factor).astype(out[name].dtype)
    return out
```

```python
from contextlib import ExitStack

import numpy as np

import concourse.bass as bass
from concourse import mybir

F32 = mybir.dt.float32
F32R = mybir.dt.float32r
BF16 = mybir.dt.bfloat16
I32 = mybir.dt.int32
ALU = mybir.AluOpType
ACT = mybir.ActivationFunctionType
AX = mybir.AxisListType

B, SEQ, D = 16, 56, 256
CTX = 1500
NH, HD = 16, 16
NKV = 8
HID = 1024
TOPK = SEQ // 2
TILES = B // 2
SLOT = 64
KD = D // 128
CT = 125
NT = CTX // CT
NCH = 3
CH = CTX // NCH
TPC = NT // NCH
QUAD = 4 * SEQ
HQ = 2 * QUAD
SCALE = float(HD) ** -0.5
CLIP = 50.0
EXP_MAX = float(np.exp(np.float64(CLIP)))
EXP_MIN = float(np.exp(np.float64(-CLIP)))
NEG = -1e30
MAGIC = 1.5 * 2.0 ** 23
QB = 127.0
R_BQK, R_BO1, R_BO2, R_LNG, R_LNB, R_NW, R_FG = 0, 384, 640, 896, 1152, 1408, 1664
R_ALL = 1920
C_BV1, C_BQ2, C_BK2, C_BV2, C_BR, C_RS = 0, 2, 6, 8, 10, 11
C_ALL = 12
K_ID, K_D8, K_D4, K_DJ, K_DH, K_COS, K_SIN = 0, 128, 136, 140, 142, 158, 174
K_ALL = 190


def spread(ap, axis, n):
    ap = ap.unsqueeze(axis)
    shape = list(ap.shape)
    shape[axis] = n
    return ap.to_broadcast(shape)


def build(nc, x, xT, ctxT, mask, w_qk, w_v, w_r, w_o, w_q2, w_k2, w_v2, w_o2, w_up, w_down,
          rows, cols, consts, out):
    with ExitStack() as ctx:
        def sb(name, shape, dt=F32):
            return ctx.enter_context(nc.sbuf_tensor(name, shape, dt))

        def sem(name):
            return ctx.enter_context(nc.semaphore(name))

        SC = ctx.enter_context(nc.psum_tensor("SC", [128, 2, 2, 512], F32))
        ACC = ctx.enter_context(nc.psum_tensor("ACC", [128, 2, 512], F32))
        W0 = ctx.enter_context(nc.psum_tensor("W0", [128, 512], F32))
        W1 = ctx.enter_context(nc.psum_tensor("W1", [128, 512], F32))
        W = [W0, W1]

        kc = sb("kc", [128, K_ALL])
        ident = kc[:, K_ID:K_ID + 128]
        d8 = kc[:, K_D8:K_D8 + 8]
        d4 = kc[:, K_D4:K_D4 + 4]
        dj = kc[:, K_DJ:K_DJ + 2]
        dh = kc[:, K_DH:K_DH + 16]
        rc = sb("rc", [128, R_ALL])
        cc = sb("cc", [128, C_ALL])
        ident_b = sb("ident_b", [128, 128], BF16)
        ones = sb("ones", [128, 64])
        ones_b = sb("ones_b", [64, 64], BF16)
        half = sb("half", [128, 1])
        mark = sb("mark", [1, 2])
        pbuf = sb("pbuf", [128, 4 * 2 * HQ])
        wqk, wv, wr, wo, wq2 = (
            pbuf[:, KD * o:KD * (o + n)].rearrange("p (k n) -> p k n", k=KD)
            for o, n in ((0, 384), (384, 128), (512, 32), (544, D), (800, 512)))
        wo2 = sb("wo2", [128, KD, D])
        wk_hi = sb("wk_hi", [128, KD, D], F32R)
        wk_lo = sb("wk_lo", [128, KD, D], F32R)
        wv_hi = sb("wv_hi", [128, KD, D], F32R)
        wv_lo = sb("wv_lo", [128, KD, D], F32R)
        wup = sb("wup", [128, KD, HID], BF16)
        wdn = sb("wdn", [128, HID // 128, D], F32R)
        wsum = sb("wsum", [128, 2])
        wscale = sb("wscale", [128, 2])
        winv = sb("winv", [128, 2])
        sgam = sb("sgam", [128, D])
        nbr = sb("nbr", [128, 1])
        rs = sb("rs", [128, 1])
        mscale = sb("mscale", [CT, B * NT])
        mbias = sb("mbias", [CT, B * NT])

        x1_all = sb("x1_all", [128, TILES, D])
        q2_all = sb("q2_all", [128, TILES, 4, 128])
        oT_all = q2_all[:, :, 0:KD, :].rearrange("p t j n -> p j t n")

        craw = sb("craw", [128, 2, KD, CH])
        chi = sb("chi", [128, NCH, KD, CH], F32R)
        clo = sb("clo", [128, NCH, KD, CH], F32R)
        kst = [sb(f"kst{i}", [128, 4, CTX], F32R) for i in range(2)]
        v2 = [sb(f"v2_{i}", [128, NT, D]) for i in range(2)]
        p2 = [pbuf[0:CT, 2 * HQ * i:2 * HQ * i + 2 * HQ] for i in range(3)]
        psum2 = pbuf[0:CT, 6 * HQ:8 * HQ]
        qh = sb("qh", [128, 4, SEQ], F32R)
        ql = sb("ql", [128, 4, SEQ], F32R)
        qbd = [[sb(f"qbd{i}{k}", [128, 4, 4, SEQ], F32R) for k in range(2)] for i in range(2)]

        raw = [v2[i][:, :, :].rearrange("p a n -> p (a n)") for i in range(2)]
        at = [0]

        def cut(n):
            i, o = at[0] // (NT * D), at[0] % (NT * D)
            if o + n > NT * D:
                i, o = i + 1, 0
            at[0] = i * NT * D + o + n
            return raw[i][:, o:o + n]

        xTt = cut(KD * 128).rearrange("p (k n) -> p k n", k=KD)
        xt = cut(D)
        xb = cut(D)
        qk = cut(384)
        rcos = cut(384)
        qkr = cut(384)
        er = cut(64)
        sg = [cut(SEQ + 4) for _ in range(3)]
        m8 = cut(8)
        qT = cut(256).rearrange("p (j n) -> p j n", j=2)
        pe = cut(2 * NKV * SLOT)
        pe4 = pe.rearrange("p (g j k) -> p g j k", g=NKV, j=2)[:, :, :, 0:SEQ]
        pe3 = pe.rearrange("p (h k) -> p h k", k=SLOT)[:, :, 0:SEQ]
        st_max = cut(16)
        st_sum = cut(16)
        st_rec = cut(16)
        oT = cut(256).rearrange("p (j n) -> p j n", j=2)
        y1 = cut(D)
        stats = cut(6)
        aggr = cut(2)
        veps = cut(1)
        rstd = cut(1)
        x1T = cut(256).rearrange("p (j n) -> p j n", j=2)
        at[0] = 0
        oTb = cut(KD * 128).rearrange("p (j n) -> p j n", j=KD)
        x1c = cut(D)
        dl = cut(D)
        xb3 = cut(D)
        x2 = cut(D)
        xn = cut(D)
        xq = cut(D // 2).bitcast(BF16)
        xqT = cut(D // 2).bitcast(BF16).rearrange("p (j n) -> p j n", j=KD)
        z_half = cut(HID)
        th = cut(HID)
        y3 = cut(D)
        stats3 = cut(6)
        small = cut(16)

        kbd = sb("kbd", [128, 2, NKV * SEQ])
        pT = sb("pT", [128, NKV, 128])
        vbd = sb("vbd", [128, 2, NKV, 32])
        negm = sb("negm", [64, SEQ], BF16)
        drop = sb("drop", [64, NH, SEQ], BF16)
        hT_hi = kst[0][:, 0, 0:HID].rearrange("p (k n) -> p k n", k=8)
        hT_lo = kst[0][:, 1, 0:HID].rearrange("p (k n) -> p k n", k=8)
        up_raw, down_raw = (raw[i][:, 0:2 * HID] for i in range(2))
        wk_raw, wv_raw = (raw[0][:, 2 * HID + 512 * i:2 * HID + 512 * i + 512] for i in range(2))
        mski = kbd[0:CT, 0, 0:B * NT].bitcast(I32)
        rec2 = kbd[:, 0, :]
        recm = kbd[:, 1, :]
        accs, accm = (pT[:, :, :].rearrange("p g n -> p (g n)")[:, 512 * i:512 * i + HQ] for i in range(2))

        const_in = sem("const_in")
        wself_in = sem("wself_in")
        wk_in = sem("wk_in")
        wv_in = sem("wv_in")
        wup_in = sem("wup_in")
        wdn_in = sem("wdn_in")
        x_in = sem("x_in")
        xT_in = sem("xT_in")
        c_in = [sem(f"c_in{c}") for c in range(NCH)]
        y_out = sem("y_out")
        set_ones = sem("set_ones")
        set_cols = sem("set_cols")
        set_mask = sem("set_mask")
        wkv_split = sem("wkv_split")
        wq_abs = sem("wq_abs")
        wq_sum = sem("wq_sum")
        wq_mean = sem("wq_mean")
        wq_inv = sem("wq_inv")
        wq_scaled = sem("wq_scaled")
        wq_round = sem("wq_round")
        wq_done = sem("wq_done")
        qk_ready = sem("qk_ready")
        rv_ready = sem("rv_ready")
        qk_biased = sem("qk_biased")
        er_ready = sem("er_ready")
        vbd_ready = sem("vbd_ready")
        rope_cos = sem("rope_cos")
        rope_sin = sem("rope_sin")
        roped = sem("roped")
        qT_ready = sem("qT_ready")
        kT_ready = sem("kT_ready")
        qT_copied = sem("qT_copied")
        kbd_ready = sem("kbd_ready")
        sig_plus = sem("sig_plus")
        sig_ready = sem("sig_ready")
        top8 = sem("top8")
        top8_out = sem("top8_out")
        negm_ready = sem("negm_ready")
        drop_ready = sem("drop_ready")
        s1_ready = sem("s1_ready")
        s1_max = sem("s1_max")
        s1_sub = sem("s1_sub")
        p1_exp = sem("p1_exp")
        p1_sum = sem("p1_sum")
        p1_rec = sem("p1_rec")
        p1_norm = sem("p1_norm")
        pT_ready = sem("pT_ready")
        pT_copied = sem("pT_copied")
        oT_ready = sem("oT_ready")
        oT_copied = sem("oT_copied")
        o1_ready = sem("o1_ready")
        xb_ready = sem("xb_ready")
        y1_ready = sem("y1_ready")
        y1_stats = sem("y1_stats")
        y1_aggr = sem("y1_aggr")
        y1_veps = sem("y1_veps")
        y1_rstd = sem("y1_rstd")
        x1_ready = sem("x1_ready")
        x1T_ready = sem("x1T_ready")
        x1T_copied = sem("x1T_copied")
        q2_ready = sem("q2_ready")
        q2_copied = sem("q2_copied")
        chi_ready = sem("chi_ready")
        clo_ready = sem("clo_ready")
        w_ready = [sem("w0_ready"), sem("w1_ready")]
        khi_ready = sem("khi_ready")
        k_ready = sem("k_ready")
        v_ready = sem("v_ready")
        qh_ready = sem("qh_ready")
        ql_ready = sem("ql_ready")
        qbd_ready = sem("qbd_ready")
        s2_ready = sem("s2_ready")
        p2_exp = sem("p2_exp")
        p2_clip = sem("p2_clip")
        p2_added = sem("p2_added")
        pv_done = sem("pv_done")
        den_ready = sem("den_ready")
        acc_copied = sem("acc_copied")
        den_read = sem("den_read")
        den_masked = sem("den_masked")
        acc_scaled = sem("acc_scaled")
        o2_ready = sem("o2_ready")
        o3_biased = sem("o3_biased")
        x1_copied = sem("x1_copied")
        d3_ready = sem("d3_ready")
        d3_steps = sem("d3_steps")
        v3_ready = sem("v3_ready")
        pow_done = sem("pow_done")
        xq_ready = sem("xq_ready")
        xqT_ready = sem("xqT_ready")
        xqT_copied = sem("xqT_copied")
        up_ready = sem("up_ready")
        z_ready = sem("z_ready")
        h_ready = sem("h_ready")
        hT_ready = sem("hT_ready")
        hThi_ready = sem("hThi_ready")
        hTlo_ready = sem("hTlo_ready")
        dn_ready = sem("dn_ready")
        y3_ready = sem("y3_ready")

        block = ctx.enter_context(nc.Block())

        @block.sync
        def _(sp):
            sp.dma_start(kc[:, :], consts).then_inc(const_in, 16)
            sp.dma_start(cc[:, :], cols).then_inc(const_in, 16)
            sp.dma_start(rc[:, :], rows.partition_broadcast(128)).then_inc(const_in, 16)
            sp.dma_start(wqk, w_qk.rearrange("(k p) n -> p k n", p=128)).then_inc(wself_in, 16)
            sp.dma_start(wv, w_v.rearrange("(k p) n -> p k n", p=128)).then_inc(wself_in, 16)
            sp.dma_start(wr, w_r.rearrange("(k p) n -> p k n", p=128)).then_inc(wself_in, 16)
            sp.dma_start(wo, w_o.rearrange("(k p) n -> p k n", p=128)).then_inc(wself_in, 16)
            sp.dma_start(wq2, w_q2.rearrange("(k p) n -> p k n", p=128)).then_inc(wself_in, 16)
            sp.dma_start(wo2[:, :, :], w_o2.rearrange("(k p) n -> p k n", p=128)).then_inc(wself_in, 16)
            sp.dma_start(mski, mask).then_inc(const_in, 16)
            sp.dma_start(wk_raw.rearrange("p (k n) -> p k n", k=KD),
                         w_k2.rearrange("(k p) n -> p k n", p=128)).then_inc(wk_in, 16)
            sp.dma_start(wv_raw.rearrange("p (k n) -> p k n", k=KD),
                         w_v2.rearrange("(k p) n -> p k n", p=128)).then_inc(wv_in, 16)
            sp.dma_start(up_raw.rearrange("p (k n) -> p k n", k=KD),
                         w_up.rearrange("(k p) n -> p k n", p=128)).then_inc(wup_in, 16)
            sp.dma_start(down_raw.rearrange("p (k n) -> p k n", k=HID // 128),
                         w_down.rearrange("(k p) n -> p k n", p=128)).then_inc(wdn_in, 16)


            def load_context(b, c, slot):
                sp.dma_start(craw[:, slot, :, :],
                             ctxT[bass.ds(b, 1), :, c * CH:(c + 1) * CH].rearrange(
                                 "o (k p) n -> p (o k) n", p=128)).then_inc(c_in[c], 16)

            for c in range(2):
                load_context(0, c, c)
            sp.wait_ge(wkv_split, 4)
            sp.wait_ge(wq_done, 2)
            sp.dma_start(xTt, xT[:, 0:128].rearrange("(k p) n -> p k n", p=128)).then_inc(xT_in, 16)
            sp.dma_start(xt, x[0, :, :]).then_inc(x_in, 16)
            with sp.Fori(1, TILES) as t:
                sp.wait_ge(rv_ready, t)
                sp.dma_start(xTt, xT[:, bass.ds(t * 128, 128)].rearrange(
                    "(k p) n -> p k n", p=128)).then_inc(xT_in, 16)
                sp.wait_ge(xb_ready, t)
                sp.dma_start(xt, x[bass.ds(t, 1), :, :].rearrange("o p n -> p (o n)")).then_inc(x_in, 16)
            def next_chunks(b, par, first=0):
                for c in range(first, NCH):
                    sp.wait_ge(clo_ready, b * NCH + (c - 1))
                    load_context(b, c, (par * NCH + c) % 2)

            next_chunks(0, 0, first=2)
            next_chunks(1, 1)
            with sp.Fori(1, TILES) as t:
                next_chunks(t * 2, 0)
                next_chunks(t * 2 + 1, 1)
            with sp.Fori(0, TILES) as t:
                sp.wait_ge(y3_ready, t + 1)
                for h in range(2):
                    sp.dma_start(out[bass.ds(t * 2 + h, 1), :, :].rearrange("o p n -> p (o n)"),
                                 y3[SLOT * h:SLOT * h + SEQ, :]).then_inc(y_out, 16)
            sp.wait_ge(y_out, 32 * TILES)

        @block.tensor
        def _(te):
            te.wait_ge(set_ones, 3)
            te.wait_ge(wq_abs, 2)
            te.matmul(W0[0:64, 0:2], ones[:, :], wsum[:, :], start=True, stop=True)
            te.matmul(W0[64:128, 0:2], ones[:, :], wsum[:, :], start=True, stop=True).then_inc(wq_sum, 1)
            te.wait_ge(wq_mean, 1)

            def stage1(t):
                te.wait_ge(xT_in, t * 16 + 16)
                for k in range(KD):
                    mm = te.matmul(W0[:, 0:384], xTt[:, k, :], wqk[:, k, :], start=k == 0, stop=k == KD - 1)
                mm.then_inc(qk_ready, 1)
                for b in range(2):
                    for k in range(KD):
                        te.matmul(W1[32 * b:32 * b + 32, 0:SLOT], wr[:, k, :],
                                  xTt[:, k, SLOT * b:SLOT * b + SLOT], start=k == 0, stop=k == KD - 1)
                for b in range(2):
                    for k in range(KD):
                        for j in range(2):
                            mm = te.matmul(W1[SLOT * j:SLOT * j + SLOT, 128 + 128 * b:256 + 128 * b],
                                           xTt[:, k, SLOT * b:SLOT * b + SLOT],
                                           wv[:, k, :], start=k == 0, stop=k == KD - 1)
                mm.then_inc(rv_ready, 1)
                te.wait_ge(roped, t + 1)
                for j in range(2):
                    mm = te.transpose(W0[:, 128 * j:128 * j + 128], qkr[:, 128 * j:128 * j + 128], ident)
                mm.then_inc(qT_ready, 1)
                te.wait_ge(er_ready, t + 1)
                te.wait_ge(vbd_ready, t * 2 + 2)
                te.transpose(W1[:, 0:128], qkr[:, 256:384], ident).then_inc(kT_ready, 1)
                te.wait_ge(qT_copied, t + 1)
                te.wait_ge(kbd_ready, t * 2 + 2)
                te.wait_ge(drop_ready, t + 1)
                for j in range(2):
                    for b in range(2):
                        o = W[j][SLOT * b:SLOT * b + SLOT, 0:NKV * SEQ]
                        te.matmul(o, qT[:, j, SLOT * b:SLOT * b + SLOT], kbd[:, b, :], start=True, stop=False)
                        mm = te.matmul(o, ones_b[32 * b:32 * b + 32, :],
                                       drop[32 * b:32 * b + 32, NKV * j:NKV * j + NKV, :],
                                       start=False, stop=True)
                    mm.then_inc(s1_ready, 1)
                te.wait_ge(s1_sub, t * 2 + 2)
                te.wait_ge(p1_norm, t + 1)
                for g in range(NKV):
                    mm = te.transpose(W[g // 4][:, 128 * (g % 4):128 * (g % 4) + 128],
                                      pe[:, 128 * g:128 * g + 128], ident)
                    if g % 4 == 3:
                        mm.then_inc(pT_ready, 1)
                te.wait_ge(pT_copied, t * 2 + 2)
                for g in range(NKV):
                    for b in range(2):
                        c = 128 * (g // 4) + SLOT * b
                        mm = te.matmul(W0[32 * (g % 4):32 * (g % 4) + 32, c:c + SLOT], vbd[:, b, g, :],
                                       pT[:, g, SLOT * b:SLOT * b + SLOT], start=True, stop=True)
                mm.then_inc(oT_ready, 1)
                te.wait_ge(oT_copied, t * 2 + 2)
                for k in range(KD):
                    mm = te.matmul(W1[:, 0:D], oT[:, k, :], wo[:, k, :], start=k == 0, stop=k == KD - 1)
                mm.then_inc(o1_ready, 1)
                te.wait_ge(x1_ready, t * 2 + 2)
                for j in range(KD):
                    mm = te.transpose(W0[:, 128 * j:128 * j + 128], y1[:, 128 * j:128 * j + 128], ident)
                mm.then_inc(x1T_ready, 1)
                te.wait_ge(x1T_copied, t + 1)
                for q in range(4):
                    for k in range(KD):
                        mm = te.matmul(W1[:, 128 * q:128 * q + 128], wq2[:, k, 128 * q:128 * q + 128],
                                       x1T[:, k, :], start=k == 0, stop=k == KD - 1)
                mm.then_inc(q2_ready, 1)
                te.wait_ge(q2_copied, t * 4 + 4)

            te.wait_ge(wself_in, 96)
            te.wait_ge(const_in, 64)
            with te.Fori(0, TILES) as t:
                stage1(t)

            three = ((0, 0), (0, 1), (1, 0))
            cparts = (chi, clo)

            def kv_piece(m, k):
                c, r = k // TPC, k % TPC
                first = isinstance(m, int) and m == 0 and c == 0
                if r == 0:
                    te.wait_ge(chi_ready, m * NCH + (c + 1))
                    te.wait_ge(clo_ready, m * NCH + (c + 1))
                if r < 2:
                    if not first:
                        te.wait_ge(v_ready, m * NT + (TPC * c + r - 1))
                    if r == 0 and c == 0 and not first:
                        te.wait_ge(den_read, m)
                    n = 0
                    for wi, ci in three:
                        w = (wk_hi, wk_lo)[wi]
                        for kk in range(KD):
                            mm = te.matmul(W[r][:, 0:CH], w[:, kk, 128 * r:128 * r + 128],
                                           cparts[ci][:, c, kk, :], start=n == 0, stop=n == 5)
                            n += 1
                    mm.then_inc(w_ready[r], 1)
                else:
                    for bank in range(2):
                        i = 2 * (r - 2) + bank
                        if r == 2:
                            te.wait_ge(k_ready, m * (2 * NCH) + (2 * c + bank + 1))
                        else:
                            te.wait_ge(v_ready, m * NT + (TPC * c + bank + 1))
                        n = 0
                        for wi, ci in three:
                            w = (wv_hi, wv_lo)[wi]
                            for kk in range(KD):
                                mm = te.matmul(W[bank][0:CT, 0:D], cparts[ci][:, c, kk, CT * i:CT * i + CT],
                                               w[:, kk, :], start=n == 0, stop=n == 5)
                                n += 1
                        mm.then_inc(w_ready[bank], 1)

            def scores(n, par, i):
                if i == 0:
                    te.wait_ge(qbd_ready, n * 2 + 2)
                if i % TPC == 0:
                    te.wait_ge(k_ready, n * (2 * NCH) + 2 * (i // TPC + 1))
                if i >= 2:
                    te.wait_ge(p2_exp, n * NT + (i - 1))
                for q in range(4):
                    for part in range(2):
                        mm = te.matmul(SC[0:CT, i % 2, q // 2, QUAD * (q % 2):QUAD * (q % 2) + QUAD],
                                       kst[par][:, q, CT * i:CT * i + CT], qbd[par][part][:, q, :, :],
                                       start=part == 0, stop=part == 1)
                mm.then_inc(s2_ready, 1)

            def weigh(n, par, i):
                te.wait_ge(p2_clip, n * NT + (i + 1))
                te.wait_ge(v_ready, n * NT + (i + 1))
                for q in range(4):
                    mm = te.matmul(ACC[64 * (q % 2):64 * (q % 2) + 64, q // 2, 0:QUAD],
                                   v2[par][0:CT, i, 64 * q:64 * q + 64],
                                   p2[i % 3][:, QUAD * q:QUAD * q + QUAD],
                                   start=i == 0, stop=i == NT - 1)
                mm.then_inc(pv_done, 1)

            def attend(n, par, project_next=True):
                for i in range(NT):
                    scores(n, par, i)
                    if i < NT - 2 and project_next:
                        kv_piece(n + 1, i)
                    if i >= 2:
                        weigh(n, par, i - 2)
                weigh(n, par, NT - 2)
                if project_next:
                    kv_piece(n + 1, NT - 2)
                weigh(n, par, NT - 1)
                if project_next:
                    kv_piece(n + 1, NT - 1)
                te.wait_ge(p2_added, n * (NT - 1) + (NT - 1))
                if project_next:
                    te.wait_ge(v_ready, n * NT + (2 * NT - 1))
                else:
                    te.wait_ge(den_read, n + 1)
                for q in range(4):
                    mm = te.matmul(W0[64 * (q % 2):64 * (q % 2) + 64, QUAD * (q // 2):QUAD * (q // 2) + QUAD],
                                   ones[0:CT, :], psum2[:, QUAD * q:QUAD * q + QUAD], start=True, stop=True)
                mm.then_inc(den_ready, 1)

            for k in range(NT):
                kv_piece(0, k)
            with te.Fori(0, TILES - 1) as t:
                attend(t * 2, 0)
                attend(t * 2 + 1, 1)
            attend(B - 2, 0)
            attend(B - 1, 1, project_next=False)

            te.wait_ge(o2_ready, B)
            te.wait_ge(wq_done, 2)
            with te.Fori(0, TILES) as t:
                te.wait_ge(o3_biased, t * 2 + 2)
                for k in range(KD):
                    mm = te.matmul(W0[:, 0:D], oTb[:, k, :], wo2[:, k, :], start=k == 0, stop=k == KD - 1)
                mm.then_inc(d3_ready, 1)
                te.wait_ge(xq_ready, t + 1)
                W1b = W1[:, 0:128].bitcast(BF16)
                for k in range(KD):
                    mm = te.transpose(W1b[:, 128 * k:128 * k + 128], xq[:, 128 * k:128 * k + 128], ident_b[:, :])
                mm.then_inc(xqT_ready, 1)
                te.wait_ge(xqT_copied, t + 1)
                for j in range(2):
                    for k in range(KD):
                        mm = te.matmul(SC[:, 0, j, :], xqT[:, k, :], wup[:, k, 512 * j:512 * j + 512],
                                       start=k == 0, stop=k == KD - 1)
                mm.then_inc(up_ready, 1)
                te.wait_ge(h_ready, t + 1)
                for k in range(8):
                    mm = te.transpose(SC[:, 1, k // 4, 128 * (k % 4):128 * (k % 4) + 128],
                                      th[:, 128 * k:128 * k + 128], ident)
                mm.then_inc(hT_ready, 1)
                te.wait_ge(hThi_ready, t + 1)
                for k in range(8):
                    te.matmul(ACC[:, 0, 0:D], hT_hi[:, k, :], wdn[:, k, :], start=k == 0, stop=False)
                te.wait_ge(hTlo_ready, t + 1)
                for k in range(8):
                    mm = te.matmul(ACC[:, 0, 0:D], hT_lo[:, k, :], wdn[:, k, :], start=False, stop=k == 7)
                mm.then_inc(dn_ready, 1)

        @block.scalar
        def _(se):
            def stage1(t):
                se.wait_ge(rv_ready, t + 1)
                se.activation(er[0:64, :], W1[0:64, 0:SLOT], ACT.Exp, bias=nbr[0:64, :], scale=-1.0)\
                  .then_inc(er_ready, 1)
                se.wait_ge(qT_ready, t + 1)
                se.copy(qT.rearrange("p j n -> p (j n)"), W0[:, 0:256]).then_inc(qT_copied, 1)
                se.wait_ge(s1_sub, t * 2 + 2)
                se.activation(pe3, pe3, ACT.Exp, scale=SCALE).then_inc(p1_exp, 1)
                se.wait_ge(pT_ready, t * 2 + 2)
                se.copy(pT[:, 0:4, :].rearrange("p g n -> p (g n)"), W0[:, :]).then_inc(pT_copied, 1)
                se.wait_ge(oT_ready, t + 1)
                for j in range(2):
                    se.activation(oT[:, j, :], W0[:, 128 * j:128 * j + 128], ACT.Identity,
                                  bias=cc[:, C_BV1 + j:C_BV1 + j + 1]).then_inc(oT_copied, 1)
                se.wait_ge(x1T_ready, t + 1)
                se.copy(x1T.rearrange("p j n -> p (j n)"), W0[:, 0:256]).then_inc(x1T_copied, 1)
                se.wait_ge(q2_ready, t + 1)
                for q in range(4):
                    se.activation(q2_all[:, bass.ds(t, 1), q, :].rearrange("p o n -> p (o n)"),
                                  W1[:, 128 * q:128 * q + 128], ACT.Identity,
                                  bias=cc[:, C_BQ2 + q:C_BQ2 + q + 1]).then_inc(q2_copied, 1)

            se.wait_ge(set_cols, 2)
            with se.Fori(0, TILES) as t:
                stage1(t)

            def evacuate(m, par, k, item0, item1):
                c, r = k // TPC, k % TPC
                if r < 2:
                    bank, item = ((0, item0 + (3 * c + 1)), (1, item1 + (3 * c + 1)))[r]
                    se.wait_ge(w_ready[bank], item)
                    for h in range(2):
                        se.activation(kst[par][64 * h:64 * h + 64, 2 * r + h, CH * c:CH * c + CH],
                                      W[bank][64 * h:64 * h + 64, 0:CH], ACT.Identity,
                                      bias=cc[64 * h:64 * h + 64, C_BK2 + r:C_BK2 + r + 1])\
                          .then_inc(khi_ready, 1)
                else:
                    for bank, item in ((0, item0), (1, item1)):
                        se.wait_ge(w_ready[bank], item + (3 * c + r))
                        se.copy(v2[par][0:CT, TPC * c + 2 * (r - 2) + bank, :], W[bank][0:CT, 0:D])\
                          .then_inc(v_ready, 1)

            def attend(n, par, project_next=True):
                for i in range(NT):
                    se.wait_ge(s2_ready, n * NT + (i + 1))
                    if i >= 3:
                        se.wait_ge(pv_done, n * NT + (i - 2))
                        se.wait_ge(p2_added, n * (NT - 1) + max(i - 3, 1))
                    col = n * NT + i
                    se.activation(p2[i % 3].rearrange("p (a n) -> p a n", a=2),
                                  SC[0:CT, i % 2, :, 0:HQ], ACT.Exp,
                                  bias=mbias[:, bass.ds(col, 1)], scale=mscale[:, bass.ds(col, 1)])\
                      .then_inc(p2_exp, 1)
                    if project_next:
                        evacuate(n + 1, 1 - par, i, n * 9 + 9, n * 9 + 9)

            se.wait_ge(set_mask, 2)
            for k in range(NT):
                evacuate(0, 0, k, 0, 0)
            with se.Fori(0, TILES - 1) as t:
                attend(t * 2, 0)
                attend(t * 2 + 1, 1)
            attend(B - 2, 0)
            attend(B - 1, 1, project_next=False)

            se.wait_ge(o2_ready, B)
            with se.Fori(0, TILES) as t:
                for j in range(KD):
                    se.activation(oTb[:, j, :],
                                  oT_all[:, j, bass.ds(t, 1), :].rearrange("p o n -> p (o n)"), ACT.Identity,
                                  bias=cc[:, C_BV2 + j:C_BV2 + j + 1]).then_inc(o3_biased, 1)
                se.wait_ge(xqT_ready, t + 1)
                se.copy(xqT.rearrange("p j n -> p (j n)"), W1[:, 0:128].bitcast(BF16)).then_inc(xqT_copied, 1)
                se.wait_ge(up_ready, t + 1)
                se.activation(th.rearrange("p (a n) -> p a n", a=2), SC[:, 0, :, :], ACT.Tanh,
                              scale=small[:, 5:6]).then_inc(z_ready, 1)
                se.activation(z_half.rearrange("p (a n) -> p a n", a=2), SC[:, 0, :, :], ACT.Identity,
                              scale=small[:, 5:6]).then_inc(z_ready, 1)
                se.wait_ge(hT_ready, t + 1)
                se.copy(hT_hi.rearrange("p (a k) n -> p a (k n)", a=2), SC[:, 1, :, :]).then_inc(hThi_ready, 1)
                se.wait_ge(dn_ready, t + 1)

        @block.gpsimd
        def _(ge):
            ge.memset(ones[:, :], 1.0).then_inc(set_ones, 1)
            ge.memset(ones_b[:, :], 1.0).then_inc(set_ones, 1)
            ge.memset(half[:, :], -0.5).then_inc(set_ones, 1)
            ge.wait_ge(set_ones, 3)
            with ge.Fori(0, TILES) as t:
                ge.wait_ge(negm_ready, t + 1)
                ge.tensor_tensor(drop[:, :, :], spread(negm[:, :], 1, NH), spread(dh[0:64, :], 2, SEQ),
                                 ALU.mult).then_inc(drop_ready, 1)
                ge.wait_ge(y1_veps, t + 1)
                ge.tensor_tensor(rstd, veps, half[:, :], ALU.pow).then_inc(y1_rstd, 1)

            def split_low(m, par, c):
                ge.wait_ge(chi_ready, m * NCH + (c + 1))
                ge.tensor_tensor(clo[:, c, :, :], craw[:, (par * NCH + c) % 2, :, :], chi[:, c, :, :].bitcast(F32), ALU.subtract)\
                  .then_inc(clo_ready, 1)

            def attend(n, par, prep0=True, prep1=True):
                for i in range(NT):
                    if i == 0 and prep0:
                        split_low(n + 1, 1 - par, 2)
                    if i == 4 and prep1:
                        split_low(n + 2, par, 0)
                    if i == 8 and prep1:
                        split_low(n + 2, par, 1)
                    if i >= 1:
                        ge.wait_ge(p2_clip, n * NT + (i + 1))
                        if i >= 2:
                            ge.wait_ge(p2_added, n * (NT - 1) + (i - 1))
                        first = p2[0] if i == 1 else psum2
                        ge.tensor_tensor(psum2, first, p2[i % 3], ALU.add)\
                          .then_inc(p2_added, 1)

            for c in range(NCH):
                split_low(0, 0, c)
            split_low(1, 1, 0)
            split_low(1, 1, 1)
            with ge.Fori(0, TILES - 1) as t:
                attend(t * 2, 0)
                attend(t * 2 + 1, 1)
            attend(B - 2, 0, prep1=False)
            attend(B - 1, 1, prep0=False, prep1=False)

            with ge.Fori(0, TILES) as t:
                for s in range(4):
                    ge.wait_ge(v3_ready, t * 4 + (s + 1))
                    ge.tensor_tensor(small[:, 2:3], small[:, 1:2], half[:, :], ALU.pow).then_inc(pow_done, 1)

        @block.vector
        def _(ve):
            ve.wait_ge(const_in, 64)
            ve.tensor_copy(ident_b[:, :], ident)
            ve.memset(mark[:, :], 0.0)
            ve.tensor_scalar(nbr[:, :], cc[:, C_BR:C_BR + 1], -1.0, None, ALU.mult).then_inc(set_cols, 1)
            ve.tensor_scalar(rs[:, :], cc[:, C_RS:C_RS + 1], 0.0, 0.3, ALU.max, ALU.min).then_inc(set_cols, 1)
            ve.tensor_scalar(mbias[:, :], mski, 0.5, None, ALU.is_gt).then_inc(set_mask, 1)
            ve.wait_ge(set_mask, 1)
            ve.tensor_scalar(mscale[:, :], mbias[:, :], SCALE, None, ALU.mult)
            ve.tensor_scalar(mbias[:, :], mbias[:, :], CLIP, -CLIP, ALU.mult, ALU.add).then_inc(set_mask, 1)

            for hi, lo, r, arrived in ((wk_hi, wk_lo, wk_raw, wk_in), (wv_hi, wv_lo, wv_raw, wv_in)):
                ve.wait_ge(arrived, 16)
                r = r.rearrange("p (k n) -> p k n", k=KD)
                ve.tensor_copy(hi[:, :, :], r).then_inc(wkv_split, 1)
                ve.wait_ge(wkv_split, 1 if r is None else (1 if hi is wk_hi else 3))
                ve.tensor_tensor(lo[:, :, :], r, hi[:, :, :].bitcast(F32), ALU.subtract).then_inc(wkv_split, 1)

            for i, (r, arrived) in enumerate(((up_raw, wup_in), (down_raw, wdn_in))):
                ve.wait_ge(arrived, 16)
                ve.tensor_reduce(wsum[:, i:i + 1], r, AX.X, ALU.add, apply_absolute_value=True)\
                  .then_inc(wq_abs, 1)
            ve.wait_ge(wq_sum, 1)
            ve.tensor_scalar(wscale[:, :], W0[:, 0:2], 1.0 / (D * HID), 1e-8, ALU.mult, ALU.max)\
              .then_inc(wq_mean, 1)
            ve.wait_ge(wq_mean, 1)
            ve.reciprocal(winv[:, :], wscale[:, :]).then_inc(wq_inv, 1)
            ve.tensor_scalar(sgam[:, :], rc[:, R_FG:R_FG + D], wscale[:, 1:2], None, ALU.mult)
            ve.wait_ge(wq_inv, 1)
            for i, (r, o) in enumerate(((up_raw, wup), (down_raw, wdn))):
                ve.tensor_scalar(r, r, winv[:, i:i + 1], MAGIC, ALU.mult, ALU.add).then_inc(wq_scaled, 1)
                ve.wait_ge(wq_scaled, i + 1)
                ve.tensor_scalar(r, r, -MAGIC, 1.0, ALU.add, ALU.min).then_inc(wq_round, 1)
                ve.wait_ge(wq_round, i + 1)
                ve.tensor_scalar(o[:, :, :].rearrange("p k n -> p (k n)"), r, -1.0, None, ALU.max)\
                  .then_inc(wq_done, 1)

            def wait_apart(semaphore, value):
                ve.wait_ge(semaphore, value)
                ve.tensor_copy(mark[:, 1:2], mark[:, 0:1])

            def stage1(t):
                ve.wait_ge(qk_ready, t + 1)
                ve.tensor_tensor(qk, W0[:, 0:384], rc[:, R_BQK:R_BQK + 384], ALU.add).then_inc(qk_biased, 1)
                ve.wait_ge(qk_biased, t + 1)
                heads = "p (h d) -> p h d"
                q3, c3, r3 = (a.rearrange(heads, d=HD) for a in (qk, rcos, qkr))
                cos = kc[:, K_COS:K_COS + HD]
                ve.tensor_tensor(c3, q3, spread(cos, 1, 24), ALU.mult).then_inc(rope_cos, 1)
                for h in range(2):
                    o, i = (slice(0, 8), slice(8, 16))[::1 - 2 * h]
                    ve.tensor_tensor(r3[:, :, o], q3[:, :, i],
                                     spread(kc[:, K_SIN + o.start:K_SIN + o.stop], 1, 24), ALU.mult)\
                      .then_inc(rope_sin, 1)
                ve.wait_ge(rope_cos, t + 1)
                ve.wait_ge(rope_sin, t * 2 + 2)
                ve.tensor_tensor(qkr, qkr, rcos, ALU.add).then_inc(roped, 1)
                ve.wait_ge(er_ready, t + 1)
                for b in range(2):
                    ve.tensor_tensor(
                        vbd[:, b, :, :].rearrange("p g (j d) -> p g j d", j=2),
                        spread(W1[:, 128 + 128 * b:256 + 128 * b].rearrange(
                            "p (g d) -> p g d", d=HD), 2, 2),
                        spread(spread(dj, 2, HD), 1, NKV), ALU.mult).then_inc(vbd_ready, 1)
                ve.tensor_scalar(er[0:64, :], er[0:64, :], 1.0, None, ALU.add).then_inc(sig_plus, 1)
                ve.wait_ge(sig_plus, t + 1)
                ve.reciprocal(sg[0][0:64, 0:SEQ], er[0:64, 0:SEQ]).then_inc(sig_ready, 1)
                wait_apart(sig_ready, t + 1)
                cur = 0
                for r in range(4):
                    nxt = 1 + r % 2
                    ve.max(m8[0:64, :], sg[cur][0:64, :]).then_inc(top8, 1)
                    wait_apart(top8, t * 4 + (r + 1))
                    ve.match_replace(sg[nxt][0:64, :], m8[0:64, :], sg[cur][0:64, :], -1.0)\
                      .then_inc(top8_out, 1)
                    wait_apart(top8_out, t * 4 + (r + 1))
                    cur = nxt
                ve.tensor_scalar(negm[:, :], sg[cur][0:64, 0:SEQ], 0.0, NEG, ALU.is_ge, ALU.mult)\
                  .then_inc(negm_ready, 1)
                ve.wait_ge(x_in, t * 16 + 16)
                ve.tensor_tensor(xb, xt, rc[:, R_BO1:R_BO1 + D], ALU.add).then_inc(xb_ready, 1)
                ve.wait_ge(kT_ready, t + 1)
                for b in range(2):
                    ve.tensor_tensor(kbd[:, b, :].rearrange("p (g k) -> p g k", g=NKV),
                                     spread(W1[:, SLOT * b:SLOT * b + SEQ], 1, NKV),
                                     spread(d8, 2, SEQ), ALU.mult).then_inc(kbd_ready, 1)
                for j in range(2):
                    ve.wait_ge(s1_ready, t * 2 + (j + 1))
                    s3 = W[j][:, 0:NKV * SEQ].rearrange("p (g k) -> p g k", g=NKV)
                    ve.tensor_reduce(st_max[:, 8 * j:8 * j + 8], s3, AX.X, ALU.max).then_inc(s1_max, 1)
                    ve.wait_ge(s1_max, t * 2 + (j + 1))
                    ve.tensor_tensor(pe4[:, :, j, :], s3, spread(st_max[:, 8 * j:8 * j + 8], 2, SEQ),
                                     ALU.subtract).then_inc(s1_sub, 1)
                ve.wait_ge(p1_exp, t + 1)
                ve.tensor_reduce(st_sum, pe3, AX.X, ALU.add).then_inc(p1_sum, 1)
                ve.wait_ge(p1_sum, t + 1)
                ve.reciprocal(st_rec, st_sum).then_inc(p1_rec, 1)
                ve.wait_ge(p1_rec, t + 1)
                ve.tensor_tensor(pe3, pe3, spread(st_rec, 2, SEQ), ALU.mult).then_inc(p1_norm, 1)
                ve.wait_ge(pT_ready, t * 2 + 2)
                ve.tensor_copy(pT[:, 4:8, :].rearrange("p g n -> p (g n)"), W1[:, :])\
                  .then_inc(pT_copied, 1)
                ve.wait_ge(o1_ready, t + 1)
                ve.tensor_tensor(y1, W1[:, 0:D], xb, ALU.add).then_inc(y1_ready, 1)
                ve.wait_ge(y1_ready, t + 1)
                ve.bn_stats(stats, y1).then_inc(y1_stats, 1)
                wait_apart(y1_stats, t + 1)
                ve.bn_aggr(aggr, stats).then_inc(y1_aggr, 1)
                ve.wait_ge(y1_aggr, t + 1)
                ve.tensor_scalar(veps, aggr[:, 1:2], 1e-5, None, ALU.add).then_inc(y1_veps, 1)
                ve.wait_ge(y1_rstd, t + 1)
                ve.tensor_scalar(y1, y1, aggr[:, 0:1], rstd, ALU.subtract, ALU.mult).then_inc(x1_ready, 1)
                ve.wait_ge(x1_ready, t * 2 + 1)
                ve.tensor_copy(x1_all[:, bass.ds(t, 1), :].rearrange("p o n -> p (o n)"), y1)\
                  .then_inc(x1_ready, 1)

            ve.wait_ge(wq_done, 2)
            ve.memset(pe, 0.0).then_inc(den_read, 1)
            ve.memset(sg[0][0:64, SEQ:SEQ + 4], 2.0)
            with ve.Fori(0, TILES) as t:
                stage1(t)

            def split_high(m, par, c):
                ve.wait_ge(c_in[c], m * 16 + 16)
                ve.tensor_copy(chi[:, c, :, :], craw[:, (par * NCH + c) % 2, :, :]).then_inc(chi_ready, 1)

            def keys_low(m, par, k):
                c, r = k // TPC, k % TPC
                if r >= 2:
                    return
                ve.wait_ge(khi_ready, m * 12 + (4 * c + 2 * r + 2))
                for h in range(2):
                    here, there = slice(64 * h, 64 * h + 64), slice(64 - 64 * h, 128 - 64 * h)
                    lo = ve.scalar_tensor_tensor(
                        kst[par][there, 2 * r + h, CH * c:CH * c + CH], W[r][here, 0:CH],
                        cc[here, C_BK2 + r:C_BK2 + r + 1],
                        kst[par][here, 2 * r + h, CH * c:CH * c + CH].bitcast(F32),
                        ALU.add, ALU.subtract)
                lo.then_inc(k_ready, 1)

            def queries(n, t, b, par, step):
                src = q2_all[:, bass.ds(t, 1), :, SLOT * b:SLOT * b + SEQ].rearrange("p o q n -> p (o q) n")
                if step == 0:
                    ve.tensor_copy(qh[:, :, :], src).then_inc(qh_ready, 1)
                elif step == 1:
                    ve.wait_ge(qh_ready, n + 1)
                    ve.tensor_tensor(ql[:, :, :], src, qh[:, :, :].bitcast(F32), ALU.subtract)\
                      .then_inc(ql_ready, 1)
                else:
                    part = (qh, ql)[step - 2]
                    ve.wait_ge(ql_ready, n + 1)
                    ve.tensor_tensor(qbd[par][step - 2][:, :, :, :],
                                     spread(part[:, :, :].bitcast(F32), 2, 4),
                                     spread(spread(d4, 2, SEQ), 1, 4), ALU.mult).then_inc(qbd_ready, 1)

            def attend(n, t, b, t_next, b_next, prep0=True, prep1=True):
                par = b
                for i in range(NT):
                    ve.wait_ge(p2_exp, n * NT + (i + 1))
                    ve.tensor_scalar(p2[i % 3], p2[i % 3], EXP_MAX, EXP_MIN, ALU.min, ALU.max)\
                      .then_inc(p2_clip, 1)
                    if i == 0 and prep0:
                        split_high(n + 1, 1 - par, 2)
                    if i == 4 and prep1:
                        split_high(n + 2, par, 0)
                    if i == 8 and prep1:
                        split_high(n + 2, par, 1)
                    if prep0:
                        if 5 <= i < 9:
                            queries(n + 1, t_next, b_next, 1 - par, i - 5)
                        keys_low(n + 1, 1 - par, i)
                ve.wait_ge(pv_done, n * NT + NT)
                ve.tensor_copy(accs.rearrange("p (a n) -> p a n", a=2), ACC[:, :, 0:QUAD]).then_inc(acc_copied, 1)
                ve.wait_ge(den_ready, n + 1)
                ve.reciprocal(rec2, W0[:, 0:HQ]).then_inc(den_read, 1)
                ve.wait_ge(den_read, n + 2)
                h4 = "p (a h q) -> p a h q"
                ve.tensor_tensor(recm.rearrange(h4, a=2, h=4), rec2.rearrange(h4, a=2, h=4),
                                 spread(spread(d4, 2, SEQ), 1, 2), ALU.mult).then_inc(den_masked, 1)
                ve.wait_ge(den_masked, n + 1)
                ve.wait_ge(acc_copied, n + 1)
                ve.tensor_tensor(accm, accs, recm, ALU.mult).then_inc(acc_scaled, 1)
                wait_apart(acc_scaled, n + 1)
                ve.tensor_reduce(oT_all[:, :, bass.ds(t, 1), SLOT * b:SLOT * b + SEQ].rearrange(
                                     "p a o q -> p (a o) q"),
                                 accm.rearrange("p (a h q) -> p a q h", a=2, h=4), AX.X, ALU.add)\
                  .then_inc(o2_ready, 1)

            for c in range(NCH):
                split_high(0, 0, c)
            for s in range(4):
                queries(0, 0, 0, 0, s)
            for k in range(NT):
                keys_low(0, 0, k)
            for c in range(2):
                ve.wait_ge(v_ready, TPC * (c + 1))
                split_high(1, 1, c)
            with ve.Fori(0, TILES - 1) as t:
                attend(t * 2, t, 0, t, 1)
                attend(t * 2 + 1, t, 1, t + 1, 0)
            attend(B - 2, TILES - 1, 0, TILES - 1, 1, prep1=False)
            attend(B - 1, TILES - 1, 1, None, None, prep0=False, prep1=False)

            K3 = 20

            def stage3(t):
                done = [0]

                def then(ins):
                    done[0] += 1
                    ins.then_inc(d3_steps, 1)
                    wait_apart(d3_steps, t * K3 + done[0])

                def layer_norm(o, v, s):
                    then(ve.bn_stats(stats3, v))
                    then(ve.bn_aggr(small[:, 6:8], stats3))
                    ve.tensor_scalar(small[:, 1:2], small[:, 7:8], 1e-5, None, ALU.add).then_inc(v3_ready, 1)
                    ve.wait_ge(pow_done, t * 4 + (s + 1))
                    return ve.tensor_scalar(o, v, small[:, 6:7], small[:, 2:3], ALU.subtract, ALU.mult)

                ve.tensor_tensor(xb3, x1_all[:, bass.ds(t, 1), :].rearrange("p o n -> p (o n)"),
                                 rc[:, R_LNB:R_LNB + D], ALU.add)
                ve.wait_ge(d3_ready, t + 1)
                then(ve.tensor_tensor(dl, W0[:, 0:D], rc[:, R_BO2:R_BO2 + D], ALU.add))
                then(ve.tensor_scalar(dl, dl, rs[:, :], None, ALU.mult))
                then(layer_norm(dl, dl, 0))
                then(ve.tensor_tensor(dl, dl, rc[:, R_LNG:R_LNG + D], ALU.mult))
                then(ve.tensor_tensor(x2, dl, xb3, ALU.add))
                then(layer_norm(x2, x2, 1))
                then(ve.tensor_tensor_reduce(xn, x2, x2, 1.0, 0.0, ALU.mult, ALU.add, small[:, 0:1]))
                ve.tensor_scalar(small[:, 1:2], small[:, 0:1], 1.0 / D, 1e-6, ALU.mult, ALU.add)\
                  .then_inc(v3_ready, 1)
                ve.wait_ge(pow_done, t * 4 + 3)
                then(ve.scalar_tensor_tensor(xn, x2, small[:, 2:3], rc[:, R_NW:R_NW + D], ALU.mult, ALU.mult))
                then(ve.tensor_reduce(small[:, 3:4], xn, AX.X, ALU.max, apply_absolute_value=True))
                then(ve.tensor_scalar(small[:, 3:4], small[:, 3:4], 1e-8, None, ALU.max))
                then(ve.reciprocal(small[:, 4:5], small[:, 3:4]))
                then(ve.tensor_scalar(xn, xn, QB, small[:, 4:5], ALU.mult, ALU.mult))
                ve.tensor_scalar(small[:, 5:6], small[:, 3:4], 0.5 / QB, wscale[:, 0:1], ALU.mult, ALU.mult)
                ve.tensor_scalar(xq, xn, MAGIC, -MAGIC, ALU.add, ALU.add).then_inc(xq_ready, 1)
                ve.wait_ge(z_ready, t * 2 + 2)
                ve.scalar_tensor_tensor(th, th, 1.0, z_half, ALU.add, ALU.mult).then_inc(h_ready, 1)
                ve.wait_ge(hThi_ready, t + 1)
                ve.tensor_tensor(hT_lo.rearrange("p (a k) n -> p a (k n)", a=2), SC[:, 1, :, :],
                                 hT_hi.bitcast(F32).rearrange("p (a k) n -> p a (k n)", a=2),
                                 ALU.subtract).then_inc(hTlo_ready, 1)
                ve.wait_ge(dn_ready, t + 1)
                then(ve.tensor_tensor(xb3, ACC[:, 0, 0:D], sgam[:, :], ALU.mult))
                then(ve.scalar_tensor_tensor(x2, x2, 2.0, xb3, ALU.mult, ALU.add))
                layer_norm(y3, x2, 3).then_inc(y3_ready, 1)
                assert done[0] == K3, done[0]
                ve.wait_ge(y_out, t * 32 + 32)

            with ve.Fori(0, TILES) as t:
                stage3(t)


def kernel(**inputs):
    import concourse.bacc as bacc
    from concourse.bass_utils import run_bass_kernel_spmd

    a = {k: np.asarray(v) for k, v in inputs.items()}

    def padded(rows):
        o = np.zeros((B, SLOT, rows.shape[-1]), np.float32)
        o[:, :SEQ] = rows
        return o.reshape(TILES, 2 * SLOT, rows.shape[-1])

    order = np.concatenate([np.arange(HD) + HD * h for j in range(2) for h in range(j, NH, 2)])
    x = padded(a["x"])
    quads = np.concatenate([np.arange(64 * q, 64 * q + 64) for q in range(4) for _ in range(2)])
    twice = np.concatenate([np.arange(HD) + HD * (h // 2) for h in range(NH)])
    w_r = np.zeros((D, 32), np.float32)
    w_r[:, :NH] = a["L0_attn_Wr"]
    rows = np.concatenate([
        a["L0_attn_bq"][order], a["L0_attn_bk"], a["L0_attn_bo"], a["L0_xattn_bo"],
        a["L0_xattn_ln_gamma"], a["L0_xattn_ln_beta"], a["L0_ffn_norm_weight"], a["L0_ffn_gamma"]])
    cols = np.zeros((128, C_ALL), np.float32)
    cols[:, C_BV1:C_BV1 + 2] = a["L0_attn_bv"][twice].reshape(2, 128).T
    cols[:, C_BQ2:C_BQ2 + 4] = a["L0_xattn_bq"][quads].reshape(4, 128).T
    cols[:, C_BK2:C_BK2 + 2] = a["L0_xattn_bk"].reshape(2, 128).T
    cols[:, C_BV2:C_BV2 + 2] = a["L0_xattn_bv"].reshape(2, 128).T
    for b in range(2):
        cols[32 * b:32 * b + NH, C_BR] = a["L0_attn_br"]
    cols[:, C_RS] = a["L0_xattn_residual_scale"]

    p = np.arange(128)[:, None]
    consts = np.zeros((128, K_ALL), np.float32)
    consts[:, K_ID:K_ID + 128] = p == np.arange(128)
    consts[:, K_D8:K_D8 + 8] = p // HD == np.arange(8)
    consts[:, K_D4:K_D4 + 4] = (p // HD) % 4 == np.arange(4)
    consts[:, K_DJ:K_DJ + 2] = p // SLOT == np.arange(2)
    heads = np.concatenate([np.arange(j, NH, 2) for j in range(2)])
    consts[:64, K_DH:K_DH + NH] = p[:64] % 32 == heads
    inv_freq = (1.0 / np.float32(1000000.0) ** (np.arange(0, HD, 2, dtype=np.float32) / HD)).astype(np.float32)
    freqs = (np.arange(SEQ, dtype=np.float32)[:, None] * inv_freq).astype(np.float32)
    for b in range(2):
        r = slice(SLOT * b, SLOT * b + SEQ)
        consts[r, K_COS:K_COS + HD] = np.tile(np.cos(freqs), 2)
        consts[r, K_SIN:K_SIN + HD] = np.concatenate([-np.sin(freqs), np.sin(freqs)], 1)

    arrays = {
        "x": x,
        "xT": x.reshape(TILES * 128, D).T,
        "ctxT": a["ctx_2048"].transpose(0, 2, 1),
        "mask": a["mask_BxS2_ik0"].reshape(B * NT, CT).T,
        "w_qk": np.concatenate([a["L0_attn_Wq"][:, order], a["L0_attn_Wk"]], 1),
        "w_v": a["L0_attn_Wv"],
        "w_r": w_r,
        "w_o": a["L0_attn_Wo"],
        "w_q2": a["L0_xattn_Wq"].T[:, quads],
        "w_k2": a["L0_xattn_Wk"].T,
        "w_v2": a["L0_xattn_Wv"].T,
        "w_o2": a["L0_xattn_Wo"].T,
        "w_up": a["L0_ffn_weight_up"].T,
        "w_down": a["L0_ffn_weight_down"].T,
        "rows": rows,
        "cols": cols,
        "consts": consts,
    }
    nc = bacc.Bacc("TRN2", target_bir_lowering=False, num_devices=1)
    feeds, args = {}, []
    for name, v in arrays.items():
        v = np.ascontiguousarray(v)
        feeds[f"in_{name}"] = v
        args.append(nc.dram_tensor(f"in_{name}", v.shape, mybir.dt.from_np(v.dtype), kind="ExternalInput").ap())
    out = nc.dram_tensor("out", (B, SEQ, D), F32, kind="ExternalOutput").ap()
    build(nc, *args, out)
    r = run_bass_kernel_spmd(nc, [feeds], core_ids=[0])
    return r.results[0]["out"]
```

```python
from contextlib import ExitStack

import numpy as np

import concourse.bass as bass
from concourse import mybir

F32 = mybir.dt.float32
F32R = mybir.dt.float32r
BF16 = mybir.dt.bfloat16
I32 = mybir.dt.int32
ALU = mybir.AluOpType
ACT = mybir.ActivationFunctionType
AX = mybir.AxisListType

B, SEQ, D = 16, 56, 256
CTX = 1500
NH, HD = 16, 16
NKV = 8
HID = 1024
TOPK = SEQ // 2
TILES = B // 2
G3 = 4
GROUPS = TILES // G3
SLOT = 64
KD = D // 128
CT = 125
NT = CTX // CT
NCH = 3
CH = CTX // NCH
TPC = NT // NCH
QUAD = 4 * SEQ
HQ = 2 * QUAD
SCALE = float(HD) ** -0.5
CLIP = 50.0
EXP_MAX = float(np.exp(np.float64(CLIP)))
EXP_MIN = float(np.exp(np.float64(-CLIP)))
NEG = -1e30
MAGIC = 1.5 * 2.0 ** 23
QB = 127.0
R_BQK, R_BO1, R_BO2, R_LNG, R_LNB, R_NW, R_FG = 0, 384, 640, 896, 1152, 1408, 1664
R_ALL = 1920
C_BV1, C_BQ2, C_BK2, C_BV2, C_BR, C_RS = 0, 2, 6, 8, 10, 11
C_ALL = 12
K_ID, K_D8, K_D4, K_DJ, K_DH, K_COS, K_SIN = 0, 128, 136, 140, 142, 158, 174
K_ALL = 190
LAG = 4


def spread(ap, axis, n):
    ap = ap.unsqueeze(axis)
    shape = list(ap.shape)
    shape[axis] = n
    return ap.to_broadcast(shape)


def build(nc, x, xT, ctxT, mask, w_qk, w_v, w_r, w_o, w_q2, w_k2, w_v2, w_o2, w_up, w_down,
          rows, cols, consts, out):
    with ExitStack() as ctx:
        def sb(name, shape, dt=F32):
            return ctx.enter_context(nc.sbuf_tensor(name, shape, dt))

        def sem(name):
            return ctx.enter_context(nc.semaphore(name))

        SC = ctx.enter_context(nc.psum_tensor("SC", [128, 2, 2, 512], F32))
        ACC = ctx.enter_context(nc.psum_tensor("ACC", [128, 2, 512], F32))
        W0 = ctx.enter_context(nc.psum_tensor("W0", [128, 512], F32))
        W1 = ctx.enter_context(nc.psum_tensor("W1", [128, 512], F32))
        W = [W0, W1]
        Wb = [w[:, :].bitcast(BF16) for w in W]

        kc = sb("kc", [128, K_ALL])
        ident = kc[:, K_ID:K_ID + 128]
        d8 = kc[:, K_D8:K_D8 + 8]
        d4 = kc[:, K_D4:K_D4 + 4]
        dj = kc[:, K_DJ:K_DJ + 2]
        dh = kc[:, K_DH:K_DH + 16]
        rc = sb("rc", [128, R_ALL])
        cc = sb("cc", [128, C_ALL])
        ident_b = sb("ident_b", [128, 128], BF16)
        ones = sb("ones", [128, 64])
        ones_b = sb("ones_b", [128, 64], BF16)
        half = sb("half", [128, G3])
        mark = sb("mark", [1, 2])
        pbuf = sb("pbuf", [128, 4 * 2 * HQ])
        wqk, wv, wr, wo, wq2 = (
            pbuf[:, KD * o:KD * (o + n)].rearrange("p (k n) -> p k n", k=KD)
            for o, n in ((0, 384), (384, 128), (512, 32), (544, D), (800, 512)))
        wo2 = sb("wo2", [128, KD, D])
        wk_hi = sb("wk_hi", [128, KD, D], F32R)
        wk_lo = sb("wk_lo", [128, KD, D], F32R)
        wv_hi = sb("wv_hi", [128, KD, D], F32R)
        wv_lo = sb("wv_lo", [128, KD, D], F32R)
        wup = sb("wup", [128, KD, HID], BF16)
        wdn = sb("wdn", [128, HID // 128, D], F32R)
        wsum = sb("wsum", [128, 2])
        wscale = sb("wscale", [128, 2])
        winv = sb("winv", [128, 2])
        sgam = sb("sgam", [128, D])
        nbr = sb("nbr", [128, 1])
        rs = sb("rs", [128, 1])
        mscale = sb("mscale", [CT, B * NT])
        mbias = sb("mbias", [CT, B * NT])

        x1_all = sb("x1_all", [128, TILES, D])
        q2_all = sb("q2_all", [128, TILES, 4, 128])
        oT_all = q2_all[:, :, 0:KD, :].rearrange("p t j n -> p j t n")

        craw = sb("craw", [128, 2, KD, CH])
        chi = sb("chi", [128, NCH, KD, CH], F32R)
        clo = sb("clo", [128, NCH, KD, CH], F32R)
        with ExitStack() as lent:
            early = lent.enter_context(nc.sbuf_tensor("early", [128, 2 * 4 * CTX], F32))
        kst = [sb(f"kst{i}", [128, 4, CTX], F32R) for i in range(2)]
        v2 = [sb(f"v2_{i}", [128, NT, D]) for i in range(2)]
        p2 = [pbuf[0:CT, 2 * HQ * i:2 * HQ * i + 2 * HQ] for i in range(3)]
        psum2 = pbuf[0:CT, 6 * HQ:8 * HQ]
        qh = sb("qh", [128, 4, SEQ], F32R)
        ql = sb("ql", [128, 4, SEQ], F32R)
        qbd = [[sb(f"qbd{i}{k}", [128, 4, 4, SEQ], F32R) for k in range(2)] for i in range(2)]

        kbd = sb("kbd", [128, 2, NKV * SEQ])
        pT = sb("pT", [128, NKV, 128])
        vbd = sb("vbd", [128, 2, NKV, 32])

        raw = [v2[i][:, :, :].rearrange("p a n -> p (a n)") for i in range(2)]
        at = [0]

        def cut(n):
            i, o = at[0] // (NT * D), at[0] % (NT * D)
            if o + n > NT * D:
                i, o = i + 1, 0
            at[0] = i * NT * D + o + n
            return raw[i][:, o:o + n]

        early_at = [0]

        def cut_early(n):
            early_at[0] += n
            assert early_at[0] <= 8 * CTX
            return early[:, early_at[0] - n:early_at[0]]

        class Tile:
            pass

        T1 = [Tile(), Tile()]
        for u, cut1 in enumerate((cut, cut_early)):
            m = T1[u]
            m.W = (W0, W1) if u == 0 else (SC[:, 0, 0, :], SC[:, 0, 1, :])
            m.P = (ACC[:, 0, :], ACC[:, 1, :]) if u == 0 else (SC[:, 1, 0, :], SC[:, 1, 1, :])
            m.xTt = cut1(KD * 128).rearrange("p (k n) -> p k n", k=KD)
            m.xt = cut1(D)
            m.xb = cut1(D)
            m.qk = cut1(384)
            m.rcos = cut1(384)
            m.qkr = cut1(384)
            m.qT = cut1(256).rearrange("p (j n) -> p j n", j=2)
            m.pe = cut1(2 * NKV * SLOT)
            m.pe4 = m.pe.rearrange("p (g j k) -> p g j k", g=NKV, j=2)[:, :, :, 0:SEQ]
            m.pe3 = m.pe.rearrange("p (h k) -> p h k", k=SLOT)[:, :, 0:SEQ]
            m.st_max = cut1(16)
            m.st_sum = cut1(16)
            m.st_rec = cut1(16)
            m.oT = cut1(256).rearrange("p (j n) -> p j n", j=2)
            m.y1 = cut1(D)
            m.stats = cut1(6)
            m.aggr = cut1(2)
            m.veps = cut1(1)
            m.rstd = cut1(1)
            m.x1T = cut1(256).rearrange("p (j n) -> p j n", j=2)
        T1[0].kbd, T1[0].pT, T1[0].vbd = kbd, pT, vbd
        T1[1].kbd = cut_early(2 * NKV * SEQ).rearrange("p (b n) -> p b n", b=2)
        T1[1].pT = cut_early(NKV * 128).rearrange("p (g n) -> p g n", g=NKV)
        T1[1].vbd = cut_early(2 * NKV * 32).rearrange("p (b g n) -> p b g n", b=2, g=NKV)
        er = cut(64)
        sg = [cut(SEQ + 4) for _ in range(3)]
        m8 = cut(8)
        negm = sb("negm", [128, SEQ], BF16)
        drop = cut_early(NH * SEQ // 2).bitcast(BF16).rearrange("p (h k) -> p h k", h=NH)
        at[0] = 0
        early_at[0] = 0
        wide = G3 * D
        oTb = cut_early(KD * G3 * 128).rearrange("p (j n) -> p j n", j=KD)
        xb3, dl, x2, xn = (cut_early(wide).rearrange("p (i n) -> p i n", i=G3) for _ in range(4))
        xq = cut_early(wide // 2).bitcast(BF16).rearrange("p (i n) -> p i n", i=G3)
        xqT = cut_early(wide // 2).bitcast(BF16).rearrange("p (i j n) -> p i j n", i=G3, j=KD)
        th = [cut_early(HID) for _ in range(G3)]
        stats3 = cut(6 * G3).rearrange("p (i n) -> p i n", i=G3)
        mv3 = cut(2 * G3).rearrange("p (i n) -> p i n", i=G3)
        ssq3, eps3, rstd3, amax3, rmax3, s5 = (cut(G3) for _ in range(6))
        bo2rs = cut(D)
        hT = [[c[:, :, :, :].rearrange("p c k n -> p (c k n)")[:, HID * i:HID * i + HID].rearrange(
            "p (k n) -> p k n", k=8) for c in (chi, clo)] for i in range(2)]
        up_raw, down_raw = (raw[i][:, 0:2 * HID] for i in range(2))
        wk_raw, wv_raw = (raw[0][:, 2 * HID + 512 * i:2 * HID + 512 * i + 512] for i in range(2))
        mski = kbd[0:CT, 0, 0:B * NT].bitcast(I32)
        accm, denm = kbd[:, 0, :], kbd[:, 1, :]
        acc_own, den_own, rec_own = (
            pT[:, :, :].rearrange("p g n -> p (g n)")[:, 128 * i:128 * i + 2 * SEQ] for i in range(3))

        const_in = sem("const_in")
        wself_in = sem("wself_in")
        wk_in = sem("wk_in")
        wv_in = sem("wv_in")
        wup_in = sem("wup_in")
        wdn_in = sem("wdn_in")
        x_in = [sem(f"x_in{u}") for u in range(2)]
        xT_in = [sem(f"xT_in{u}") for u in range(2)]
        c_in = [sem(f"c_in{c}") for c in range(NCH)]
        y_out = sem("y_out")
        set_ones = sem("set_ones")
        set_cols = sem("set_cols")
        set_mask = sem("set_mask")
        wkv_split = sem("wkv_split")
        wq_abs = sem("wq_abs")
        wq_sum = sem("wq_sum")
        wq_mean = sem("wq_mean")
        wq_inv = sem("wq_inv")
        wq_scaled = sem("wq_scaled")
        wq_round = sem("wq_round")
        wq_done = sem("wq_done")
        qk_ready = sem("qk_ready")
        rv_ready = sem("rv_ready")
        qk_biased = sem("qk_biased")
        er_ready = sem("er_ready")
        vbd_ready = sem("vbd_ready")
        rope_cos = sem("rope_cos")
        rope_sin = sem("rope_sin")
        roped = sem("roped")
        qT_ready = sem("qT_ready")
        kT_ready = sem("kT_ready")
        qT_copied = sem("qT_copied")
        kbd_ready = sem("kbd_ready")
        sig_plus = sem("sig_plus")
        sig_ready = sem("sig_ready")
        top8 = sem("top8")
        top8_out = sem("top8_out")
        negm_ready = sem("negm_ready")
        drop_ready = sem("drop_ready")
        s1_ready = sem("s1_ready")
        s1_max = sem("s1_max")
        s1_sub = sem("s1_sub")
        p1_exp = sem("p1_exp")
        p1_sum = sem("p1_sum")
        p1_rec = sem("p1_rec")
        p1_norm = sem("p1_norm")
        pT_ready = sem("pT_ready")
        pTa_copied = sem("pTa_copied")
        pTb_copied = sem("pTb_copied")
        oT_ready = sem("oT_ready")
        oT_copied = sem("oT_copied")
        o1_ready = sem("o1_ready")
        xb_ready = sem("xb_ready")
        y1_ready = sem("y1_ready")
        y1_stats = sem("y1_stats")
        y1_aggr = sem("y1_aggr")
        y1_veps = sem("y1_veps")
        y1_rstd = sem("y1_rstd")
        x1_ready = sem("x1_ready")
        x1T_ready = sem("x1T_ready")
        x1T_copied = sem("x1T_copied")
        q2_ready = sem("q2_ready")
        q2_copied = sem("q2_copied")
        chi_ready = sem("chi_ready")
        clo_ready = sem("clo_ready")
        w_ready = [sem("w0_ready"), sem("w1_ready")]
        khi_ready = sem("khi_ready")
        k_ready = sem("k_ready")
        v_ready = sem("v_ready")
        qh_ready = sem("qh_ready")
        ql_ready = sem("ql_ready")
        qbd_ready = sem("qbd_ready")
        s2_ready = sem("s2_ready")
        p2_exp = sem("p2_exp")
        p2_clip = sem("p2_clip")
        p2_added = sem("p2_added")
        pv_done = sem("pv_done")
        den_ready = sem("den_ready")
        acc_read = sem("acc_read")
        acc_folded = sem("acc_folded")
        den_read = sem("den_read")
        den_folded = sem("den_folded")
        rec_ready = sem("rec_ready")
        o2_ready = sem("o2_ready")
        bo2_scaled = sem("bo2_scaled")
        o3_biased = sem("o3_biased")
        d3_ready = sem("d3_ready")
        d3_steps = sem("d3_steps")
        v3_ready = sem("v3_ready")
        pow_done = sem("pow_done")
        xq_ready = sem("xq_ready")
        xqT_ready = sem("xqT_ready")
        xqT_copied = sem("xqT_copied")
        up_ready = sem("up_ready")
        z_ready = sem("z_ready")
        h_ready = sem("h_ready")
        hT_ready = sem("hT_ready")
        hThi_ready = sem("hThi_ready")
        hTlo_ready = sem("hTlo_ready")
        dn_ready = sem("dn_ready")
        dn_read = sem("dn_read")
        y3_ready = sem("y3_ready")

        block = ctx.enter_context(nc.Block())

        @block.sync
        def _(sp):
            sp.dma_start(kc[:, :], consts).then_inc(const_in, 16)
            sp.dma_start(cc[:, :], cols).then_inc(const_in, 16)
            sp.dma_start(rc[:, :], rows.partition_broadcast(128)).then_inc(const_in, 16)
            sp.dma_start(wqk, w_qk.rearrange("(k p) n -> p k n", p=128)).then_inc(wself_in, 16)
            sp.dma_start(wv, w_v.rearrange("(k p) n -> p k n", p=128)).then_inc(wself_in, 16)
            sp.dma_start(wr, w_r.rearrange("(k p) n -> p k n", p=128)).then_inc(wself_in, 16)
            sp.dma_start(wo, w_o.rearrange("(k p) n -> p k n", p=128)).then_inc(wself_in, 16)
            sp.dma_start(wq2, w_q2.rearrange("(k p) n -> p k n", p=128)).then_inc(wself_in, 16)
            sp.dma_start(wo2[:, :, :], w_o2.rearrange("(k p) n -> p k n", p=128)).then_inc(wself_in, 16)
            sp.dma_start(mski, mask).then_inc(const_in, 16)
            sp.dma_start(wk_raw.rearrange("p (k n) -> p k n", k=KD),
                         w_k2.rearrange("(k p) n -> p k n", p=128)).then_inc(wk_in, 16)
            sp.dma_start(wv_raw.rearrange("p (k n) -> p k n", k=KD),
                         w_v2.rearrange("(k p) n -> p k n", p=128)).then_inc(wv_in, 16)
            sp.dma_start(up_raw.rearrange("p (k n) -> p k n", k=KD),
                         w_up.rearrange("(k p) n -> p k n", p=128)).then_inc(wup_in, 16)
            sp.dma_start(down_raw.rearrange("p (k n) -> p k n", k=HID // 128),
                         w_down.rearrange("(k p) n -> p k n", p=128)).then_inc(wdn_in, 16)


            def load_context(b, c, slot):
                sp.dma_start(craw[:, slot, :, :],
                             ctxT[bass.ds(b, 1), :, c * CH:(c + 1) * CH].rearrange(
                                 "o (k p) n -> p (o k) n", p=128)).then_inc(c_in[c], 16)

            for c in range(2):
                load_context(0, c, c)
            sp.wait_ge(wkv_split, 4)
            sp.wait_ge(wq_done, 2)
            for u in range(2):
                sp.dma_start(T1[u].xTt, xT[:, 128 * u:128 * u + 128].rearrange(
                    "(k p) n -> p k n", p=128)).then_inc(xT_in[u], 16)
                sp.dma_start(T1[u].xt, x[u, :, :]).then_inc(x_in[u], 16)
            with sp.Fori(1, TILES // 2) as r:
                for u in range(2):
                    sp.wait_ge(rv_ready, r * 2 + (u - 1))
                    sp.dma_start(T1[u].xTt, xT[:, bass.ds((r * 2 + u) * 128, 128)].rearrange(
                        "(k p) n -> p k n", p=128)).then_inc(xT_in[u], 16)
                for u in range(2):
                    sp.wait_ge(xb_ready, r * 2 + (u - 1))
                    sp.dma_start(T1[u].xt, x[bass.ds(r * 2 + u, 1), :, :].rearrange(
                        "o p n -> p (o n)")).then_inc(x_in[u], 16)
            def next_chunks(b, par, first=0):
                for c in range(first, NCH):
                    sp.wait_ge(clo_ready, b * NCH + (c - 1))
                    load_context(b, c, (par * NCH + c) % 2)

            next_chunks(0, 0, first=2)
            next_chunks(1, 1)
            with sp.Fori(1, TILES) as t:
                next_chunks(t * 2, 0)
                next_chunks(t * 2 + 1, 1)
            with sp.Fori(0, GROUPS) as g:
                sp.wait_ge(y3_ready, g + 1)
                for h in range(2):
                    sp.dma_start(out[bass.ds(g * (2 * G3), 2 * G3), :, :].rearrange(
                                     "(i h) p n -> h p i n", h=2)[h],
                                 x1_all[SLOT * h:SLOT * h + SEQ, bass.ds(g * G3, G3), :]).then_inc(y_out, 16)
            sp.wait_ge(y_out, 32 * GROUPS)

        @block.tensor
        def _(te):
            te.wait_ge(set_ones, 3)
            te.wait_ge(wq_abs, 2)
            te.matmul(W0[0:64, 0:2], ones[:, :], wsum[:, :], start=True, stop=True).then_inc(den_ready, 1)
            te.matmul(W0[64:128, 0:2], ones[:, :], wsum[:, :], start=True, stop=True).then_inc(wq_sum, 1)
            te.wait_ge(wq_mean, 1)

            def stage1(r, u, phase):
                t, m = r * 2 + u, T1[u]
                if phase == 0:
                    te.wait_ge(xT_in[u], r * 16 + 16)
                    for k in range(KD):
                        mm = te.matmul(m.P[0][:, 0:384], m.xTt[:, k, :], wqk[:, k, :], start=k == 0, stop=k == KD - 1)
                    mm.then_inc(qk_ready, 1)
                    for b in range(2):
                        for k in range(KD):
                            te.matmul(m.P[1][64 * u + 32 * b:64 * u + 32 * b + 32, 0:SLOT], wr[:, k, :],
                                      m.xTt[:, k, SLOT * b:SLOT * b + SLOT], start=k == 0, stop=k == KD - 1)
                    for b in range(2):
                        for k in range(KD):
                            for j in range(2):
                                mm = te.matmul(m.P[1][SLOT * j:SLOT * j + SLOT, 128 + 128 * b:256 + 128 * b],
                                               m.xTt[:, k, SLOT * b:SLOT * b + SLOT],
                                               wv[:, k, :], start=k == 0, stop=k == KD - 1)
                    mm.then_inc(rv_ready, 1)
                elif phase == 1:
                    te.wait_ge(roped, t + 1)
                    for j in range(2):
                        mm = te.transpose(m.W[0][:, 128 * j:128 * j + 128], m.qkr[:, 128 * j:128 * j + 128], ident)
                    mm.then_inc(qT_ready, 1)
                    te.wait_ge(er_ready, t + 1)
                    te.wait_ge(vbd_ready, t * 2 + 2)
                    te.transpose(m.W[1][:, 0:128], m.qkr[:, 256:384], ident).then_inc(kT_ready, 1)
                elif phase == 2:
                    te.wait_ge(qT_copied, t + 1)
                    te.wait_ge(kbd_ready, t * 2 + 2)
                    te.wait_ge(drop_ready, r + 1)
                    for j in range(2):
                        for b in range(2):
                            o = m.W[j][SLOT * b:SLOT * b + SLOT, 0:NKV * SEQ]
                            te.matmul(o, m.qT[:, j, SLOT * b:SLOT * b + SLOT], m.kbd[:, b, :], start=True, stop=False)
                            rows_b = slice(64 * u + 32 * b, 64 * u + 32 * b + 32)
                            mm = te.matmul(o, ones_b[rows_b, :],
                                           drop[rows_b, NKV * j:NKV * j + NKV, :],
                                           start=False, stop=True)
                        mm.then_inc(s1_ready, 1)
                elif phase == 3:
                    te.wait_ge(s1_sub, t * 2 + 2)
                    te.wait_ge(p1_norm, t + 1)
                    for g in range(NKV):
                        mm = te.transpose(m.W[g // 4][:, 128 * (g % 4):128 * (g % 4) + 128],
                                          m.pe[:, 128 * g:128 * g + 128], ident)
                        if g % 4 == 3:
                            mm.then_inc(pT_ready, 1)
                elif phase == 4:
                    te.wait_ge(pTa_copied, t + 1)
                    te.wait_ge(pTb_copied, t + 1)
                    for g in range(NKV):
                        for b in range(2):
                            c = 128 * (g // 4) + SLOT * b
                            mm = te.matmul(m.W[0][32 * (g % 4):32 * (g % 4) + 32, c:c + SLOT], m.vbd[:, b, g, :],
                                           m.pT[:, g, SLOT * b:SLOT * b + SLOT], start=True, stop=True)
                    mm.then_inc(oT_ready, 1)
                elif phase == 5:
                    te.wait_ge(oT_copied, t * 2 + 2)
                    for k in range(KD):
                        mm = te.matmul(m.W[1][:, 0:D], m.oT[:, k, :], wo[:, k, :], start=k == 0, stop=k == KD - 1)
                    mm.then_inc(o1_ready, 1)
                elif phase == 6:
                    te.wait_ge(x1_ready, t * 2 + 2)
                    for j in range(KD):
                        mm = te.transpose(m.W[0][:, 128 * j:128 * j + 128], m.y1[:, 128 * j:128 * j + 128], ident)
                    mm.then_inc(x1T_ready, 1)
                elif phase == 7:
                    te.wait_ge(x1T_copied, t + 1)
                    for q in range(4):
                        for k in range(KD):
                            mm = te.matmul(m.W[1][:, 128 * q:128 * q + 128], wq2[:, k, 128 * q:128 * q + 128],
                                           m.x1T[:, k, :], start=k == 0, stop=k == KD - 1)
                    mm.then_inc(q2_ready, 1)
                elif phase == 8:
                    te.wait_ge(q2_copied, t * 4 + 4)

            te.wait_ge(wself_in, 96)
            te.wait_ge(const_in, 64)
            def pair(r, more):
                for phase in (1, 2):
                    for u in range(2):
                        stage1(r, u, phase)
                if more:
                    for u in range(2):
                        stage1(r + 1, u, 0)
                for phase in range(3, 9):
                    for u in range(2):
                        stage1(r, u, phase)

            for u in range(2):
                stage1(0, u, 0)
            with te.Fori(0, TILES // 2 - 1) as r:
                pair(r, True)
            pair(TILES // 2 - 1, False)

            three = ((0, 0), (0, 1), (1, 0))
            cparts = (chi, clo)

            def kv_piece(m, k, prev=False):
                c, r = k // TPC, k % TPC
                first = isinstance(m, int) and m == 0 and c == 0
                if r == 0:
                    te.wait_ge(chi_ready, m * NCH + (c + 1))
                    te.wait_ge(clo_ready, m * NCH + (c + 1))
                if r < 2:
                    if not first:
                        te.wait_ge(v_ready, m * NT + (TPC * c + r - 1))
                    n = 0
                    for wi, ci in three:
                        w = (wk_hi, wk_lo)[wi]
                        for kk in range(KD):
                            mm = te.matmul(W[r][:, 0:CH], w[:, kk, 128 * r:128 * r + 128],
                                           cparts[ci][:, c, kk, :], start=n == 0, stop=n == 5)
                            n += 1
                    mm.then_inc(w_ready[r], 1)
                else:
                    for bank in range(2):
                        i = 2 * (r - 2) + bank
                        if r == 2:
                            te.wait_ge(k_ready, m * (2 * NCH) + (2 * c + bank + 1))
                        else:
                            te.wait_ge(v_ready, m * NT + (TPC * c + bank + 1))
                        if r == 3 and c == 0 and bank == 0 and prev:
                            te.wait_ge(den_read, m - 1)
                        n = 0
                        for wi, ci in three:
                            w = (wv_hi, wv_lo)[wi]
                            for kk in range(KD):
                                mm = te.matmul(W[bank][0:CT, 0:D], cparts[ci][:, c, kk, CT * i:CT * i + CT],
                                               w[:, kk, :], start=n == 0, stop=n == 5)
                                n += 1
                        mm.then_inc(w_ready[bank], 1)

            def scores(n, par, i, prev):
                if i == 0:
                    te.wait_ge(qbd_ready, n * 2 + 2)
                if i % TPC == 0:
                    te.wait_ge(k_ready, n * (2 * NCH) + 2 * (i // TPC + 1))
                if i >= 2 or prev:
                    te.wait_ge(p2_exp, n * NT + (i - 1))
                for q in range(4):
                    for part in range(2):
                        mm = te.matmul(SC[0:CT, i % 2, q // 2, QUAD * (q % 2):QUAD * (q % 2) + QUAD],
                                       kst[par][:, q, CT * i:CT * i + CT], qbd[par][part][:, q, :, :],
                                       start=part == 0, stop=part == 1)
                mm.then_inc(s2_ready, 1)

            def weigh(n, par, i, prev=False):
                te.wait_ge(p2_clip, n * NT + (i + 1))
                te.wait_ge(v_ready, n * NT + (i + 1))
                if i == 0 and prev:
                    te.wait_ge(acc_read, n)
                for q in range(4):
                    mm = te.matmul(ACC[64 * (q % 2):64 * (q % 2) + 64, q // 2, 0:QUAD],
                                   v2[par][0:CT, i, 64 * q:64 * q + 64],
                                   p2[i % 3][:, QUAD * q:QUAD * q + QUAD],
                                   start=i == 0, stop=i == NT - 1)
                mm.then_inc(pv_done, 1)

            def denominators(n, project):
                te.wait_ge(p2_added, n * (NT - 1) + (NT - 1))
                if project:
                    te.wait_ge(v_ready, n * NT + (2 * NT + 1))
                for q in range(4):
                    mm = te.matmul(W0[64 * (q % 2):64 * (q % 2) + 64, QUAD * (q // 2):QUAD * (q // 2) + QUAD],
                                   ones[0:CT, :], psum2[:, QUAD * q:QUAD * q + QUAD], start=True, stop=True)
                mm.then_inc(den_ready, 1)

            def step(n, par, i, project, prev):
                scores(n, par, i, prev)
                if project:
                    kv_piece(n + 1, i, prev)
                if i >= 2:
                    weigh(n, par, i - 2, prev)
                elif prev:
                    weigh(n - 1, 1 - par, NT - 2 + i)
                if i == 2 and prev:
                    denominators(n - 1, project)

            def batch(n, par, project, project_next):
                for i in range(LAG, NT):
                    step(n, par, i, project, True)
                for i in range(LAG):
                    step(n + 1, 1 - par, i, project_next, True)

            for k in range(NT):
                kv_piece(0, k)
            for i in range(LAG):
                step(0, 0, i, True, False)
            with te.Fori(0, TILES - 1) as t:
                batch(t * 2, 0, True, True)
                batch(t * 2 + 1, 1, True, True)
            batch(B - 2, 0, True, False)
            for i in range(LAG, NT):
                step(B - 1, 1, i, False, True)
            weigh(B - 1, 1, NT - 2)
            weigh(B - 1, 1, NT - 1)
            denominators(B - 1, False)

            te.wait_ge(o2_ready, B)
            te.wait_ge(wq_done, 2)
            def up(g, i):
                te.wait_ge(xqT_copied, g * 2 + (i // 2 + 1))
                if i >= 2:
                    te.wait_ge(h_ready, g * G3 + (i - 1))
                for j in range(2):
                    for k in range(KD):
                        mm = te.matmul(SC[:, i % 2, j, :], xqT[:, i, k, :], wup[:, k, 512 * j:512 * j + 512],
                                       start=k == 0, stop=k == KD - 1)
                mm.then_inc(up_ready, 1)

            def turn(g, i):
                te.wait_ge(h_ready, g * G3 + (i + 1))
                for hh in range(2):
                    if i >= 1:
                        te.wait_ge(hTlo_ready, g * (2 * G3) + (2 * i + hh - 1))
                    for k in range(4):
                        mm = te.transpose(ACC[:, hh, 128 * k:128 * k + 128],
                                          th[i][:, 512 * hh + 128 * k:512 * hh + 128 * k + 128], ident)
                    mm.then_inc(hT_ready, 1)

            def down(g, i):
                if i >= 2:
                    te.wait_ge(dn_read, g * G3 + (i - 1))
                for part, ready in ((0, hThi_ready), (1, hTlo_ready)):
                    for hh in range(2):
                        te.wait_ge(ready, g * (2 * G3) + (2 * i + hh + 1))
                        for k in range(4 * hh, 4 * hh + 4):
                            mm = te.matmul(W[i % 2][:, 0:D], hT[i % 2][part][:, k, :],
                                           wdn[:, k, :], start=part == 0 and k == 0, stop=part == 1 and k == 7)
                mm.then_inc(dn_ready, 1)

            with te.Fori(0, GROUPS) as g:
                te.wait_ge(o3_biased, g * 2 + 2)
                for i in range(G3):
                    for k in range(KD):
                        mm = te.matmul(SC[:, 0, i // 2, D * (i % 2):D * (i % 2) + D],
                                       oTb[:, k, 128 * i:128 * i + 128], wo2[:, k, :],
                                       start=k == 0, stop=k == KD - 1)
                mm.then_inc(d3_ready, 1)
                for pair in range(2):
                    te.wait_ge(xq_ready, g * 2 + (pair + 1))
                    for i in (2 * pair, 2 * pair + 1):
                        for k in range(KD):
                            o = 128 * (KD * (i % 2) + k)
                            mm = te.transpose(Wb[pair][:, o:o + 128], xq[:, i, 128 * k:128 * k + 128], ident_b[:, :])
                    mm.then_inc(xqT_ready, 1)
                for i in range(G3 + 2):
                    if i < G3:
                        up(g, i)
                    if 1 <= i <= G3:
                        turn(g, i - 1)
                    if i >= 2:
                        down(g, i - 2)

        @block.scalar
        def _(se):
            def stage1(r, u, phase):
                t, m = r * 2 + u, T1[u]
                if phase == 0:
                    se.wait_ge(rv_ready, t + 1)
                    half_u = slice(64 * u, 64 * u + 64)
                    se.activation(er[half_u, :], m.P[1][half_u, 0:SLOT], ACT.Exp, bias=nbr[half_u, :], scale=-1.0)\
                      .then_inc(er_ready, 1)
                elif phase == 1:
                    se.wait_ge(qT_ready, t + 1)
                    se.copy(m.qT.rearrange("p j n -> p (j n)"), m.W[0][:, 0:256]).then_inc(qT_copied, 1)
                elif phase == 2:
                    se.wait_ge(s1_sub, t * 2 + 2)
                    se.activation(m.pe3, m.pe3, ACT.Exp, scale=SCALE).then_inc(p1_exp, 1)
                elif phase == 3:
                    se.wait_ge(pT_ready, t * 2 + 2)
                    se.copy(m.pT[:, 0:4, :].rearrange("p g n -> p (g n)"), m.W[0][:, :]).then_inc(pTa_copied, 1)
                elif phase == 4:
                    se.wait_ge(oT_ready, t + 1)
                    for j in range(2):
                        se.activation(m.oT[:, j, :], m.W[0][:, 128 * j:128 * j + 128], ACT.Identity,
                                      bias=cc[:, C_BV1 + j:C_BV1 + j + 1]).then_inc(oT_copied, 1)
                elif phase == 5:
                    se.wait_ge(x1T_ready, t + 1)
                    se.copy(m.x1T.rearrange("p j n -> p (j n)"), m.W[0][:, 0:256]).then_inc(x1T_copied, 1)
                elif phase == 6:
                    se.wait_ge(q2_ready, t + 1)
                    for q in range(4):
                        se.activation(q2_all[:, bass.ds(t, 1), q, :].rearrange("p o n -> p (o n)"),
                                      m.W[1][:, 128 * q:128 * q + 128], ACT.Identity,
                                      bias=cc[:, C_BQ2 + q:C_BQ2 + q + 1]).then_inc(q2_copied, 1)

            se.wait_ge(set_cols, 2)
            def pair(r, more):
                for phase in (1, 2):
                    for u in range(2):
                        stage1(r, u, phase)
                if more:
                    for u in range(2):
                        stage1(r + 1, u, 0)
                for phase in range(3, 7):
                    for u in range(2):
                        stage1(r, u, phase)

            for u in range(2):
                stage1(0, u, 0)
            with se.Fori(0, TILES // 2 - 1) as r:
                pair(r, True)
            pair(TILES // 2 - 1, False)

            def evacuate(m, par, k, item0, item1):
                c, r = k // TPC, k % TPC
                if r < 2:
                    bank, item = ((0, item0 + (3 * c + 1)), (1, item1 + (3 * c + 1)))[r]
                    se.wait_ge(w_ready[bank], item)
                    for h in range(2):
                        se.activation(kst[par][64 * h:64 * h + 64, 2 * r + h, CH * c:CH * c + CH],
                                      W[bank][64 * h:64 * h + 64, 0:CH], ACT.Identity,
                                      bias=cc[64 * h:64 * h + 64, C_BK2 + r:C_BK2 + r + 1])\
                          .then_inc(khi_ready, 1)
                else:
                    for bank, item in ((0, item0), (1, item1)):
                        se.wait_ge(w_ready[bank], item + (3 * c + r))
                        se.copy(v2[par][0:CT, TPC * c + 2 * (r - 2) + bank, :], W[bank][0:CT, 0:D])\
                          .then_inc(v_ready, 1)

            def step(n, par, i, project, prev):
                se.wait_ge(s2_ready, n * NT + (i + 1))
                if i >= 3:
                    se.wait_ge(pv_done, n * NT + (i - 2))
                    se.wait_ge(p2_added, n * (NT - 1) + max(i - 3, 1))
                elif prev:
                    se.wait_ge(pv_done, n * NT + (i - 2))
                    se.wait_ge(p2_added, n * (NT - 1) + (i - 2))
                col = n * NT + i
                se.activation(p2[i % 3].rearrange("p (a n) -> p a n", a=2),
                              SC[0:CT, i % 2, :, 0:HQ], ACT.Exp,
                              bias=mbias[:, bass.ds(col, 1)], scale=mscale[:, bass.ds(col, 1)])\
                  .then_inc(p2_exp, 1)
                if project:
                    evacuate(n + 1, 1 - par, i, n * 9 + 9, n * 9 + 9)

            def batch(n, par, project, project_next):
                for i in range(LAG, NT):
                    step(n, par, i, project, True)
                for i in range(LAG):
                    step(n + 1, 1 - par, i, project_next, True)

            se.wait_ge(set_mask, 2)
            for k in range(NT):
                evacuate(0, 0, k, 0, 0)
            for i in range(LAG):
                step(0, 0, i, True, False)
            with se.Fori(0, TILES - 1) as t:
                batch(t * 2, 0, True, True)
                batch(t * 2 + 1, 1, True, True)
            batch(B - 2, 0, True, False)
            for i in range(LAG, NT):
                step(B - 1, 1, i, False, True)

            se.wait_ge(o2_ready, B)
            with se.Fori(0, GROUPS) as g:
                for j in range(KD):
                    se.activation(oTb[:, j, :].rearrange("p (t n) -> p t n", t=G3),
                                  oT_all[:, j, bass.ds(g * G3, G3), :], ACT.Identity,
                                  bias=cc[:, C_BV2 + j:C_BV2 + j + 1]).then_inc(o3_biased, 1)
                for pair in range(2):
                    se.wait_ge(xqT_ready, g * 2 + (pair + 1))
                    se.copy(xqT[:, 2 * pair:2 * pair + 2, :, :].rearrange("p i j n -> p (i j n)"),
                            Wb[pair][:, 0:512]).then_inc(xqT_copied, 1)
                for i in range(G3 + 1):
                    if i < G3:
                        se.wait_ge(up_ready, g * G3 + (i + 1))
                        se.activation(th[i].rearrange("p (a n) -> p a n", a=2), SC[:, i % 2, :, :], ACT.Tanh,
                                      scale=s5[:, i:i + 1]).then_inc(z_ready, 1)
                    if i >= 1:
                        if i >= 3:
                            se.wait_ge(dn_ready, g * G3 + (i - 2))
                        for hh in range(2):
                            se.wait_ge(hT_ready, g * (2 * G3) + (2 * (i - 1) + hh + 1))
                            se.copy(hT[(i - 1) % 2][0][:, 4 * hh:4 * hh + 4, :].rearrange("p k n -> p (k n)"),
                                    ACC[:, hh, :]).then_inc(hThi_ready, 1)

        @block.gpsimd
        def _(ge):
            ge.memset(ones[:, :], 1.0).then_inc(set_ones, 1)
            ge.memset(ones_b[:, :], 1.0).then_inc(set_ones, 1)
            ge.memset(half[:, :], -0.5).then_inc(set_ones, 1)
            ge.wait_ge(set_ones, 3)
            def dropped(r):
                ge.wait_ge(negm_ready, r + 1)
                ge.tensor_tensor(drop, spread(negm[:, :], 1, NH), spread(dh, 2, SEQ), ALU.mult)\
                  .then_inc(drop_ready, 1)

            def root(r):
                for u in range(2):
                    ge.wait_ge(y1_veps, r * 2 + (u + 1))
                    ge.tensor_tensor(T1[u].rstd, T1[u].veps, half[:, 0:1], ALU.pow).then_inc(y1_rstd, 1)

            dropped(0)
            with ge.Fori(0, TILES // 2 - 1) as r:
                root(r)
                dropped(r + 1)
            root(TILES // 2 - 1)

            def split_low(m, par, c):
                ge.wait_ge(chi_ready, m * NCH + (c + 1))
                ge.tensor_tensor(clo[:, c, :, :], craw[:, (par * NCH + c) % 2, :, :], chi[:, c, :, :].bitcast(F32), ALU.subtract)\
                  .then_inc(clo_ready, 1)

            def attend(n, par, prep0=True, prep1=True):
                for i in range(NT):
                    if i == 0 and prep0:
                        split_low(n + 1, 1 - par, 2)
                    if i == 4 and prep1:
                        split_low(n + 2, par, 0)
                    if i == 8 and prep1:
                        split_low(n + 2, par, 1)
                    if i >= 1:
                        ge.wait_ge(p2_clip, n * NT + (i + 1))
                        if i == 1:
                            ge.wait_ge(den_ready, n + 1)
                        if i >= 2:
                            ge.wait_ge(p2_added, n * (NT - 1) + (i - 1))
                        first = p2[0] if i == 1 else psum2
                        ge.tensor_tensor(psum2, first, p2[i % 3], ALU.add)\
                          .then_inc(p2_added, 1)

            for c in range(NCH):
                split_low(0, 0, c)
            split_low(1, 1, 0)
            split_low(1, 1, 1)
            with ge.Fori(0, TILES - 1) as t:
                attend(t * 2, 0)
                attend(t * 2 + 1, 1)
            attend(B - 2, 0, prep1=False)
            attend(B - 1, 1, prep0=False, prep1=False)

            with ge.Fori(0, GROUPS) as g:
                for s in range(4):
                    ge.wait_ge(v3_ready, g * 4 + (s + 1))
                    ge.tensor_tensor(rstd3, eps3, half[:, :], ALU.pow).then_inc(pow_done, 1)

        @block.vector
        def _(ve):
            ve.wait_ge(const_in, 64)
            ve.tensor_copy(ident_b[:, :], ident)
            ve.memset(mark[:, :], 0.0)
            ve.tensor_scalar(nbr[:, :], cc[:, C_BR:C_BR + 1], -1.0, None, ALU.mult).then_inc(set_cols, 1)
            ve.tensor_scalar(rs[:, :], cc[:, C_RS:C_RS + 1], 0.0, 0.3, ALU.max, ALU.min).then_inc(set_cols, 1)
            ve.tensor_scalar(mbias[:, :], mski, 0.5, None, ALU.is_gt).then_inc(set_mask, 1)
            ve.wait_ge(set_mask, 1)
            ve.tensor_scalar(mscale[:, :], mbias[:, :], SCALE, None, ALU.mult)
            ve.tensor_scalar(mbias[:, :], mbias[:, :], CLIP, -CLIP, ALU.mult, ALU.add).then_inc(set_mask, 1)

            for hi, lo, r, arrived in ((wk_hi, wk_lo, wk_raw, wk_in), (wv_hi, wv_lo, wv_raw, wv_in)):
                ve.wait_ge(arrived, 16)
                r = r.rearrange("p (k n) -> p k n", k=KD)
                ve.tensor_copy(hi[:, :, :], r).then_inc(wkv_split, 1)
                ve.wait_ge(wkv_split, 1 if r is None else (1 if hi is wk_hi else 3))
                ve.tensor_tensor(lo[:, :, :], r, hi[:, :, :].bitcast(F32), ALU.subtract).then_inc(wkv_split, 1)

            for i, (r, arrived) in enumerate(((up_raw, wup_in), (down_raw, wdn_in))):
                ve.wait_ge(arrived, 16)
                ve.tensor_reduce(wsum[:, i:i + 1], r, AX.X, ALU.add, apply_absolute_value=True)\
                  .then_inc(wq_abs, 1)
            ve.wait_ge(wq_sum, 1)
            ve.tensor_scalar(wscale[:, :], W0[:, 0:2], 1.0 / (D * HID), 1e-8, ALU.mult, ALU.max)\
              .then_inc(wq_mean, 1)
            ve.wait_ge(wq_mean, 1)
            ve.reciprocal(winv[:, :], wscale[:, :]).then_inc(wq_inv, 1)
            ve.tensor_scalar(sgam[:, :], rc[:, R_FG:R_FG + D], wscale[:, 1:2], None, ALU.mult)
            ve.wait_ge(wq_inv, 1)
            for i, (r, o) in enumerate(((up_raw, wup), (down_raw, wdn))):
                ve.tensor_scalar(r, r, winv[:, i:i + 1], MAGIC, ALU.mult, ALU.add).then_inc(wq_scaled, 1)
                ve.wait_ge(wq_scaled, i + 1)
                ve.tensor_scalar(r, r, -MAGIC, 1.0, ALU.add, ALU.min).then_inc(wq_round, 1)
                ve.wait_ge(wq_round, i + 1)
                ve.tensor_scalar(o[:, :, :].rearrange("p k n -> p (k n)"), r, -1.0, None, ALU.max)\
                  .then_inc(wq_done, 1)

            def wait_apart(semaphore, value):
                ve.wait_ge(semaphore, value)
                ve.tensor_copy(mark[:, 1:2], mark[:, 0:1])

            def stage1(r, u, phase):
                t, m = r * 2 + u, T1[u]
                if phase == 0:
                    ve.wait_ge(qk_ready, t + 1)
                    ve.tensor_tensor(m.qk, m.P[0][:, 0:384], rc[:, R_BQK:R_BQK + 384], ALU.add).then_inc(qk_biased, 1)
                    ve.wait_ge(qk_biased, t + 1)
                    heads = "p (h d) -> p h d"
                    q3, c3, r3 = (a.rearrange(heads, d=HD) for a in (m.qk, m.rcos, m.qkr))
                    cos = kc[:, K_COS:K_COS + HD]
                    ve.tensor_tensor(c3, q3, spread(cos, 1, 24), ALU.mult).then_inc(rope_cos, 1)
                    for h in range(2):
                        o, i = (slice(0, 8), slice(8, 16))[::1 - 2 * h]
                        ve.tensor_tensor(r3[:, :, o], q3[:, :, i],
                                         spread(kc[:, K_SIN + o.start:K_SIN + o.stop], 1, 24), ALU.mult)\
                          .then_inc(rope_sin, 1)
                    ve.wait_ge(rope_cos, t + 1)
                    ve.wait_ge(rope_sin, t * 2 + 2)
                    ve.tensor_tensor(m.qkr, m.qkr, m.rcos, ALU.add).then_inc(roped, 1)
                elif phase == 1:
                    ve.wait_ge(er_ready, t + 1)
                    for b in range(2):
                        ve.tensor_tensor(
                            m.vbd[:, b, :, :].rearrange("p g (j d) -> p g j d", j=2),
                            spread(m.P[1][:, 128 + 128 * b:256 + 128 * b].rearrange(
                                "p (g d) -> p g d", d=HD), 2, 2),
                            spread(spread(dj, 2, HD), 1, NKV), ALU.mult).then_inc(vbd_ready, 1)
                elif phase == 2:
                    ve.wait_ge(x_in[u], r * 16 + 16)
                    ve.tensor_tensor(m.xb, m.xt, rc[:, R_BO1:R_BO1 + D], ALU.add).then_inc(xb_ready, 1)
                    ve.wait_ge(kT_ready, t + 1)
                    for b in range(2):
                        ve.tensor_tensor(m.kbd[:, b, :].rearrange("p (g k) -> p g k", g=NKV),
                                         spread(m.W[1][:, SLOT * b:SLOT * b + SEQ], 1, NKV),
                                         spread(d8, 2, SEQ), ALU.mult).then_inc(kbd_ready, 1)
                elif phase == 3:
                    for j in range(2):
                        ve.wait_ge(s1_ready, t * 2 + (j + 1))
                        s3 = m.W[j][:, 0:NKV * SEQ].rearrange("p (g k) -> p g k", g=NKV)
                        ve.tensor_reduce(m.st_max[:, 8 * j:8 * j + 8], s3, AX.X, ALU.max).then_inc(s1_max, 1)
                        ve.wait_ge(s1_max, t * 2 + (j + 1))
                        ve.tensor_tensor(m.pe4[:, :, j, :], s3, spread(m.st_max[:, 8 * j:8 * j + 8], 2, SEQ),
                                         ALU.subtract).then_inc(s1_sub, 1)
                elif phase == 4:
                    ve.wait_ge(p1_exp, t + 1)
                    ve.tensor_reduce(m.st_sum, m.pe3, AX.X, ALU.add).then_inc(p1_sum, 1)
                    ve.wait_ge(p1_sum, t + 1)
                    ve.reciprocal(m.st_rec, m.st_sum).then_inc(p1_rec, 1)
                    ve.wait_ge(p1_rec, t + 1)
                    ve.tensor_tensor(m.pe3, m.pe3, spread(m.st_rec, 2, SEQ), ALU.mult).then_inc(p1_norm, 1)
                elif phase == 5:
                    ve.wait_ge(pT_ready, t * 2 + 2)
                    ve.tensor_copy(m.pT[:, 4:8, :].rearrange("p g n -> p (g n)"), m.W[1][:, :])\
                      .then_inc(pTb_copied, 1)
                elif phase == 6:
                    ve.wait_ge(o1_ready, t + 1)
                    ve.tensor_tensor(m.y1, m.W[1][:, 0:D], m.xb, ALU.add).then_inc(y1_ready, 1)
                    ve.wait_ge(y1_ready, t + 1)
                    ve.bn_stats(m.stats, m.y1).then_inc(y1_stats, 1)
                    wait_apart(y1_stats, t + 1)
                    ve.bn_aggr(m.aggr, m.stats).then_inc(y1_aggr, 1)
                    ve.wait_ge(y1_aggr, t + 1)
                    ve.tensor_scalar(m.veps, m.aggr[:, 1:2], 1e-5, None, ALU.add).then_inc(y1_veps, 1)
                elif phase == 7:
                    ve.wait_ge(y1_rstd, t + 1)
                    ve.tensor_scalar(m.y1, m.y1, m.aggr[:, 0:1], m.rstd, ALU.subtract, ALU.mult).then_inc(x1_ready, 1)
                    ve.wait_ge(x1_ready, t * 2 + 1)
                    ve.tensor_copy(x1_all[:, bass.ds(t, 1), :].rearrange("p o n -> p (o n)"), m.y1)\
                      .then_inc(x1_ready, 1)

            def route(r):
                ve.wait_ge(er_ready, r * 2 + 2)
                ve.tensor_scalar(er, er, 1.0, None, ALU.add).then_inc(sig_plus, 1)
                ve.wait_ge(sig_plus, r + 1)
                ve.reciprocal(sg[0][:, 0:SEQ], er[:, 0:SEQ]).then_inc(sig_ready, 1)
                wait_apart(sig_ready, r + 1)
                cur = 0
                for k in range(4):
                    nxt = 1 + k % 2
                    ve.max(m8, sg[cur]).then_inc(top8, 1)
                    wait_apart(top8, r * 4 + (k + 1))
                    ve.match_replace(sg[nxt], m8, sg[cur], -1.0).then_inc(top8_out, 1)
                    wait_apart(top8_out, r * 4 + (k + 1))
                    cur = nxt
                ve.tensor_scalar(negm[:, :], sg[cur][:, 0:SEQ], 0.0, NEG, ALU.is_ge, ALU.mult)\
                  .then_inc(negm_ready, 1)

            ve.wait_ge(wq_done, 2)
            for m in T1:
                ve.memset(m.pe, 0.0)
            ve.memset(sg[0][:, SEQ:SEQ + 4], 2.0)

            def pair(r, more):
                for phase in range(2, 6):
                    for u in range(2):
                        stage1(r, u, phase)
                if more:
                    for u in range(2):
                        stage1(r + 1, u, 0)
                for phase in (6, 7):
                    for u in range(2):
                        stage1(r, u, phase)
                if more:
                    for u in range(2):
                        stage1(r + 1, u, 1)
                    route(r + 1)

            for phase in range(2):
                for u in range(2):
                    stage1(0, u, phase)
            route(0)
            with ve.Fori(0, TILES // 2 - 1) as r:
                pair(r, True)
            pair(TILES // 2 - 1, False)

            def split_high(m, par, c):
                ve.wait_ge(c_in[c], m * 16 + 16)
                ve.tensor_copy(chi[:, c, :, :], craw[:, (par * NCH + c) % 2, :, :]).then_inc(chi_ready, 1)

            def keys_low(m, par, k):
                c, r = k // TPC, k % TPC
                if r >= 2:
                    return
                ve.wait_ge(khi_ready, m * 12 + (4 * c + 2 * r + 2))
                for h in range(2):
                    here, there = slice(64 * h, 64 * h + 64), slice(64 - 64 * h, 128 - 64 * h)
                    lo = ve.scalar_tensor_tensor(
                        kst[par][there, 2 * r + h, CH * c:CH * c + CH], W[r][here, 0:CH],
                        cc[here, C_BK2 + r:C_BK2 + r + 1],
                        kst[par][here, 2 * r + h, CH * c:CH * c + CH].bitcast(F32),
                        ALU.add, ALU.subtract)
                lo.then_inc(k_ready, 1)

            def queries(n, t, b, par, step):
                src = q2_all[:, bass.ds(t, 1), :, SLOT * b:SLOT * b + SEQ].rearrange("p o q n -> p (o q) n")
                if step == 0:
                    ve.tensor_copy(qh[:, :, :], src).then_inc(qh_ready, 1)
                elif step == 1:
                    ve.wait_ge(qh_ready, n + 1)
                    ve.tensor_tensor(ql[:, :, :], src, qh[:, :, :].bitcast(F32), ALU.subtract)\
                      .then_inc(ql_ready, 1)
                else:
                    part = (qh, ql)[step - 2]
                    ve.wait_ge(ql_ready, n + 1)
                    ve.tensor_tensor(qbd[par][step - 2][:, :, :, :],
                                     spread(part[:, :, :].bitcast(F32), 2, 4),
                                     spread(spread(d4, 2, SEQ), 1, 4), ALU.mult).then_inc(qbd_ready, 1)

            h4 = "p (a h q) -> p a h q"

            def only_own(o, src):
                return ve.tensor_tensor(o.rearrange(h4, a=2, h=4), src, spread(spread(d4, 2, SEQ), 1, 2), ALU.mult)

            def fold(o, src):
                return ve.tensor_reduce(o.rearrange("p (a q) -> p a q", a=2),
                                        src.rearrange("p (a h q) -> p a q h", a=2, h=4), AX.X, ALU.add)

            def finish(n, t, b, part):
                if part == 0:
                    ve.wait_ge(pv_done, n * NT + NT)
                    only_own(accm, ACC[:, :, 0:QUAD].rearrange("p a (h q) -> p a h q", h=4)).then_inc(acc_read, 1)
                elif part == 1:
                    wait_apart(acc_read, n + 1)
                    fold(acc_own, accm).then_inc(acc_folded, 1)
                    ve.wait_ge(den_ready, n + 2)
                    only_own(denm, W0[:, 0:HQ].rearrange(h4, a=2, h=4)).then_inc(den_read, 1)
                    wait_apart(den_read, n + 1)
                    fold(den_own, denm).then_inc(den_folded, 1)
                elif part == 2:
                    ve.wait_ge(den_folded, n + 1)
                    ve.reciprocal(rec_own, den_own).then_inc(rec_ready, 1)
                else:
                    ve.wait_ge(acc_folded, n + 1)
                    ve.wait_ge(rec_ready, n + 1)
                    ve.tensor_tensor(oT_all[:, :, bass.ds(t, 1), SLOT * b:SLOT * b + SEQ].rearrange(
                                         "p a o q -> p (a o) q"),
                                     acc_own.rearrange("p (a q) -> p a q", a=2),
                                     rec_own.rearrange("p (a q) -> p a q", a=2), ALU.mult)\
                      .then_inc(o2_ready, 1)

            def step(n, t, b, i, next0, next1, prev=None):
                ve.wait_ge(p2_exp, n * NT + (i + 1))
                ve.tensor_scalar(p2[i % 3], p2[i % 3], EXP_MAX, EXP_MIN, ALU.min, ALU.max)\
                  .then_inc(p2_clip, 1)
                if i == 0 and next0:
                    split_high(n + 1, 1 - b, 2)
                if i == 4 and next1:
                    split_high(n + 2, b, 0)
                if i == 8 and next1:
                    split_high(n + 2, b, 1)
                if next0:
                    if 5 <= i < 9:
                        queries(n + 1, t if b == 0 else t + 1, 1 - b, 1 - b, i - 5)
                    keys_low(n + 1, 1 - b, i)
                if prev is not None:
                    for part in {1: (0,), 2: (1,), 3: (2, 3)}.get(i, ()):
                        finish(n - 1, *prev, part)

            def batch(n, t, b, next0, next1, next2):
                t1, b1 = (t, 1) if b == 0 else (t + 1, 0)
                for i in range(LAG, NT):
                    step(n, t, b, i, next0, next1)
                for i in range(LAG):
                    step(n + 1, t1, b1, i, next1, next2, prev=(t, b))

            for c in range(NCH):
                split_high(0, 0, c)
            for s in range(4):
                queries(0, 0, 0, 0, s)
            for k in range(NT):
                keys_low(0, 0, k)
            for c in range(2):
                ve.wait_ge(v_ready, TPC * (c + 1))
                split_high(1, 1, c)
            for i in range(LAG):
                step(0, 0, 0, i, True, True)
            with ve.Fori(0, TILES - 1) as t:
                batch(t * 2, t, 0, True, True, True)
                batch(t * 2 + 1, t, 1, True, True, True)
            batch(B - 2, TILES - 1, 0, True, False, False)
            for i in range(LAG, NT):
                step(B - 1, TILES - 1, 1, i, False, False)
            for part in range(4):
                finish(B - 1, TILES - 1, 1, part)

            K3 = 20
            ve.tensor_scalar(bo2rs, rc[:, R_BO2:R_BO2 + D], rs[:, :], None, ALU.mult).then_inc(bo2_scaled, 1)
            ve.wait_ge(bo2_scaled, 1)

            def stage3(g):
                done = [0]
                tiles = range(G3)

                def then(ins, apart=False):
                    done[0] += 1
                    ins.then_inc(d3_steps, 1)
                    (wait_apart if apart else ve.wait_ge)(d3_steps, g * K3 + done[0])

                def moments(v, s, with_stats=True):
                    if with_stats:
                        for i in tiles:
                            last = ve.bn_stats(stats3[:, i, :], v[:, i, :])
                        then(last, apart=True)
                    for i in tiles:
                        last = ve.bn_aggr(mv3[:, i, :], stats3[:, i, :])
                    then(last)
                    ve.tensor_scalar(eps3, mv3[:, :, 1], 1e-5, None, ALU.add).then_inc(v3_ready, 1)

                def row(name):
                    return rc[:, name:name + D]

                ve.tensor_tensor(xb3, x1_all[:, bass.ds(g * G3, G3), :], spread(row(R_LNB), 1, G3), ALU.add)
                ve.wait_ge(d3_ready, g + 1)
                then(ve.scalar_tensor_tensor(
                    dl, SC[:, 0, :, :].rearrange("p a (i n) -> p (a i) n", i=2), rs[:, :],
                    spread(bo2rs, 1, G3), ALU.mult, ALU.add), apart=True)
                moments(dl, 0)
                for i in tiles:
                    last = ve.scalar_tensor_tensor(dl[:, i, :], dl[:, i, :], mv3[:, i, 0:1], row(R_LNG),
                                                   ALU.subtract, ALU.mult)
                then(last)
                ve.wait_ge(pow_done, g * 4 + 1)
                for i in tiles:
                    last = ve.scalar_tensor_tensor(x2[:, i, :], dl[:, i, :], rstd3[:, i:i + 1], xb3[:, i, :],
                                                   ALU.mult, ALU.add)
                then(last, apart=True)
                moments(x2, 1)
                ve.wait_ge(pow_done, g * 4 + 2)
                for i in tiles:
                    last = ve.tensor_scalar(x2[:, i, :], x2[:, i, :], mv3[:, i, 0:1], rstd3[:, i:i + 1],
                                            ALU.subtract, ALU.mult)
                then(last, apart=True)
                for i in tiles:
                    last = ve.tensor_tensor_reduce(xn[:, i, :], x2[:, i, :], x2[:, i, :], 1.0, 0.0,
                                                   ALU.mult, ALU.add, ssq3[:, i:i + 1])
                then(last)
                ve.tensor_scalar(eps3, ssq3, 1.0 / D, 1e-6, ALU.mult, ALU.add).then_inc(v3_ready, 1)
                ve.wait_ge(pow_done, g * 4 + 3)
                for i in tiles:
                    last = ve.scalar_tensor_tensor(xn[:, i, :], x2[:, i, :], rstd3[:, i:i + 1], row(R_NW),
                                                   ALU.mult, ALU.mult)
                then(last, apart=True)
                then(ve.tensor_reduce(amax3, xn, AX.X, ALU.max, apply_absolute_value=True))
                then(ve.tensor_scalar(amax3, amax3, 1e-8, None, ALU.max))
                then(ve.reciprocal(rmax3, amax3))
                for i in tiles:
                    last = ve.tensor_scalar(xn[:, i, :], xn[:, i, :], QB, rmax3[:, i:i + 1], ALU.mult, ALU.mult)
                then(last)
                ve.tensor_scalar(s5, amax3, 0.5 / QB, wscale[:, 0:1], ALU.mult, ALU.mult)
                for pair in range(2):
                    ve.tensor_scalar(xq[:, 2 * pair:2 * pair + 2, :], xn[:, 2 * pair:2 * pair + 2, :],
                                     MAGIC, -MAGIC, ALU.add, ALU.add).then_inc(xq_ready, 1)
                for i in range(G3 + 2):
                    if i < G3:
                        ve.wait_ge(z_ready, g * G3 + (i + 1))
                        ve.scalar_tensor_tensor(th[i].rearrange("p (a n) -> p a n", a=2),
                                                th[i].rearrange("p (a n) -> p a n", a=2), 1.0,
                                                SC[:, i % 2, :, :], ALU.add, ALU.mult).then_inc(h_ready, 1)
                    if 1 <= i <= G3:
                        hi, lo = hT[(i - 1) % 2]
                        if i >= 3:
                            ve.wait_ge(dn_ready, g * G3 + (i - 2))
                        for hh in range(2):
                            ks = slice(4 * hh, 4 * hh + 4)
                            ve.wait_ge(hThi_ready, g * (2 * G3) + (2 * (i - 1) + hh + 1))
                            ve.tensor_tensor(lo[:, ks, :].rearrange("p k n -> p (k n)"), ACC[:, hh, :],
                                             hi[:, ks, :].bitcast(F32).rearrange("p k n -> p (k n)"),
                                             ALU.subtract).then_inc(hTlo_ready, 1)
                    if i >= 2:
                        j = i - 2
                        ve.wait_ge(dn_ready, g * G3 + (j + 1))
                        ve.scalar_tensor_tensor(xb3[:, j, :], W[j % 2][:, 0:D], s5[:, j:j + 1],
                                                sgam[:, :], ALU.mult, ALU.mult).then_inc(dn_read, 1)
                        ve.wait_ge(dn_read, g * G3 + (j + 1))
                        then(ve.scalar_tensor_tensor(x2[:, j, :], x2[:, j, :], 2.0, xb3[:, j, :],
                                                     ALU.mult, ALU.add), apart=True)
                        last = ve.bn_stats(stats3[:, j, :], x2[:, j, :])
                then(last, apart=True)
                moments(x2, 3, with_stats=False)
                wait_apart(pow_done, g * 4 + 4)
                for i in tiles:
                    last = ve.tensor_scalar(x1_all[:, bass.ds(g * G3 + i, 1), :].rearrange("p o n -> p (o n)"),
                                            x2[:, i, :], mv3[:, i, 0:1], rstd3[:, i:i + 1],
                                            ALU.subtract, ALU.mult)
                last.then_inc(y3_ready, 1)
                assert done[0] == K3, done[0]

            with ve.Fori(0, GROUPS) as g:
                stage3(g)


def kernel(**inputs):
    import concourse.bacc as bacc
    from concourse.bass_utils import run_bass_kernel_spmd

    a = {k: np.asarray(v) for k, v in inputs.items()}

    def padded(rows):
        o = np.zeros((B, SLOT, rows.shape[-1]), np.float32)
        o[:, :SEQ] = rows
        return o.reshape(TILES, 2 * SLOT, rows.shape[-1])

    order = np.concatenate([np.arange(HD) + HD * h for j in range(2) for h in range(j, NH, 2)])
    x = padded(a["x"])
    quads = np.concatenate([np.arange(64 * q, 64 * q + 64) for q in range(4) for _ in range(2)])
    twice = np.concatenate([np.arange(HD) + HD * (h // 2) for h in range(NH)])
    w_r = np.zeros((D, 32), np.float32)
    w_r[:, :NH] = a["L0_attn_Wr"]
    rows = np.concatenate([
        a["L0_attn_bq"][order], a["L0_attn_bk"], a["L0_attn_bo"], a["L0_xattn_bo"],
        a["L0_xattn_ln_gamma"], a["L0_xattn_ln_beta"], a["L0_ffn_norm_weight"], a["L0_ffn_gamma"]])
    cols = np.zeros((128, C_ALL), np.float32)
    cols[:, C_BV1:C_BV1 + 2] = a["L0_attn_bv"][twice].reshape(2, 128).T
    cols[:, C_BQ2:C_BQ2 + 4] = a["L0_xattn_bq"][quads].reshape(4, 128).T
    cols[:, C_BK2:C_BK2 + 2] = a["L0_xattn_bk"].reshape(2, 128).T
    cols[:, C_BV2:C_BV2 + 2] = a["L0_xattn_bv"].reshape(2, 128).T
    for b in range(4):
        cols[32 * b:32 * b + NH, C_BR] = a["L0_attn_br"]
    cols[:, C_RS] = a["L0_xattn_residual_scale"]

    p = np.arange(128)[:, None]
    consts = np.zeros((128, K_ALL), np.float32)
    consts[:, K_ID:K_ID + 128] = p == np.arange(128)
    consts[:, K_D8:K_D8 + 8] = p // HD == np.arange(8)
    consts[:, K_D4:K_D4 + 4] = (p // HD) % 4 == np.arange(4)
    consts[:, K_DJ:K_DJ + 2] = p // SLOT == np.arange(2)
    heads = np.concatenate([np.arange(j, NH, 2) for j in range(2)])
    consts[:, K_DH:K_DH + NH] = p % 32 == heads
    inv_freq = (1.0 / np.float32(1000000.0) ** (np.arange(0, HD, 2, dtype=np.float32) / HD)).astype(np.float32)
    freqs = (np.arange(SEQ, dtype=np.float32)[:, None] * inv_freq).astype(np.float32)
    for b in range(2):
        r = slice(SLOT * b, SLOT * b + SEQ)
        consts[r, K_COS:K_COS + HD] = np.tile(np.cos(freqs), 2)
        consts[r, K_SIN:K_SIN + HD] = np.concatenate([-np.sin(freqs), np.sin(freqs)], 1)

    arrays = {
        "x": x,
        "xT": x.reshape(TILES * 128, D).T,
        "ctxT": a["ctx_2048"].transpose(0, 2, 1),
        "mask": a["mask_BxS2_ik0"].reshape(B * NT, CT).T,
        "w_qk": np.concatenate([a["L0_attn_Wq"][:, order], a["L0_attn_Wk"]], 1),
        "w_v": a["L0_attn_Wv"],
        "w_r": w_r,
        "w_o": a["L0_attn_Wo"],
        "w_q2": a["L0_xattn_Wq"].T[:, quads],
        "w_k2": a["L0_xattn_Wk"].T,
        "w_v2": a["L0_xattn_Wv"].T,
        "w_o2": a["L0_xattn_Wo"].T,
        "w_up": a["L0_ffn_weight_up"].T,
        "w_down": a["L0_ffn_weight_down"].T,
        "rows": rows,
        "cols": cols,
        "consts": consts,
    }
    nc = bacc.Bacc("TRN2", target_bir_lowering=False, num_devices=1)
    feeds, args = {}, []
    for name, v in arrays.items():
        v = np.ascontiguousarray(v)
        feeds[f"in_{name}"] = v
        args.append(nc.dram_tensor(f"in_{name}", v.shape, mybir.dt.from_np(v.dtype), kind="ExternalInput").ap())
    out = nc.dram_tensor("out", (B, SEQ, D), F32, kind="ExternalOutput").ap()
    build(nc, *args, out)
    r = run_bass_kernel_spmd(nc, [feeds], core_ids=[0])
    return r.results[0]["out"]
```

```python
from contextlib import ExitStack

import numpy as np

import concourse.bass as bass
from concourse import mybir

F32 = mybir.dt.float32
F32R = mybir.dt.float32r
BF16 = mybir.dt.bfloat16
I32 = mybir.dt.int32
ALU = mybir.AluOpType
ACT = mybir.ActivationFunctionType
AX = mybir.AxisListType

B, SEQ, D = 16, 56, 256
CTX = 1500
NH, HD = 16, 16
NKV = 8
HID = 1024
TOPK = SEQ // 2
TILES = B // 2
G3 = 4
GROUPS = TILES // G3
SLOT = 64
KD = D // 128
CT = 125
NT = CTX // CT
NCH = 3
CH = CTX // NCH
TPC = NT // NCH
QUAD = 4 * SEQ
HQ = 2 * QUAD
SCALE = float(HD) ** -0.5
CLIP = 50.0
EXP_MAX = float(np.exp(np.float64(CLIP)))
EXP_MIN = float(np.exp(np.float64(-CLIP)))
NEG = -1e30
MAGIC = 1.5 * 2.0 ** 23
QB = 127.0
R_BQK, R_BO1, R_BO2, R_LNG, R_LNB, R_NW, R_FG = 0, 384, 640, 896, 1152, 1408, 1664
R_ALL = 1920
C_BV1, C_BQ2, C_BK2, C_BV2, C_BR, C_RS = 0, 2, 4, 6, 8, 9
C_ALL = 10
K_ID, K_D8, K_D4, K_DJ, K_DH, K_COS, K_SIN = 0, 128, 136, 140, 142, 158, 174
K_ALL = 190
FRONT_AT = 6
FRONT_OPS = 21
POWER_OPS = (3, 9, 12)
LATE = 3
LAG = 4


def spread(ap, axis, n):
    ap = ap.unsqueeze(axis)
    shape = list(ap.shape)
    shape[axis] = n
    return ap.to_broadcast(shape)


def build(nc, x, xT, ctxT, mask, w_qk, w_v, w_r, w_o, w_q2, w_k2, w_v2, w_o2, w_up, w_down,
          rows, cols, consts, out):
    with ExitStack() as ctx:
        def sb(name, shape, dt=F32):
            return ctx.enter_context(nc.sbuf_tensor(name, shape, dt))

        def sem(name):
            return ctx.enter_context(nc.semaphore(name))

        SC = ctx.enter_context(nc.psum_tensor("SC", [128, 2, 2, 512], F32))
        ACC = ctx.enter_context(nc.psum_tensor("ACC", [128, 2, 512], F32))
        W0 = ctx.enter_context(nc.psum_tensor("W0", [128, 512], F32))
        W1 = ctx.enter_context(nc.psum_tensor("W1", [128, 512], F32))
        W = [W0, W1]
        ALL8 = [W0, W1, ACC[:, 0, :], ACC[:, 1, :]] + [SC[:, i // 2, i % 2, :] for i in range(4)]
        Wb = [w[:, :].bitcast(BF16) for w in W]

        kc = sb("kc", [128, K_ALL])
        ident = kc[:, K_ID:K_ID + 128]
        d8 = kc[:, K_D8:K_D8 + 8]
        d4 = kc[:, K_D4:K_D4 + 4]
        dj = kc[:, K_DJ:K_DJ + 2]
        dh = kc[:, K_DH:K_DH + 16]
        rc = sb("rc", [128, R_ALL])
        cc = sb("cc", [128, C_ALL])
        ident_b = sb("ident_b", [128, 128], BF16)
        ones = sb("ones", [128, 64])
        ones_b = sb("ones_b", [128, 64], BF16)
        half = sb("half", [128, G3])
        mark = sb("mark", [1, 256])
        pbuf = sb("pbuf", [128, 4 * 2 * HQ])
        wqk, wv, wr, wo, wq2 = (
            pbuf[:, KD * o:KD * (o + n)].rearrange("p (k n) -> p k n", k=KD)
            for o, n in ((0, 384), (384, 128), (512, 32), (544, D), (800, D)))
        wo2 = sb("wo2", [128, KD, D])
        wk_hi = sb("wk_hi", [128, KD, D], F32R)
        wk_lo = sb("wk_lo", [128, KD, D], F32R)
        wv_hi = sb("wv_hi", [128, KD, D], F32R)
        wv_lo = sb("wv_lo", [128, KD, D], F32R)
        wup = sb("wup", [128, KD, HID], BF16)
        wdn = sb("wdn", [128, HID // 128, D], F32R)
        wsum = sb("wsum", [128, 2])
        wscale = sb("wscale", [128, 2])
        winv = sb("winv", [128, 2])
        sgam = sb("sgam", [128, D])
        nbr = sb("nbr", [128, 1])
        rs = sb("rs", [128, 1])
        mscale = sb("mscale", [CT, B * NT])
        mbias = sb("mbias", [CT, B * NT])

        x1_all = sb("x1_all", [128, TILES, D])
        q2_all = sb("q2_all", [128, TILES, KD, 128])
        oT_all = q2_all[:, :, :, :].rearrange("p t j n -> p j t n")

        craw = sb("craw", [128, 2, KD, CH])
        chi = sb("chi", [128, NCH, KD, CH], F32R)
        clo = sb("clo", [128, NCH, KD, CH], F32R)
        with ExitStack() as lent:
            early = lent.enter_context(nc.sbuf_tensor("early", [128, 2 * 4 * CTX], F32))
        kst = [sb(f"kst{i}", [128, 4, CTX], F32R) for i in range(2)]
        v2 = [sb(f"v2_{i}", [128, NT, D]) for i in range(2)]
        p2 = [pbuf[0:CT, 2 * HQ * i:2 * HQ * i + 2 * HQ] for i in range(3)]
        psum2 = pbuf[0:CT, 6 * HQ:8 * HQ]
        qh = sb("qh", [128, KD, SEQ], F32R)
        ql = sb("ql", [128, KD, SEQ], F32R)
        qbd = [[sb(f"qbd{i}{k}", [128, 4, 4, SEQ], F32R) for k in range(2)] for i in range(2)]

        kbd = sb("kbd", [128, 2, NKV * SEQ])
        pT = sb("pT", [128, NKV, 128])
        vbd = sb("vbd", [128, 2, NKV, 32])

        raw = [v2[i][:, :, :].rearrange("p a n -> p (a n)") for i in range(2)]
        at = [0]

        def cut(n):
            i, o = at[0] // (NT * D), at[0] % (NT * D)
            if o + n > NT * D:
                i, o = i + 1, 0
            at[0] = i * NT * D + o + n
            return raw[i][:, o:o + n]

        early_at = [0]

        def cut_early(n):
            early_at[0] += n
            assert early_at[0] <= 8 * CTX
            return early[:, early_at[0] - n:early_at[0]]

        class Tile:
            pass

        T1 = [Tile(), Tile()]
        for u, cut1 in enumerate((cut, cut_early)):
            m = T1[u]
            m.W = (W0, W1) if u == 0 else (SC[:, 0, 0, :], SC[:, 0, 1, :])
            m.P = (ACC[:, 0, :], ACC[:, 1, :]) if u == 0 else (SC[:, 1, 0, :], SC[:, 1, 1, :])
            m.xTt = cut1(KD * 128).rearrange("p (k n) -> p k n", k=KD)
            m.xt = cut1(D)
            m.xb = cut1(D)
            m.qk = cut1(384)
            m.rcos = cut1(384)
            m.qkr = cut1(384)
            m.qT = cut1(256).rearrange("p (j n) -> p j n", j=2)
            m.pe = cut1(2 * NKV * SLOT)
            m.pe4 = m.pe.rearrange("p (g j k) -> p g j k", g=NKV, j=2)[:, :, :, 0:SEQ]
            m.pe3 = m.pe.rearrange("p (h k) -> p h k", k=SLOT)[:, :, 0:SEQ]
            m.st_max = cut1(16)
            m.st_sum = cut1(16)
            m.st_rec = cut1(16)
            m.oT = cut1(256).rearrange("p (j n) -> p j n", j=2)
            m.y1 = cut1(D)
            m.stats = cut1(6)
            m.aggr = cut1(2)
            m.veps = cut1(1)
            m.rstd = cut1(1)
            m.x1T = cut1(256).rearrange("p (j n) -> p j n", j=2)
        T1[0].kbd, T1[0].pT, T1[0].vbd = kbd, pT, vbd
        T1[1].kbd = cut_early(2 * NKV * SEQ).rearrange("p (b n) -> p b n", b=2)
        T1[1].pT = cut_early(NKV * 128).rearrange("p (g n) -> p g n", g=NKV)
        T1[1].vbd = cut_early(2 * NKV * 32).rearrange("p (b g n) -> p b g n", b=2, g=NKV)
        er = cut(64)
        sg = [cut(SEQ + 4) for _ in range(3)]
        m8 = cut(8)
        negm = sb("negm", [128, SEQ], BF16)
        drop = cut_early(NH * SEQ // 2).bitcast(BF16).rearrange("p (h k) -> p h k", h=NH)
        up_raw, down_raw = (cut_early(2 * HID) for _ in range(2))
        wk_raw, wv_raw = pbuf[:, 3072:3072 + KD * D], cut(KD * D)
        at[0] = 0
        early_at[0] = 0
        wide = G3 * D
        xb3, x2 = (cut_early(wide).rearrange("p (i n) -> p i n", i=G3) for _ in range(2))
        xq = cut_early(wide // 2).bitcast(BF16).rearrange("p (i n) -> p i n", i=G3)
        xqT = cut_early(wide // 2).bitcast(BF16).rearrange("p (i j n) -> p i j n", i=G3, j=KD)
        th = [cut_early(HID) for _ in range(G3)]
        stats3 = cut(6 * G3).rearrange("p (i n) -> p i n", i=G3)
        mv3 = cut(2 * G3).rearrange("p (i n) -> p i n", i=G3)
        eps3, rstd3 = (cut(G3) for _ in range(2))
        xq_all = sb("xq_all", [128, TILES, D], BF16)
        s5_all = sb("s5_all", [128, TILES])
        oTb = sb("oTb", [128, KD, 128])
        f_small = sb("f_small", [128, 13])
        f_stats, f_mv = f_small[:, 0:6], f_small[:, 6:8]
        f_eps, f_rstd, f_ssq, f_amax, f_rmax = (f_small[:, 8 + i:9 + i] for i in range(5))
        pT_flat = pT[:, :, :].rearrange("p g n -> p (g n)")
        vbd_flat = vbd[:, :, :, :].rearrange("p b g n -> p (b g n)")
        f_dl, f_xb = pT_flat[:, 3 * 128:3 * 128 + D], pT_flat[:, 3 * 128 + D:3 * 128 + 2 * D]
        f_x2, f_xn = vbd_flat[:, 0:D], vbd_flat[:, D:2 * D]
        bo2rs = sb("bo2rs", [128, D])
        hT = [[c[:, :, :, :].rearrange("p c k n -> p (c k n)")[:, HID * i:HID * i + HID].rearrange(
            "p (k n) -> p k n", k=8) for c in (chi, clo)] for i in range(2)]
        mski = sb("mski", [CT, B * NT], I32)
        accm, denm = kbd[:, 0, :], kbd[:, 1, :]
        acc_own, den_own, rec_own = (
            pT[:, :, :].rearrange("p g n -> p (g n)")[:, 128 * i:128 * i + 2 * SEQ] for i in range(3))

        const_in = sem("const_in")
        rows_in = sem("rows_in")
        mask_in = sem("mask_in")
        wproj_in = sem("wproj_in")
        wself_in = sem("wself_in")
        wk_in = sem("wk_in")
        wv_in = sem("wv_in")
        wup_in = sem("wup_in")
        wdn_in = sem("wdn_in")
        x_in = [sem(f"x_in{u}") for u in range(2)]
        xT_in = [sem(f"xT_in{u}") for u in range(2)]
        c_in = [sem(f"c_in{c}") for c in range(NCH)]
        y_out = sem("y_out")
        set_ones = sem("set_ones")
        set_cols = sem("set_cols")
        set_mask = sem("set_mask")
        whi_ready = sem("whi_ready")
        wlo_ready = sem("wlo_ready")
        wq_abs = sem("wq_abs")
        wq_sum = sem("wq_sum")
        wq_mean = sem("wq_mean")
        wq_inv = sem("wq_inv")
        wq_scaled = sem("wq_scaled")
        wq_round = sem("wq_round")
        wq_done = sem("wq_done")
        qk_ready = sem("qk_ready")
        rv_ready = sem("rv_ready")
        qk_biased = sem("qk_biased")
        er_ready = sem("er_ready")
        vbd_ready = sem("vbd_ready")
        rope_cos = sem("rope_cos")
        rope_sin = sem("rope_sin")
        roped = sem("roped")
        qT_ready = sem("qT_ready")
        kT_ready = sem("kT_ready")
        qT_copied = sem("qT_copied")
        kbd_ready = sem("kbd_ready")
        sig_plus = sem("sig_plus")
        sig_ready = sem("sig_ready")
        top8 = sem("top8")
        top8_out = sem("top8_out")
        negm_ready = sem("negm_ready")
        drop_ready = sem("drop_ready")
        s1_ready = sem("s1_ready")
        s1_max = sem("s1_max")
        s1_sub = sem("s1_sub")
        p1_exp = sem("p1_exp")
        p1_sum = sem("p1_sum")
        p1_rec = sem("p1_rec")
        p1_norm = sem("p1_norm")
        pT_ready = sem("pT_ready")
        pTa_copied = sem("pTa_copied")
        pTb_copied = sem("pTb_copied")
        oT_ready = sem("oT_ready")
        oT_copied = sem("oT_copied")
        o1_ready = sem("o1_ready")
        xb_ready = sem("xb_ready")
        y1_ready = sem("y1_ready")
        y1_stats = sem("y1_stats")
        y1_aggr = sem("y1_aggr")
        y1_veps = sem("y1_veps")
        y1_rstd = sem("y1_rstd")
        x1_ready = sem("x1_ready")
        x1_kept = sem("x1_kept")
        x1T_ready = sem("x1T_ready")
        x1T_copied = sem("x1T_copied")
        q2_ready = sem("q2_ready")
        q2_copied = sem("q2_copied")
        chi_ready = sem("chi_ready")
        clo_ready = sem("clo_ready")
        first_ready = sem("first_ready")
        w_ready = [sem("w0_ready"), sem("w1_ready")]
        khi_ready = sem("khi_ready")
        k_ready = sem("k_ready")
        v_ready = sem("v_ready")
        qh_ready = sem("qh_ready")
        ql_ready = sem("ql_ready")
        qbd_ready = sem("qbd_ready")
        s2_ready = sem("s2_ready")
        p2_exp = sem("p2_exp")
        p2_clip = sem("p2_clip")
        p2_added = sem("p2_added")
        pv_done = sem("pv_done")
        den_ready = sem("den_ready")
        acc_read = sem("acc_read")
        acc_folded = sem("acc_folded")
        den_read = sem("den_read")
        den_folded = sem("den_folded")
        rec_ready = sem("rec_ready")
        o2_ready = sem("o2_ready")
        bo2_scaled = sem("bo2_scaled")
        o3_biased = sem("o3_biased")
        d3_ready = sem("d3_ready")
        d3_read = sem("d3_read")
        f3_steps = sem("f3_steps")
        x2_ready = sem("x2_ready")
        x2_stats = sem("x2_stats")
        x2_aggr = sem("x2_aggr")
        v3_ready = sem("v3_ready")
        pow_done = sem("pow_done")
        xq_ready = sem("xq_ready")
        xqT_ready = sem("xqT_ready")
        xqT_copied = sem("xqT_copied")
        up_ready = sem("up_ready")
        z_ready = sem("z_ready")
        h_ready = sem("h_ready")
        hT_ready = sem("hT_ready")
        hThi_ready = sem("hThi_ready")
        hTlo_ready = sem("hTlo_ready")
        dn_ready = sem("dn_ready")
        dn_read = sem("dn_read")
        y3_ready = sem("y3_ready")

        block = ctx.enter_context(nc.Block())

        @block.sync
        def _(sp):
            def rows_of(u, t):
                sp.dma_start(T1[u].xTt, xT[:, 128 * t:128 * t + 128].rearrange(
                    "(k p) n -> p k n", p=128)).then_inc(xT_in[u], 16)

            def by_k(o, w, semaphore):
                sp.dma_start(o, w.rearrange("(k p) n -> p k n", p=128)).then_inc(semaphore, 16)

            rows_of(0, 0)
            by_k(wqk, w_qk, wproj_in)
            sp.dma_start(kc[:, :], consts).then_inc(const_in, 16)
            sp.dma_start(cc[:, :], cols).then_inc(const_in, 16)
            by_k(wv, w_v, wproj_in)
            by_k(wr, w_r, wproj_in)
            rows_of(1, 1)
            sp.dma_start(rc[:, :], rows.partition_broadcast(128)).then_inc(rows_in, 16)
            for u in range(2):
                sp.dma_start(T1[u].xt, x[u, :, :]).then_inc(x_in[u], 16)
            by_k(wo, w_o, wself_in)
            by_k(wq2, w_q2, wself_in)
            by_k(wo2[:, :, :], w_o2, wself_in)
            by_k(wk_raw.rearrange("p (k n) -> p k n", k=KD), w_k2, wk_in)
            by_k(wv_raw.rearrange("p (k n) -> p k n", k=KD), w_v2, wv_in)
            sp.dma_start(mski[:, :], mask).then_inc(mask_in, 16)

            def load_context(b, c, slot):
                sp.dma_start(craw[:, slot, :, :],
                             ctxT[bass.ds(b, 1), :, c * CH:(c + 1) * CH].rearrange(
                                 "o (k p) n -> p (o k) n", p=128)).then_inc(c_in[c], 16)

            for c in range(2):
                load_context(0, c, c)
            by_k(up_raw.rearrange("p (k n) -> p k n", k=KD), w_up, wup_in)
            by_k(down_raw.rearrange("p (k n) -> p k n", k=HID // 128), w_down, wdn_in)
            with sp.Fori(1, TILES // 2) as r:
                for u in range(2):
                    sp.wait_ge(rv_ready, r * 2 + (u - 1))
                    sp.dma_start(T1[u].xTt, xT[:, bass.ds((r * 2 + u) * 128, 128)].rearrange(
                        "(k p) n -> p k n", p=128)).then_inc(xT_in[u], 16)
                for u in range(2):
                    sp.wait_ge(xb_ready, r * 2 + (u - 1))
                    sp.dma_start(T1[u].xt, x[bass.ds(r * 2 + u, 1), :, :].rearrange(
                        "o p n -> p (o n)")).then_inc(x_in[u], 16)
            def next_chunks(b, par, first=0):
                for c in range(first, NCH):
                    sp.wait_ge(clo_ready, b * NCH + (c - 1))
                    load_context(b, c, (par * NCH + c) % 2)

            next_chunks(0, 0, first=2)
            next_chunks(1, 1)
            with sp.Fori(1, TILES) as t:
                next_chunks(t * 2, 0)
                next_chunks(t * 2 + 1, 1)
            with sp.Fori(0, GROUPS) as g:
                sp.wait_ge(y3_ready, g + 1)
                for h in range(2):
                    sp.dma_start(out[bass.ds(g * (2 * G3), 2 * G3), :, :].rearrange(
                                     "(i h) p n -> h p i n", h=2)[h],
                                 x1_all[SLOT * h:SLOT * h + SEQ, bass.ds(g * G3, G3), :]).then_inc(y_out, 16)
            sp.wait_ge(y_out, 32 * GROUPS)

        @block.tensor
        def _(te):
            def stage1(r, u, phase):
                t, m = r * 2 + u, T1[u]
                if phase == 0:
                    te.wait_ge(xT_in[u], r * 16 + 16)
                    for k in range(KD):
                        mm = te.matmul(m.P[0][:, 0:384], m.xTt[:, k, :], wqk[:, k, :], start=k == 0, stop=k == KD - 1)
                    mm.then_inc(qk_ready, 1)
                    for b in range(2):
                        for k in range(KD):
                            te.matmul(m.P[1][64 * u + 32 * b:64 * u + 32 * b + 32, 0:SLOT], wr[:, k, :],
                                      m.xTt[:, k, SLOT * b:SLOT * b + SLOT], start=k == 0, stop=k == KD - 1)
                    for b in range(2):
                        for k in range(KD):
                            for j in range(2):
                                mm = te.matmul(m.P[1][SLOT * j:SLOT * j + SLOT, 128 + 128 * b:256 + 128 * b],
                                               m.xTt[:, k, SLOT * b:SLOT * b + SLOT],
                                               wv[:, k, :], start=k == 0, stop=k == KD - 1)
                    mm.then_inc(rv_ready, 1)
                elif phase == 1:
                    te.wait_ge(roped, t + 1)
                    for j in range(2):
                        mm = te.transpose(m.W[0][:, 128 * j:128 * j + 128], m.qkr[:, 128 * j:128 * j + 128], ident)
                    mm.then_inc(qT_ready, 1)
                    te.transpose(m.W[1][:, 0:128], m.qkr[:, 256:384], ident).then_inc(kT_ready, 1)
                elif phase == 2:
                    te.wait_ge(qT_copied, t + 1)
                    te.wait_ge(kbd_ready, t * 2 + 2)
                    te.wait_ge(drop_ready, r + 1)
                    for j in range(2):
                        for b in range(2):
                            o = m.W[j][SLOT * b:SLOT * b + SLOT, 0:NKV * SEQ]
                            te.matmul(o, m.qT[:, j, SLOT * b:SLOT * b + SLOT], m.kbd[:, b, :], start=True, stop=False)
                            rows_b = slice(64 * u + 32 * b, 64 * u + 32 * b + 32)
                            mm = te.matmul(o, ones_b[rows_b, :],
                                           drop[rows_b, NKV * j:NKV * j + NKV, :],
                                           start=False, stop=True)
                        mm.then_inc(s1_ready, 1)
                elif phase == 3:
                    te.wait_ge(s1_sub, t * 2 + 2)
                    te.wait_ge(p1_norm, t + 1)
                    for g in range(NKV):
                        mm = te.transpose(m.W[g // 4][:, 128 * (g % 4):128 * (g % 4) + 128],
                                          m.pe[:, 128 * g:128 * g + 128], ident)
                        if g % 4 == 3:
                            mm.then_inc(pT_ready, 1)
                elif phase == 4:
                    te.wait_ge(vbd_ready, t * 2 + 2)
                    te.wait_ge(pTa_copied, t + 1)
                    te.wait_ge(pTb_copied, t + 1)
                    for g in range(NKV):
                        for b in range(2):
                            c = 128 * (g // 4) + SLOT * b
                            mm = te.matmul(m.W[0][32 * (g % 4):32 * (g % 4) + 32, c:c + SLOT], m.vbd[:, b, g, :],
                                           m.pT[:, g, SLOT * b:SLOT * b + SLOT], start=True, stop=True)
                    mm.then_inc(oT_ready, 1)
                elif phase == 5:
                    te.wait_ge(oT_copied, t * 2 + 2)
                    for k in range(KD):
                        mm = te.matmul(m.W[1][:, 0:D], m.oT[:, k, :], wo[:, k, :], start=k == 0, stop=k == KD - 1)
                    mm.then_inc(o1_ready, 1)
                elif phase == 6:
                    te.wait_ge(x1_ready, t + 1)
                    for j in range(KD):
                        mm = te.transpose(m.W[0][:, 128 * j:128 * j + 128], m.y1[:, 128 * j:128 * j + 128], ident)
                    mm.then_inc(x1T_ready, 1)
                elif phase == 7:
                    te.wait_ge(x1T_copied, t + 1)
                    for q in range(KD):
                        for k in range(KD):
                            mm = te.matmul(m.W[1][:, 128 * q:128 * q + 128], wq2[:, k, 128 * q:128 * q + 128],
                                           m.x1T[:, k, :], start=k == 0, stop=k == KD - 1)
                    mm.then_inc(q2_ready, 1)
                elif phase == 8:
                    te.wait_ge(q2_copied, t * KD + KD)

            te.wait_ge(wproj_in, 48)
            te.wait_ge(const_in, 32)
            te.wait_ge(set_ones, 3)

            def pair(r, more):
                for u in range(2):
                    stage1(r, u, 2)
                if more:
                    for u in range(2):
                        te.wait_ge(er_ready, r * 2 + (u + 1))
                        te.wait_ge(vbd_ready, r * 4 + (2 * u + 2))
                        stage1(r + 1, u, 0)
                for phase in range(3, 8):
                    for u in range(2):
                        stage1(r, u, phase)
                for u in range(2):
                    stage1(r, u, 8)
                    if more:
                        stage1(r + 1, u, 1)

            for phase in range(2):
                for u in range(2):
                    stage1(0, u, phase)
            te.wait_ge(wself_in, 48)
            with te.Fori(0, TILES // 2 - 1) as r:
                pair(r, True)
            pair(TILES // 2 - 1, False)

            three = ((0, 0), (0, 1), (1, 0))
            cparts = (chi, clo)

            def kv_piece(m, k, prev=False, front=None, banks=(0, 1)):
                c, r = k // TPC, k % TPC
                if r == 0 and 0 in banks:
                    te.wait_ge(chi_ready, m * NCH + (c + 1))
                    te.wait_ge(clo_ready, m * NCH + (c + 1))
                if r < 2:
                    if 0 not in banks:
                        return
                    te.wait_ge(v_ready, m * NT + (TPC * c + r - 1))
                    n = 0
                    for wi, ci in three:
                        w = (wk_hi, wk_lo)[wi]
                        for kk in range(KD):
                            mm = te.matmul(W[r][:, 0:CH], w[:, kk, 128 * r:128 * r + 128],
                                           cparts[ci][:, c, kk, :], start=n == 0, stop=n == 5)
                            n += 1
                    mm.then_inc(w_ready[r], 1)
                else:
                    for bank in banks:
                        i = 2 * (r - 2) + bank
                        if r == 2:
                            te.wait_ge(k_ready, m * (2 * NCH) + (2 * c + bank + 1))
                        else:
                            te.wait_ge(v_ready, m * NT + (TPC * c + bank + 1))
                        if r == 3 and c == 0 and bank == 0 and prev:
                            te.wait_ge(den_read, m - 1)
                        if k == 7 and bank == 0 and front is not None:
                            te.wait_ge(d3_read, front + 1)
                        n = 0
                        for wi, ci in three:
                            w = (wv_hi, wv_lo)[wi]
                            for kk in range(KD):
                                mm = te.matmul(W[bank][0:CT, 0:D], cparts[ci][:, c, kk, CT * i:CT * i + CT],
                                               w[:, kk, :], start=n == 0, stop=n == 5)
                                n += 1
                        mm.then_inc(w_ready[bank], 1)

            def scores(n, par, i, prev):
                if i == 0:
                    te.wait_ge(qbd_ready, n * 4 + 4)
                if i % TPC == 0:
                    te.wait_ge(k_ready, n * (2 * NCH) + 2 * (i // TPC + 1))
                if i >= 2 or prev:
                    te.wait_ge(p2_exp, n * NT + (i - 1))
                for q in range(4):
                    for part in range(2):
                        mm = te.matmul(SC[0:CT, i % 2, q // 2, QUAD * (q % 2):QUAD * (q % 2) + QUAD],
                                       kst[par][:, q, CT * i:CT * i + CT], qbd[par][part][:, q, :, :],
                                       start=part == 0, stop=part == 1)
                mm.then_inc(s2_ready, 1)

            def weigh(n, par, i, prev=False):
                te.wait_ge(p2_clip, n * NT + (i + 1))
                te.wait_ge(v_ready, n * NT + (i + 1))
                if i == 0 and prev:
                    te.wait_ge(acc_read, n)
                for q in range(4):
                    mm = te.matmul(ACC[64 * (q % 2):64 * (q % 2) + 64, q // 2, 0:QUAD],
                                   v2[par][0:CT, i, 64 * q:64 * q + 64],
                                   p2[i % 3][:, QUAD * q:QUAD * q + QUAD],
                                   start=i == 0, stop=i == NT - 1)
                mm.then_inc(pv_done, 1)

            def add_denominators(source, start=True, stop=True):
                for q in range(4):
                    mm = te.matmul(W0[64 * (q % 2):64 * (q % 2) + 64, QUAD * (q // 2):QUAD * (q // 2) + QUAD],
                                   ones[0:CT, :], source[:, QUAD * q:QUAD * q + QUAD],
                                   start=start and (stop or q < 2), stop=stop and (start or q >= 2))
                return mm

            def denominators(n, project):
                te.wait_ge(p2_added, n * (NT - 1) + (NT - 1))
                if project:
                    te.wait_ge(v_ready, n * NT + (2 * NT + 1))
                add_denominators(psum2).then_inc(den_ready, 1)

            def out_project(tile):
                te.wait_ge(o3_biased, tile * 2 + 2)
                for k in range(KD):
                    mm = te.matmul(W0[:, 0:D], oTb[:, k, :], wo2[:, k, :], start=k == 0, stop=k == KD - 1)
                mm.then_inc(d3_ready, 1)

            def step(n, par, i, project, prev, front=None):
                scores(n, par, i, prev)
                if project:
                    kv_piece(n + 1, i, prev, front, banks=(0,))
                if i >= 2:
                    weigh(n, par, i - 2, prev)
                elif prev:
                    weigh(n - 1, 1 - par, NT - 2 + i)
                if project:
                    kv_piece(n + 1, i, prev, front, banks=(1,))
                if i == 2 and prev:
                    denominators(n - 1, project)
                if i == 6 and front is not None:
                    te.wait_ge(v_ready, n * NT + (NT + 5))
                    out_project(front)

            def batch(n, par, project, project_next, front=None):
                for i in range(LAG, NT):
                    step(n, par, i, project, True, front)
                for i in range(LAG):
                    step(n + 1, 1 - par, i, project_next, True)

            def first_item(item):
                c, r = divmod(item, 6)
                bank = ALL8[item % 8]
                if r == 0:
                    te.wait_ge(chi_ready, c + 1)
                    te.wait_ge(clo_ready, c + 1)
                if item >= 8:
                    before_c, before_r = divmod(item - 8, 6)
                    if before_r < 2:
                        te.wait_ge(k_ready, 2 * before_c + before_r + 1)
                    else:
                        te.wait_ge(v_ready, TPC * before_c + before_r - 1)
                if item == 7:
                    te.wait_ge(wq_mean, 1)
                n = 0
                for wi, ci in three:
                    for kk in range(KD):
                        if r < 2:
                            mm = te.matmul(bank[:, 0:CH], (wk_hi, wk_lo)[wi][:, kk, 128 * r:128 * r + 128],
                                           cparts[ci][:, c, kk, :], start=n == 0, stop=n == 5)
                        else:
                            mm = te.matmul(bank[0:CT, 0:D], cparts[ci][:, c, kk, CT * (r - 2):CT * (r - 1)],
                                           (wv_hi, wv_lo)[wi][:, kk, :], start=n == 0, stop=n == 5)
                        n += 1
                mm.then_inc(first_ready, 1)

            te.wait_ge(whi_ready, 2)
            te.wait_ge(wlo_ready, 2)
            for item in range(6 * NCH):
                if item == 6:
                    te.wait_ge(wq_abs, 2)
                    te.matmul(ALL8[7][0:64, 0:2], ones[:, :], wsum[:, :], start=True, stop=True).then_inc(den_ready, 1)
                    te.matmul(ALL8[7][64:128, 0:2], ones[:, :], wsum[:, :], start=True, stop=True).then_inc(wq_sum, 1)
                first_item(item)
            te.wait_ge(k_ready, 2 * NCH)
            te.wait_ge(v_ready, NT - 2)
            for i in range(LAG):
                step(0, 0, i, True, False)
            batch(0, 0, True, True)
            batch(1, 1, True, True)
            with te.Fori(1, TILES - 1) as t:
                batch(t * 2, 0, True, True, front=t - 1)
                batch(t * 2 + 1, 1, True, True)
            batch(B - 2, 0, True, False, front=TILES - 2)
            for i in range(LAG, NT):
                step(B - 1, 1, i, False, True)
            te.wait_ge(den_read, B - 1)
            add_denominators(p2[(NT - 3) % 3], stop=False)
            weigh(B - 1, 1, NT - 2)
            add_denominators(p2[(NT - 2) % 3], start=False, stop=False)
            te.wait_ge(p2_added, B * (NT - 1) - LATE)
            add_denominators(psum2, start=False, stop=False)
            weigh(B - 1, 1, NT - 1)
            add_denominators(p2[(NT - 1) % 3], start=False).then_inc(den_ready, 1)

            def turn_rows(g, pair):
                bank = 1 - g % 2
                te.wait_ge(xq_ready, 2 * g + pair + 1)
                if g > 0:
                    te.wait_ge(dn_read, G3 * g - 1)
                if pair == 1:
                    te.wait_ge(xqT_copied, 2 * g + 1)
                for i in (2 * pair, 2 * pair + 1):
                    for k in range(KD):
                        o = 128 * (KD * (i % 2) + k)
                        mm = te.transpose(Wb[bank][:, o:o + 128], xq[:, i, 128 * k:128 * k + 128], ident_b[:, :])
                mm.then_inc(xqT_ready, 1)

            def up(g, i):
                t = G3 * g + i
                te.wait_ge(xqT_copied, 2 * g + i // 2 + 1)
                if t >= 2:
                    te.wait_ge(h_ready, t - 1)
                for j in range(2):
                    for k in range(KD):
                        mm = te.matmul(SC[:, i % 2, j, :], xqT[:, i, k, :], wup[:, k, 512 * j:512 * j + 512],
                                       start=k == 0, stop=k == KD - 1)
                mm.then_inc(up_ready, 1)

            def turn(g, i):
                t = G3 * g + i
                te.wait_ge(h_ready, t + 1)
                for hh in range(2):
                    if t >= 1:
                        te.wait_ge(hTlo_ready, 2 * t + hh - 1)
                    for k in range(4):
                        mm = te.transpose(ACC[:, hh, 128 * k:128 * k + 128],
                                          th[i][:, 512 * hh + 128 * k:512 * hh + 128 * k + 128], ident)
                    mm.then_inc(hT_ready, 1)

            def down(g, i):
                t = G3 * g + i
                if t >= 2:
                    te.wait_ge(dn_read, t - 1)
                for part, ready in ((0, hThi_ready), (1, hTlo_ready)):
                    for hh in range(2):
                        te.wait_ge(ready, 2 * t + hh + 1)
                        for k in range(4 * hh, 4 * hh + 4):
                            mm = te.matmul(W[i % 2][:, 0:D], hT[i % 2][part][:, k, :],
                                           wdn[:, k, :], start=part == 0 and k == 0, stop=part == 1 and k == 7)
                mm.then_inc(dn_ready, 1)

            te.wait_ge(wq_done, 2)
            te.wait_ge(p2_exp, B * NT)
            for g in range(GROUPS):
                turn_rows(g, 0)
                up(g, 0)
                up(g, 1)
                if g == 0:
                    out_project(TILES - 1)
                turn_rows(g, 1)
                if g == 0:
                    te.wait_ge(acc_read, B)
                turn(g, 0)
                if g == 0:
                    te.wait_ge(d3_read, TILES)
                for i in range(2, G3):
                    up(g, i)
                    turn(g, i - 1)
                    down(g, i - 2)
                turn(g, G3 - 1)
                down(g, G3 - 2)
                down(g, G3 - 1)

        @block.scalar
        def _(se):
            def stage1(r, u, phase):
                t, m = r * 2 + u, T1[u]
                if phase == 0:
                    se.wait_ge(rv_ready, t + 1)
                    half_u = slice(64 * u, 64 * u + 64)
                    se.activation(er[half_u, :], m.P[1][half_u, 0:SLOT], ACT.Exp, bias=nbr[half_u, :], scale=-1.0)\
                      .then_inc(er_ready, 1)
                elif phase == 1:
                    se.wait_ge(qT_ready, t + 1)
                    se.copy(m.qT.rearrange("p j n -> p (j n)"), m.W[0][:, 0:256]).then_inc(qT_copied, 1)
                elif phase == 2:
                    se.wait_ge(s1_sub, t * 2 + 2)
                    se.activation(m.pe3, m.pe3, ACT.Exp, scale=SCALE).then_inc(p1_exp, 1)
                elif phase == 3:
                    se.wait_ge(pT_ready, t * 2 + 2)
                    se.copy(m.pT[:, 0:4, :].rearrange("p g n -> p (g n)"), m.W[0][:, :]).then_inc(pTa_copied, 1)
                elif phase == 4:
                    se.wait_ge(oT_ready, t + 1)
                    for j in range(2):
                        se.activation(m.oT[:, j, :], m.W[0][:, 128 * j:128 * j + 128], ACT.Identity,
                                      bias=cc[:, C_BV1 + j:C_BV1 + j + 1]).then_inc(oT_copied, 1)
                elif phase == 5:
                    se.wait_ge(x1_ready, t + 1)
                    se.copy(x1_all[:, bass.ds(t, 1), :].rearrange("p o n -> p (o n)"), m.y1)\
                      .then_inc(x1_kept, 1)
                    se.wait_ge(x1T_ready, t + 1)
                    se.copy(m.x1T.rearrange("p j n -> p (j n)"), m.W[0][:, 0:256]).then_inc(x1T_copied, 1)
                elif phase == 6:
                    se.wait_ge(q2_ready, t + 1)
                    for q in range(KD):
                        se.activation(q2_all[:, bass.ds(t, 1), q, :].rearrange("p o n -> p (o n)"),
                                      m.W[1][:, 128 * q:128 * q + 128], ACT.Identity,
                                      bias=cc[:, C_BQ2 + q:C_BQ2 + q + 1]).then_inc(q2_copied, 1)

            se.wait_ge(set_cols, 2)
            def pair(r, more):
                for phase in (1, 2):
                    for u in range(2):
                        stage1(r, u, phase)
                if more:
                    for u in range(2):
                        stage1(r + 1, u, 0)
                for phase in range(3, 7):
                    for u in range(2):
                        stage1(r, u, phase)

            for u in range(2):
                stage1(0, u, 0)
            for hi, r, arrived in ((wk_hi, wk_raw, wk_in), (wv_hi, wv_raw, wv_in)):
                se.wait_ge(arrived, 16)
                se.copy(hi[:, :, :].rearrange("p k n -> p (k n)"), r).then_inc(whi_ready, 1)
            with se.Fori(0, TILES // 2 - 1) as r:
                pair(r, True)
            for i, (r, o, arrived) in enumerate(((up_raw, wup, wup_in), (down_raw, wdn, wdn_in))):
                se.wait_ge(arrived, 16)
                se.activation(o[:, :, :].rearrange("p k n -> p (k n)"), r, ACT.Abs,
                              accum_out=wsum[:, i:i + 1]).then_inc(wq_abs, 1)
            pair(TILES // 2 - 1, False)

            def evacuate_keys(par, c, r, bank):
                for h in range(2):
                    se.activation(kst[par][64 * h:64 * h + 64, 2 * r + h, CH * c:CH * c + CH],
                                  bank[64 * h:64 * h + 64, 0:CH], ACT.Identity,
                                  bias=cc[64 * h:64 * h + 64, C_BK2 + r:C_BK2 + r + 1]).then_inc(khi_ready, 1)

            def evacuate(m, par, k, uses):
                c, r = k // TPC, k % TPC
                if isinstance(m, int) and m == 1 and k == 0:
                    se.wait_ge(wq_done, 2)
                if r < 2:
                    se.wait_ge(w_ready[r], uses + (3 * c + 1))
                    evacuate_keys(par, c, r, W[r])
                else:
                    for bank in range(2):
                        se.wait_ge(w_ready[bank], uses + (3 * c + r))
                        se.copy(v2[par][0:CT, TPC * c + 2 * (r - 2) + bank, :], W[bank][0:CT, 0:D])\
                          .then_inc(v_ready, 1)

            def bias_sums(tile):
                se.wait_ge(o2_ready, tile * 2 + 2)
                for j in range(KD):
                    se.activation(oTb[:, j, :], oT_all[:, j, bass.ds(tile, 1), :].rearrange("p o n -> p (o n)"),
                                  ACT.Identity, bias=cc[:, C_BV2 + j:C_BV2 + j + 1]).then_inc(o3_biased, 1)

            def step(n, par, i, project, prev, front=None):
                se.wait_ge(s2_ready, n * NT + (i + 1))
                if i >= 3:
                    se.wait_ge(pv_done, n * NT + (i - 2))
                    se.wait_ge(p2_added, n * (NT - 1) + max(i - 3, 1))
                elif prev:
                    se.wait_ge(pv_done, n * NT + (i - 2))
                    se.wait_ge(p2_added, n * (NT - 1) + (i - 2))
                col = n * NT + i
                se.activation(p2[i % 3].rearrange("p (a n) -> p a n", a=2),
                              SC[0:CT, i % 2, :, 0:HQ], ACT.Exp,
                              bias=mbias[:, bass.ds(col, 1)], scale=mscale[:, bass.ds(col, 1)])\
                  .then_inc(p2_exp, 1)
                if project:
                    evacuate(n + 1, 1 - par, i, n * 9)
                if i == 4 and front is not None:
                    bias_sums(front)

            def batch(n, par, project, project_next, front=None):
                for i in range(LAG, NT):
                    step(n, par, i, project, True, front)
                for i in range(LAG):
                    step(n + 1, 1 - par, i, project_next, True)

            se.wait_ge(set_mask, 2)
            for item in range(6 * NCH):
                c, r = divmod(item, 6)
                se.wait_ge(first_ready, item + 1)
                if r < 2:
                    evacuate_keys(0, c, r, ALL8[item % 8])
                else:
                    se.copy(v2[0][0:CT, TPC * c + r - 2, :], ALL8[item % 8][0:CT, 0:D]).then_inc(v_ready, 1)
            for i in range(LAG):
                step(0, 0, i, True, False)
            batch(0, 0, True, True)
            batch(1, 1, True, True)
            with se.Fori(1, TILES - 1) as t:
                batch(t * 2, 0, True, True, front=t - 1)
                batch(t * 2 + 1, 1, True, True)
            batch(B - 2, 0, True, False, front=TILES - 2)
            for i in range(LAG, NT):
                step(B - 1, 1, i, False, True)

            def copy_rows(g, pair):
                se.wait_ge(xqT_ready, 2 * g + pair + 1)
                se.copy(xqT[:, 2 * pair:2 * pair + 2, :, :].rearrange("p i j n -> p (i j n)"),
                        Wb[1 - g % 2][:, 0:512]).then_inc(xqT_copied, 1)

            def gate(g, i):
                t = G3 * g + i
                se.wait_ge(up_ready, t + 1)
                se.activation(th[i].rearrange("p (a n) -> p a n", a=2), SC[:, i % 2, :, :], ACT.Tanh,
                              scale=s5_all[:, t:t + 1]).then_inc(z_ready, 1)

            def split_h(g, i):
                t = G3 * g + i
                if t >= 2:
                    se.wait_ge(dn_ready, t - 1)
                for hh in range(2):
                    se.wait_ge(hT_ready, 2 * t + hh + 1)
                    se.copy(hT[i % 2][0][:, 4 * hh:4 * hh + 4, :].rearrange("p k n -> p (k n)"),
                            ACC[:, hh, :]).then_inc(hThi_ready, 1)

            for g in range(GROUPS):
                copy_rows(g, 0)
                gate(g, 0)
                if g == 0:
                    bias_sums(TILES - 1)
                gate(g, 1)
                copy_rows(g, 1)
                for i in range(2, G3):
                    split_h(g, i - 2)
                    gate(g, i)
                split_h(g, G3 - 2)
                split_h(g, G3 - 1)

        @block.gpsimd
        def _(ge):
            ge.memset(ones[:, :], 1.0).then_inc(set_ones, 1)
            ge.memset(ones_b[:, :], 1.0).then_inc(set_ones, 1)
            ge.memset(half[:, :], -0.5).then_inc(set_ones, 1)
            ge.wait_ge(set_ones, 3)
            def dropped(r):
                ge.wait_ge(negm_ready, r + 1)
                ge.tensor_tensor(drop, spread(negm[:, :], 1, NH), spread(dh, 2, SEQ), ALU.mult)\
                  .then_inc(drop_ready, 1)

            def root(r):
                for u in range(2):
                    ge.wait_ge(y1_veps, r * 2 + (u + 1))
                    ge.tensor_tensor(T1[u].rstd, T1[u].veps, half[:, 0:1], ALU.pow).then_inc(y1_rstd, 1)

            def split_low(m, par, c):
                ge.wait_ge(chi_ready, m * NCH + (c + 1))
                ge.tensor_tensor(clo[:, c, :, :], craw[:, (par * NCH + c) % 2, :, :],
                                 chi[:, c, :, :].bitcast(F32), ALU.subtract).then_inc(clo_ready, 1)

            def rotate(r, u):
                heads = "p (h d) -> p h d"
                ge.wait_ge(qk_biased, r * 2 + (u + 1))
                ge.tensor_tensor(T1[u].rcos.rearrange(heads, d=HD), T1[u].qk.rearrange(heads, d=HD),
                                 spread(kc[:, K_COS:K_COS + HD], 1, 24), ALU.mult).then_inc(rope_cos, 1)

            def residual(r):
                for u in range(2):
                    ge.wait_ge(x_in[u], r * 16 + 16)
                    ge.tensor_tensor(T1[u].xb, T1[u].xt, rc[:, R_BO1:R_BO1 + D], ALU.add).then_inc(xb_ready, 1)

            rotate(0, 0)
            rotate(0, 1)
            ge.wait_ge(rows_in, 16)
            dropped(0)
            for i, (hi, lo, r) in enumerate(((wk_hi, wk_lo, wk_raw), (wv_hi, wv_lo, wv_raw))):
                ge.wait_ge(whi_ready, i + 1)
                ge.tensor_tensor(lo[:, :, :].rearrange("p k n -> p (k n)"), r,
                                 hi[:, :, :].rearrange("p k n -> p (k n)").bitcast(F32), ALU.subtract)\
                  .then_inc(wlo_ready, 1)
            with ge.Fori(0, TILES // 2 - 1) as r:
                residual(r)
                rotate(r + 1, 0)
                root(r)
                rotate(r + 1, 1)
                dropped(r + 1)
            residual(TILES // 2 - 1)
            split_low(0, 0, 0)
            root(TILES // 2 - 1)
            split_low(0, 0, 1)
            split_low(0, 0, 2)

            def front_power(tile, s):
                ge.wait_ge(v3_ready, tile * 3 + (s + 1))
                ge.tensor_tensor(f_rstd, f_eps, half[:, 0:1], ALU.pow).then_inc(pow_done, 1)

            def attend(n, par, prep0=True, prep1=True, front=None, tiles=NT):
                for i in range(tiles):
                    if front is not None:
                        for s, at_op in enumerate(POWER_OPS):
                            if at_op == i - FRONT_AT + NT * par:
                                front_power(front, s)
                    if i == 0 and prep0:
                        split_low(n + 1, 1 - par, 2)
                    if i == 4 and prep1:
                        split_low(n + 2, par, 0)
                    if i == 8 and prep1:
                        split_low(n + 2, par, 1)
                    if i >= 1:
                        ge.wait_ge(p2_clip, n * NT + (i + 1))
                        if i == 1:
                            ge.wait_ge(den_ready, n + 1)
                        if i >= 2:
                            ge.wait_ge(p2_added, n * (NT - 1) + (i - 1))
                        first = p2[0] if i == 1 else psum2
                        ge.tensor_tensor(psum2, first, p2[i % 3], ALU.add)\
                          .then_inc(p2_added, 1)

            split_low(1, 1, 0)
            split_low(1, 1, 1)
            attend(0, 0)
            attend(1, 1)
            with ge.Fori(1, TILES - 1) as t:
                attend(t * 2, 0, front=t - 1)
                attend(t * 2 + 1, 1, front=t - 1)
            attend(B - 2, 0, prep1=False, front=TILES - 2)
            attend(B - 1, 1, prep0=False, prep1=False, front=TILES - 2, tiles=NT - LATE)
            for s in range(3):
                front_power(TILES - 1, s)

            with ge.Fori(0, GROUPS) as g:
                ge.wait_ge(v3_ready, g + (3 * TILES + 1))
                ge.tensor_tensor(rstd3, eps3, half[:, :], ALU.pow).then_inc(pow_done, 1)

        @block.vector
        def _(ve):
            ve.wait_ge(const_in, 32)
            ve.tensor_copy(ident_b[:, :], ident)
            ve.memset(mark[:, :], 0.0)
            ve.tensor_scalar(nbr[:, :], cc[:, C_BR:C_BR + 1], -1.0, None, ALU.mult).then_inc(set_cols, 1)
            ve.tensor_scalar(rs[:, :], cc[:, C_RS:C_RS + 1], 0.0, 0.3, ALU.max, ALU.min).then_inc(set_cols, 1)

            def masks():
                ve.wait_ge(mask_in, 16)
                ve.tensor_scalar(mbias[:, :], mski[:, :], 0.5, None, ALU.is_gt).then_inc(set_mask, 1)
                ve.wait_ge(set_mask, 1)
                ve.tensor_scalar(mscale[:, :], mbias[:, :], SCALE, None, ALU.mult)
                ve.tensor_scalar(mbias[:, :], mbias[:, :], CLIP, -CLIP, ALU.mult, ALU.add).then_inc(set_mask, 1)

            def ternary(part):
                if part == 0:
                    ve.wait_ge(wq_sum, 1)
                    ve.tensor_scalar(wscale[:, :], ALL8[7][:, 0:2], 1.0 / (D * HID), 1e-8, ALU.mult, ALU.max)\
                      .then_inc(wq_mean, 1)
                    ve.wait_ge(wq_mean, 1)
                    ve.reciprocal(winv[:, :], wscale[:, :]).then_inc(wq_inv, 1)
                elif part == 1:
                    ve.tensor_scalar(sgam[:, :], rc[:, R_FG:R_FG + D], wscale[:, 1:2], None, ALU.mult)
                    ve.wait_ge(wq_inv, 1)
                else:
                    i, s = divmod(part - 2, 3)
                    r, o = ((up_raw, wup), (down_raw, wdn))[i]
                    if s == 0:
                        ve.tensor_scalar(r, r, winv[:, i:i + 1], MAGIC, ALU.mult, ALU.add).then_inc(wq_scaled, 1)
                    elif s == 1:
                        ve.wait_ge(wq_scaled, i + 1)
                        ve.tensor_scalar(r, r, -MAGIC, 1.0, ALU.add, ALU.min).then_inc(wq_round, 1)
                    else:
                        ve.wait_ge(wq_round, i + 1)
                        ve.tensor_scalar(o[:, :, :].rearrange("p k n -> p (k n)"), r, -1.0, None, ALU.max)\
                          .then_inc(wq_done, 1)

            marks = [0]

            def wait_apart(semaphore, value):
                marks[0] += 1
                ve.wait_ge(semaphore, value)
                ve.tensor_copy(mark[:, marks[0]:marks[0] + 1], mark[:, 0:1])

            def rope(r, u, part):
                t, m = r * 2 + u, T1[u]
                heads = "p (h d) -> p h d"
                q3, r3 = (a.rearrange(heads, d=HD) for a in (m.qk, m.qkr))
                if part == 0:
                    ve.wait_ge(qk_ready, t + 1)
                    ve.tensor_tensor(m.qk, m.P[0][:, 0:384], rc[:, R_BQK:R_BQK + 384], ALU.add).then_inc(qk_biased, 1)
                elif part < 3:
                    if part == 1:
                        ve.wait_ge(qk_biased, t + 1)
                    o, i = (slice(0, 8), slice(8, 16))[::3 - 2 * part]
                    ve.tensor_tensor(r3[:, :, o], q3[:, :, i],
                                     spread(kc[:, K_SIN + o.start:K_SIN + o.stop], 1, 24), ALU.mult)\
                      .then_inc(rope_sin, 1)
                else:
                    ve.wait_ge(rope_cos, t + 1)
                    ve.wait_ge(rope_sin, t * 2 + 2)
                    ve.tensor_tensor(m.qkr, m.qkr, m.rcos, ALU.add).then_inc(roped, 1)

            def stage1(r, u, phase):
                t, m = r * 2 + u, T1[u]
                if phase == 0:
                    for part in range(4):
                        rope(r, u, part)
                elif phase == 1:
                    ve.wait_ge(er_ready, t + 1)
                    for b in range(2):
                        ve.tensor_tensor(
                            m.vbd[:, b, :, :].rearrange("p g (j d) -> p g j d", j=2),
                            spread(m.P[1][:, 128 + 128 * b:256 + 128 * b].rearrange(
                                "p (g d) -> p g d", d=HD), 2, 2),
                            spread(spread(dj, 2, HD), 1, NKV), ALU.mult).then_inc(vbd_ready, 1)
                elif phase == 2:
                    ve.wait_ge(kT_ready, t + 1)
                    for b in range(2):
                        ve.tensor_tensor(m.kbd[:, b, :].rearrange("p (g k) -> p g k", g=NKV),
                                         spread(m.W[1][:, SLOT * b:SLOT * b + SEQ], 1, NKV),
                                         spread(d8, 2, SEQ), ALU.mult).then_inc(kbd_ready, 1)
                elif phase == 3:
                    for j in range(2):
                        ve.wait_ge(s1_ready, t * 2 + (j + 1))
                        s3 = m.W[j][:, 0:NKV * SEQ].rearrange("p (g k) -> p g k", g=NKV)
                        ve.tensor_reduce(m.st_max[:, 8 * j:8 * j + 8], s3, AX.X, ALU.max).then_inc(s1_max, 1)
                        ve.wait_ge(s1_max, t * 2 + (j + 1))
                        ve.tensor_tensor(m.pe4[:, :, j, :], s3, spread(m.st_max[:, 8 * j:8 * j + 8], 2, SEQ),
                                         ALU.subtract).then_inc(s1_sub, 1)
                elif phase == 4:
                    ve.wait_ge(p1_exp, t + 1)
                    ve.tensor_reduce(m.st_sum, m.pe3, AX.X, ALU.add).then_inc(p1_sum, 1)
                    ve.wait_ge(p1_sum, t + 1)
                    ve.reciprocal(m.st_rec, m.st_sum).then_inc(p1_rec, 1)
                    ve.wait_ge(p1_rec, t + 1)
                    ve.tensor_tensor(m.pe3, m.pe3, spread(m.st_rec, 2, SEQ), ALU.mult).then_inc(p1_norm, 1)
                elif phase == 5:
                    ve.wait_ge(pT_ready, t * 2 + 2)
                    ve.tensor_copy(m.pT[:, 4:8, :].rearrange("p g n -> p (g n)"), m.W[1][:, :])\
                      .then_inc(pTb_copied, 1)
                elif phase == 6:
                    ve.wait_ge(o1_ready, t + 1)
                    ve.wait_ge(xb_ready, t + 1)
                    ve.tensor_tensor(m.y1, m.W[1][:, 0:D], m.xb, ALU.add).then_inc(y1_ready, 1)
                    ve.wait_ge(y1_ready, t + 1)
                    ve.bn_stats(m.stats, m.y1).then_inc(y1_stats, 1)
                    wait_apart(y1_stats, t + 1)
                    ve.bn_aggr(m.aggr, m.stats).then_inc(y1_aggr, 1)
                    ve.wait_ge(y1_aggr, t + 1)
                    ve.tensor_scalar(m.veps, m.aggr[:, 1:2], 1e-5, None, ALU.add).then_inc(y1_veps, 1)
                elif phase == 7:
                    ve.wait_ge(y1_rstd, t + 1)
                    ve.tensor_scalar(m.y1, m.y1, m.aggr[:, 0:1], m.rstd, ALU.subtract, ALU.mult).then_inc(x1_ready, 1)

            def route(r):
                ve.wait_ge(er_ready, r * 2 + 2)
                ve.tensor_scalar(er, er, 1.0, None, ALU.add).then_inc(sig_plus, 1)
                ve.wait_ge(sig_plus, r + 1)
                ve.reciprocal(sg[0][:, 0:SEQ], er[:, 0:SEQ]).then_inc(sig_ready, 1)
                wait_apart(sig_ready, r + 1)
                cur = 0
                for k in range(4):
                    nxt = 1 + k % 2
                    ve.max(m8, sg[cur]).then_inc(top8, 1)
                    rope(r, 1, k)
                    wait_apart(top8, r * 4 + (k + 1))
                    ve.match_replace(sg[nxt], m8, sg[cur], -1.0).then_inc(top8_out, 1)
                    wait_apart(top8_out, r * 4 + (k + 1))
                    cur = nxt
                ve.tensor_scalar(negm[:, :], sg[cur][:, 0:SEQ], 0.0, NEG, ALU.is_ge, ALU.mult)\
                  .then_inc(negm_ready, 1)

            for m in T1:
                ve.memset(m.pe, 0.0)
            ve.memset(sg[0][:, SEQ:SEQ + 4], 2.0)

            def pair(r, more):
                for phase in (2, 1, 3, 4, 5):
                    for u in range(2):
                        stage1(r, u, phase)
                if more:
                    stage1(r + 1, 0, 0)
                else:
                    for c in range(2):
                        split_high(0, 0, c)
                for phase in (6, 7):
                    for u in range(2):
                        stage1(r, u, phase)
                if more:
                    route(r + 1)

            ve.wait_ge(rows_in, 16)
            stage1(0, 0, 0)
            route(0)
            with ve.Fori(0, TILES // 2 - 1) as r:
                pair(r, True)

            def split_high(m, par, c):
                ve.wait_ge(c_in[c], m * 16 + 16)
                ve.tensor_copy(chi[:, c, :, :], craw[:, (par * NCH + c) % 2, :, :]).then_inc(chi_ready, 1)

            def lower_keys(par, c, r, bank):
                for h in range(2):
                    here, there = slice(64 * h, 64 * h + 64), slice(64 - 64 * h, 128 - 64 * h)
                    lo = ve.scalar_tensor_tensor(
                        kst[par][there, 2 * r + h, CH * c:CH * c + CH], bank[here, 0:CH],
                        cc[here, C_BK2 + r:C_BK2 + r + 1],
                        kst[par][here, 2 * r + h, CH * c:CH * c + CH].bitcast(F32),
                        ALU.add, ALU.subtract)
                lo.then_inc(k_ready, 1)

            def first_keys_low(c, r):
                ve.wait_ge(khi_ready, 4 * c + 2 * r + 2)
                lower_keys(0, c, r, ALL8[(6 * c + r) % 8])

            def keys_low(m, par, k):
                c, r = k // TPC, k % TPC
                if r < 2:
                    ve.wait_ge(khi_ready, m * 12 + (4 * c + 2 * r + 2))
                    lower_keys(par, c, r, W[r])

            def queries(n, t, b, par, step):
                if step < 2:
                    src = q2_all[:, bass.ds(t, 1), :, SLOT * b:SLOT * b + SEQ].rearrange("p o j n -> p (o j) n")
                    if step == 0:
                        ve.tensor_copy(qh[:, :, :], src).then_inc(qh_ready, 1)
                    else:
                        ve.wait_ge(qh_ready, n + 1)
                        ve.tensor_tensor(ql[:, :, :], src, qh[:, :, :].bitcast(F32), ALU.subtract)\
                          .then_inc(ql_ready, 1)
                    return
                which, s = divmod(step - 2, 2)
                here = slice(64 * s, 64 * s + 64)
                ve.wait_ge(ql_ready, n + 1)
                for h in range(2):
                    o = qbd[par][which][64 * h:64 * h + 64, :, :, :].rearrange("p (j s) a n -> p s j a n", s=2)
                    ins = ve.tensor_tensor(o[:, s], spread((qh, ql)[which][here, :, :].bitcast(F32), 2, 4),
                                           spread(spread(d4[here, :], 2, SEQ), 1, KD), ALU.mult)
                ins.then_inc(qbd_ready, 1)

            h4 = "p (a h q) -> p a h q"

            def only_own(o, src):
                return ve.tensor_tensor(o.rearrange(h4, a=2, h=4), src, spread(spread(d4, 2, SEQ), 1, 2), ALU.mult)

            def fold(o, src):
                return ve.tensor_reduce(o.rearrange("p (a q) -> p a q", a=2),
                                        src.rearrange("p (a h q) -> p a q h", a=2, h=4), AX.X, ALU.add)

            def finish(n, t, b, part):
                if part == 0:
                    ve.wait_ge(pv_done, n * NT + NT)
                    only_own(accm, ACC[:, :, 0:QUAD].rearrange("p a (h q) -> p a h q", h=4)).then_inc(acc_read, 1)
                elif part == 1:
                    wait_apart(acc_read, n + 1)
                    fold(acc_own, accm).then_inc(acc_folded, 1)
                    ve.wait_ge(den_ready, n + 2)
                    only_own(denm, W0[:, 0:HQ].rearrange(h4, a=2, h=4)).then_inc(den_read, 1)
                    wait_apart(den_read, n + 1)
                    fold(den_own, denm).then_inc(den_folded, 1)
                elif part == 2:
                    ve.wait_ge(den_folded, n + 1)
                    ve.reciprocal(rec_own, den_own).then_inc(rec_ready, 1)
                else:
                    ve.wait_ge(acc_folded, n + 1)
                    ve.wait_ge(rec_ready, n + 1)
                    ve.tensor_tensor(oT_all[:, :, bass.ds(t, 1), SLOT * b:SLOT * b + SEQ].rearrange(
                                         "p a o q -> p (a o) q"),
                                     acc_own.rearrange("p (a q) -> p a q", a=2),
                                     rec_own.rearrange("p (a q) -> p a q", a=2), ALU.mult)\
                      .then_inc(o2_ready, 1)

            counted = [op not in (0, *POWER_OPS) for op in range(FRONT_OPS)]
            per_tile = sum(counted)

            def front(op, tile):
                row = {name: rc[:, name:name + D] for name in (R_LNG, R_LNB, R_NW)}
                mean, var = f_mv[:, 0:1], f_mv[:, 1:2]
                x1 = x1_all[:, bass.ds(tile, 1), :].rearrange("p o n -> p (o n)")
                before = tile * per_tile + sum(counted[:op])
                if op == 0:
                    ve.wait_ge(d3_ready, tile + 1)
                elif op == 1:
                    ve.wait_ge(d3_read, tile + 1)
                elif op in (2, 8, 11, 18, 19, 20):
                    wait_apart(f3_steps, before)
                else:
                    ve.wait_ge(f3_steps, before)
                if op in (6, 10, 13):
                    ve.wait_ge(pow_done, tile * 3 + ((6, 10, 13).index(op) + 1))
                if op == 0:
                    ins = ve.scalar_tensor_tensor(f_dl, W0[:, 0:D], rs[:, :], bo2rs[:, :], ALU.mult, ALU.add)
                elif op == 1:
                    ins = ve.bn_stats(f_stats, f_dl)
                elif op == 2:
                    ins = ve.bn_aggr(f_mv, f_stats)
                elif op == 3:
                    ins = ve.tensor_scalar(f_eps, var, 1e-5, None, ALU.add)
                elif op == 4:
                    ins = ve.scalar_tensor_tensor(f_dl, f_dl, mean, row[R_LNG], ALU.subtract, ALU.mult)
                elif op == 5:
                    ins = ve.tensor_tensor(f_xb, x1, row[R_LNB], ALU.add)
                elif op == 6:
                    ins = ve.scalar_tensor_tensor(f_x2, f_dl, f_rstd, f_xb, ALU.mult, ALU.add)
                elif op == 7:
                    ins = ve.bn_stats(f_stats, f_x2)
                elif op == 8:
                    ins = ve.bn_aggr(f_mv, f_stats)
                elif op == 9:
                    ins = ve.tensor_scalar(f_eps, var, 1e-5, None, ALU.add)
                elif op == 10:
                    ins = ve.tensor_scalar(f_x2, f_x2, mean, f_rstd, ALU.subtract, ALU.mult)
                elif op == 11:
                    ins = ve.tensor_tensor_reduce(f_xn, f_x2, f_x2, 1.0, 0.0, ALU.mult, ALU.add, f_ssq)
                elif op == 12:
                    ins = ve.tensor_scalar(f_eps, f_ssq, 1.0 / D, 1e-6, ALU.mult, ALU.add)
                elif op == 13:
                    ins = ve.scalar_tensor_tensor(f_xn, f_x2, f_rstd, row[R_NW], ALU.mult, ALU.mult)
                elif op == 14:
                    ins = ve.tensor_reduce(f_amax, f_xn, AX.X, ALU.max, apply_absolute_value=True)
                elif op == 15:
                    ins = ve.tensor_scalar(f_amax, f_amax, 1e-8, None, ALU.max)
                elif op == 16:
                    ins = ve.reciprocal(f_rmax, f_amax)
                elif op == 17:
                    ins = ve.tensor_scalar(f_xn, f_xn, QB, f_rmax, ALU.mult, ALU.mult)
                elif op == 18:
                    ins = ve.tensor_scalar(xq_all[:, bass.ds(tile, 1), :].rearrange("p o n -> p (o n)"), f_xn,
                                           MAGIC, -MAGIC, ALU.add, ALU.add)
                elif op == 19:
                    ins = ve.tensor_scalar(s5_all[:, bass.ds(tile, 1)], f_amax, 0.5 / QB, wscale[:, 0:1],
                                           ALU.mult, ALU.mult)
                else:
                    ins = ve.tensor_copy(x1, f_x2)
                ins.then_inc(d3_read if op == 0 else v3_ready if op in POWER_OPS else f3_steps, 1)

            def step(n, t, b, i, next0, next1, prev=None, op=None, tile=None):
                ve.wait_ge(p2_exp, n * NT + (i + 1))
                ve.tensor_scalar(p2[i % 3], p2[i % 3], EXP_MAX, EXP_MIN, ALU.min, ALU.max)\
                  .then_inc(p2_clip, 1)
                if i == 0 and next0:
                    split_high(n + 1, 1 - b, 2)
                if i == 4 and next1:
                    split_high(n + 2, b, 0)
                if i == 8 and next1:
                    split_high(n + 2, b, 1)
                if prev is not None:
                    for part in {1: (0,), 2: (1,), 3: (2, 3)}.get(i, ()):
                        finish(n - 1, *prev, part)
                if next0:
                    for part in {5: (0,), 6: (1, 2), 7: (3, 4), 10: (5,)}.get(i, ()):
                        queries(n + 1, t if b == 0 else t + 1, 1 - b, 1 - b, part)
                    keys_low(n + 1, 1 - b, i)
                if tile is not None and 0 <= op < FRONT_OPS:
                    front(op, tile)

            def batch(n, t, b, next0, next1, next2, tile=None):
                t1, b1 = (t, 1) if b == 0 else (t + 1, 0)
                for i in range(LAG, NT):
                    step(n, t, b, i, next0, next1, None, NT * b + i - FRONT_AT, tile)
                for i in range(LAG):
                    step(n + 1, t1, b1, i, next1, next2, (t, b), NT * (b + 1) + i - FRONT_AT, tile)

            pair(TILES // 2 - 1, False)
            split_high(0, 0, 2)
            masks()
            ve.tensor_scalar(bo2rs[:, :], rc[:, R_BO2:R_BO2 + D], rs[:, :], None, ALU.mult).then_inc(bo2_scaled, 1)
            ve.wait_ge(bo2_scaled, 1)
            for part in range(6):
                queries(0, 0, 0, 0, part)
            for c in range(NCH):
                for r in range(2):
                    first_keys_low(c, r)
                    if c == 0 and r == 1:
                        ternary(0)
                        ternary(1)
                if c >= 1:
                    ve.wait_ge(v_ready, TPC * c)
                    split_high(1, 1, c - 1)
                for part in ((2,), (3,), (4, 5, 6, 7))[c]:
                    ternary(part)
            for i in range(LAG):
                step(0, 0, 0, i, True, True)
            batch(0, 0, 0, True, True, True)
            batch(1, 0, 1, True, True, True)
            with ve.Fori(1, TILES - 1) as t:
                batch(t * 2, t, 0, True, True, True, t - 1)
                batch(t * 2 + 1, t, 1, True, True, True, t - 1)
            batch(B - 2, TILES - 1, 0, True, False, False, TILES - 2)
            for i in range(LAG, NT):
                step(B - 1, TILES - 1, 1, i, False, False, None, NT + i - FRONT_AT, TILES - 2)
            for op in range(2 * NT - FRONT_AT, FRONT_OPS):
                front(op, TILES - 2)

            def rows_in_order(g):
                for pair in range(2):
                    wait_apart(f3_steps, (TILES - 1 + g) * per_tile)
                    ve.tensor_copy(xq[:, 2 * pair:2 * pair + 2, :],
                                   xq_all[:, G3 * g + 2 * pair:G3 * g + 2 * pair + 2, :]).then_inc(xq_ready, 1)

            def h_rows(g, i):
                ve.wait_ge(z_ready, G3 * g + i + 1)
                ve.scalar_tensor_tensor(th[i].rearrange("p (a n) -> p a n", a=2),
                                        th[i].rearrange("p (a n) -> p a n", a=2), 1.0,
                                        SC[:, i % 2, :, :], ALU.add, ALU.mult).then_inc(h_ready, 1)

            def h_low(g, i):
                t = G3 * g + i
                hi, lo = hT[i % 2]
                for hh in range(2):
                    ks = slice(4 * hh, 4 * hh + 4)
                    ve.wait_ge(hThi_ready, 2 * t + hh + 1)
                    ve.tensor_tensor(lo[:, ks, :].rearrange("p k n -> p (k n)"), ACC[:, hh, :],
                                     hi[:, ks, :].bitcast(F32).rearrange("p k n -> p (k n)"),
                                     ALU.subtract).then_inc(hTlo_ready, 1)

            def add_ffn(g, i):
                t = G3 * g + i
                ve.wait_ge(dn_ready, t + 1)
                ve.scalar_tensor_tensor(xb3[:, i, :], W[i % 2][:, 0:D], s5_all[:, t:t + 1],
                                        sgam[:, :], ALU.mult, ALU.mult).then_inc(dn_read, 1)
                ve.wait_ge(dn_read, t + 1)
                ve.scalar_tensor_tensor(x2[:, i, :], x1_all[:, t, :], 2.0, xb3[:, i, :],
                                        ALU.mult, ALU.add).then_inc(x2_ready, 1)
                wait_apart(x2_ready, t + 1)
                ve.bn_stats(stats3[:, i, :], x2[:, i, :]).then_inc(x2_stats, 1)

            def last_norm(g, part):
                if part == 0:
                    wait_apart(x2_stats, G3 * g + G3)
                    for i in range(G3):
                        last = ve.bn_aggr(mv3[:, i, :], stats3[:, i, :])
                    last.then_inc(x2_aggr, 1)
                    ve.wait_ge(x2_aggr, g + 1)
                    ve.tensor_scalar(eps3, mv3[:, :, 1], 1e-5, None, ALU.add).then_inc(v3_ready, 1)
                else:
                    ve.wait_ge(pow_done, 3 * TILES + g + 1)
                    for i in range(G3):
                        last = ve.tensor_scalar(x1_all[:, G3 * g + i, :], x2[:, i, :], mv3[:, i, 0:1],
                                                rstd3[:, i:i + 1], ALU.subtract, ALU.mult)
                    last.then_inc(y3_ready, 1)

            next_op = [0]

            def last_front(n):
                for op in range(next_op[0], min(next_op[0] + n, FRONT_OPS)):
                    front(op, TILES - 1)
                next_op[0] += n

            rows_in_order(0)
            for part in range(4):
                finish(B - 1, TILES - 1, 1, part)
            for g in range(GROUPS):
                h_rows(g, 0)
                if g == 0:
                    last_front(1)
                else:
                    last_norm(g - 1, 0)
                h_rows(g, 1)
                if g == 0:
                    last_front(3)
                else:
                    last_norm(g - 1, 1)
                h_low(g, 0)
                for i in range(2, G3):
                    if g == 0:
                        last_front(3)
                    h_rows(g, i)
                    if g == 0:
                        last_front(2)
                    h_low(g, i - 1)
                    if g == 0:
                        last_front(1)
                    add_ffn(g, i - 2)
                if g == 0:
                    last_front(FRONT_OPS)
                h_low(g, G3 - 1)
                if g + 1 < GROUPS:
                    rows_in_order(g + 1)
                add_ffn(g, G3 - 2)
                add_ffn(g, G3 - 1)
            for part in range(2):
                last_norm(GROUPS - 1, part)


def kernel(**inputs):
    import concourse.bacc as bacc
    from concourse.bass_utils import run_bass_kernel_spmd

    a = {k: np.asarray(v) for k, v in inputs.items()}

    def padded(rows):
        o = np.zeros((B, SLOT, rows.shape[-1]), np.float32)
        o[:, :SEQ] = rows
        return o.reshape(TILES, 2 * SLOT, rows.shape[-1])

    order = np.concatenate([np.arange(HD) + HD * h for j in range(2) for h in range(j, NH, 2)])
    x = padded(a["x"])
    twice = np.concatenate([np.arange(HD) + HD * (h // 2) for h in range(NH)])
    w_r = np.zeros((D, 32), np.float32)
    w_r[:, :NH] = a["L0_attn_Wr"]
    rows = np.concatenate([
        a["L0_attn_bq"][order], a["L0_attn_bk"], a["L0_attn_bo"], a["L0_xattn_bo"],
        a["L0_xattn_ln_gamma"], a["L0_xattn_ln_beta"], a["L0_ffn_norm_weight"], a["L0_ffn_gamma"]])
    cols = np.zeros((128, C_ALL), np.float32)
    cols[:, C_BV1:C_BV1 + 2] = a["L0_attn_bv"][twice].reshape(2, 128).T
    cols[:, C_BQ2:C_BQ2 + 2] = a["L0_xattn_bq"].reshape(2, 128).T
    cols[:, C_BK2:C_BK2 + 2] = a["L0_xattn_bk"].reshape(2, 128).T
    cols[:, C_BV2:C_BV2 + 2] = a["L0_xattn_bv"].reshape(2, 128).T
    for b in range(4):
        cols[32 * b:32 * b + NH, C_BR] = a["L0_attn_br"]
    cols[:, C_RS] = a["L0_xattn_residual_scale"]

    p = np.arange(128)[:, None]
    consts = np.zeros((128, K_ALL), np.float32)
    consts[:, K_ID:K_ID + 128] = p == np.arange(128)
    consts[:, K_D8:K_D8 + 8] = p // HD == np.arange(8)
    consts[:, K_D4:K_D4 + 4] = (p // HD) % 4 == np.arange(4)
    consts[:, K_DJ:K_DJ + 2] = p // SLOT == np.arange(2)
    heads = np.concatenate([np.arange(j, NH, 2) for j in range(2)])
    consts[:, K_DH:K_DH + NH] = p % 32 == heads
    inv_freq = (1.0 / np.float32(1000000.0) ** (np.arange(0, HD, 2, dtype=np.float32) / HD)).astype(np.float32)
    freqs = (np.arange(SEQ, dtype=np.float32)[:, None] * inv_freq).astype(np.float32)
    for b in range(2):
        r = slice(SLOT * b, SLOT * b + SEQ)
        consts[r, K_COS:K_COS + HD] = np.tile(np.cos(freqs), 2)
        consts[r, K_SIN:K_SIN + HD] = np.concatenate([-np.sin(freqs), np.sin(freqs)], 1)

    arrays = {
        "x": x,
        "xT": x.reshape(TILES * 128, D).T,
        "ctxT": a["ctx_2048"].transpose(0, 2, 1),
        "mask": a["mask_BxS2_ik0"].reshape(B * NT, CT).T,
        "w_qk": np.concatenate([a["L0_attn_Wq"][:, order], a["L0_attn_Wk"]], 1),
        "w_v": a["L0_attn_Wv"],
        "w_r": w_r,
        "w_o": a["L0_attn_Wo"],
        "w_q2": a["L0_xattn_Wq"].T,
        "w_k2": a["L0_xattn_Wk"].T,
        "w_v2": a["L0_xattn_Wv"].T,
        "w_o2": a["L0_xattn_Wo"].T,
        "w_up": a["L0_ffn_weight_up"].T,
        "w_down": a["L0_ffn_weight_down"].T,
        "rows": rows,
        "cols": cols,
        "consts": consts,
    }
    nc = bacc.Bacc("TRN2", target_bir_lowering=False, num_devices=1)
    feeds, args = {}, []
    for name, v in arrays.items():
        v = np.ascontiguousarray(v)
        feeds[f"in_{name}"] = v
        args.append(nc.dram_tensor(f"in_{name}", v.shape, mybir.dt.from_np(v.dtype), kind="ExternalInput").ap())
    out = nc.dram_tensor("out", (B, SEQ, D), F32, kind="ExternalOutput").ap()
    build(nc, *args, out)
    r = run_bass_kernel_spmd(nc, [feeds], core_ids=[0])
    return r.results[0]["out"]
```
